# Optimizing a Trainium2 kernel written in Bass

```python
import numpy as np
import jax
import jax.numpy as jnp

def _softmax(x, axis=-1):
    return jax.nn.softmax(x, axis=axis)

def _gelu(x):
    return jax.nn.gelu(x, approximate=True)

def _silu(x):
    return jax.nn.silu(x)

def _sigmoid(x):
    return jax.nn.sigmoid(x)

def _layernorm(x, axis=-1, eps=1e-05):
    m = jnp.mean(x, axis=axis, keepdims=True)
    v = jnp.var(x, axis=axis, keepdims=True)
    return (x - m) / jnp.sqrt(v + eps)

def _scatter_add(tgt, idx, src, axis=0):
    return tgt.at[idx].add(src)

def _segment_sum(src, seg, n):
    return jax.ops.segment_sum(src, seg, n)
kernel_name = 'mk_early_fusion_embed_d1_tok_img256_r4_4e968b'

def setup_inputs(seed: int=0):
    np.random.seed(seed)
    _w = jnp.asarray

    def _rec_inputs():
        import jax
        import jax.numpy as jnp
        _rk = jax.random.key(seed)
        x = -0.00040386 + 0.999972 * jax.random.normal(jax.random.fold_in(_rk, 1), (64, 128, 64, 3), jnp.float32)
        x_txt = jax.random.randint(jax.random.fold_in(_rk, 51), (64, 77), 0, 100, jnp.int32)
        return (x, x_txt)
    x, x_txt = _rec_inputs()

    def _L0_tok_setup():
        import jax, jax.numpy as jnp
        import numpy as np
        B, T, J, LAT = (128, 128, 64, 64)
        EPS = 1e-05

        def layernorm(x, g, b):
            m = jnp.mean(x, axis=-1, keepdims=True)
            v = jnp.var(x, axis=-1, keepdims=True)
            return (x - m) * jax.lax.rsqrt(v + EPS) * g + b

        def conv2d(x, w, b, pad):
            y = jax.lax.conv_general_dilated(x, w, window_strides=(1, 1), padding=pad, dimension_numbers=('NCHW', 'OIHW', 'NCHW'))
            return y + b[None, :, None, None]
        key = jax.random.key(seed)
        ks = jax.random.split(key, 10)
        s = 0.02
        return {'x': jax.random.normal(ks[0], (B, T, J, 3), dtype=jnp.float32), 'ln0_g': jnp.ones((J * 3,), jnp.float32), 'ln0_b': jnp.zeros((J * 3,), jnp.float32), 'ln1_g': jnp.ones((J * 2,), jnp.float32), 'ln1_b': jnp.zeros((J * 2,), jnp.float32), 'conv1_w': jax.random.normal(ks[1], (T, T, 5, 3), jnp.float32) * s, 'conv1_b': jnp.zeros((T,), jnp.float32), 'conv2_w': jax.random.normal(ks[2], (T, T, 5, 2), jnp.float32) * s, 'conv2_b': jnp.zeros((T,), jnp.float32), 'conv3_w': jax.random.normal(ks[3], (2 * T, T, 5, 2), jnp.float32) * s, 'conv3_b': jnp.zeros((2 * T,), jnp.float32), 'out_w': jax.random.normal(ks[4], (2 * J, LAT), jnp.float32) * s, 'out_b': jnp.zeros((LAT,), jnp.float32)}
    _L0_tok_all = _L0_tok_setup()
    _L0_tok_in = {k: v for k, v in _L0_tok_all.items() if k in ('ln0_g', 'ln0_b', 'ln1_g', 'ln1_b', 'conv1_w', 'conv1_b', 'conv2_w', 'conv2_b', 'conv3_w', 'conv3_b', 'out_w', 'out_b')}
    del _L0_tok_all

    def _L0_txt_setup():
        import math
        import jax, jax.numpy as jnp
        import numpy as np
        L, H, D, F, V, S = (4, 8, 64, 256, 100, 512)
        DH = D // H
        EPS = 1e-05

        def positional_encoding(seq_len, d):
            pos = jnp.arange(seq_len, dtype=jnp.float32)[:, None]
            div = jnp.exp(jnp.arange(0, d, 2, dtype=jnp.float32) * (-math.log(10000.0) / d))
            pe = jnp.zeros((seq_len, d), dtype=jnp.float32)
            pe = pe.at[:, 0::2].set(jnp.sin(pos * div))
            pe = pe.at[:, 1::2].set(jnp.cos(pos * div))
            return pe

        def layer_norm(x, g, b):
            mu = jnp.mean(x, axis=-1, keepdims=True)
            var = jnp.mean(jnp.square(x - mu), axis=-1, keepdims=True)
            return (x - mu) * jax.lax.rsqrt(var + EPS) * g + b
        key = jax.random.key(seed)
        ks = jax.random.split(key, 16)
        tokens = jax.random.randint(ks[0], (4, S), 0, V)
        emb = jax.random.normal(ks[1], (V, D), jnp.float32) * 0.02
        emb = emb.at[0].set(0.0)

        def w(k, shape):
            fan = shape[-2] + shape[-1]
            return jax.random.uniform(k, shape, jnp.float32, -1.0, 1.0) * math.sqrt(6.0 / fan)
        return dict(tokens=tokens, emb=emb, Wq=w(ks[2], (L, D, D)), bq=jnp.zeros((L, D)), Wv=w(ks[3], (L, D, D)), bv=jnp.zeros((L, D)), Wo=w(ks[4], (L, D, D)), bo=jnp.zeros((L, D)), W1=w(ks[5], (L, D, F)), b1=jnp.zeros((L, F)), W2=w(ks[6], (L, F, D)), b2=jnp.zeros((L, D)), ln1_g=jnp.ones((L, D)), ln1_b=jnp.zeros((L, D)), ln2_g=jnp.ones((L, D)), ln2_b=jnp.zeros((L, D)), fin_g=jnp.ones((D,)), fin_b=jnp.zeros((D,)))
    _L0_txt_all = _L0_txt_setup()
    _L0_txt_in = {k: v for k, v in _L0_txt_all.items() if k in ('emb', 'Wq', 'bq', 'Wv', 'bv', 'Wo', 'bo', 'W1', 'b1', 'W2', 'b2', 'ln1_g', 'ln1_b', 'ln2_g', 'ln2_b', 'fin_g', 'fin_b')}
    del _L0_txt_all

    def _L0_attn_setup():
        import jax, jax.numpy as jnp
        import numpy as np
        DIM = 64
        HEADS = 4
        HEAD_DIM = DIM // HEADS
        SCALE = HEAD_DIM ** (-0.5)
        key = jax.random.key(seed)
        ks = jax.random.split(key, 9)
        B, N, C = (2, 1024, DIM)
        x = jax.random.normal(ks[0], (B, N, C), dtype=jnp.float32)
        lim = np.sqrt(6.0 / (C + C)).astype(np.float32)

        def w(k):
            return jax.random.uniform(k, (C, C), dtype=jnp.float32, minval=-lim, maxval=lim)
        return {'x': x, 'Wq': w(ks[1]), 'bq': jnp.zeros((C,), jnp.float32), 'Wk': w(ks[2]), 'bk': jnp.zeros((C,), jnp.float32), 'Wv': w(ks[3]), 'bv': jnp.zeros((C,), jnp.float32), 'Wo': w(ks[4]), 'bo': jnp.zeros((C,), jnp.float32)}
    _L0_attn_all = _L0_attn_setup()
    _L0_attn_in = {k: v for k, v in _L0_attn_all.items() if k in ('Wq', 'bq', 'Wk', 'bk', 'Wv', 'bv', 'Wo', 'bo')}
    del _L0_attn_all

    def _L0_ffn_setup():
        import jax, jax.numpy as jnp
        import numpy as np
        C = 64
        HID = 256
        E = 8
        TEMP = 1.0
        key = jax.random.key(seed)
        ks = jax.random.split(key, 7)
        x = jax.random.normal(ks[0], (8, 4096, C), dtype=jnp.float32)
        W1 = jax.random.normal(ks[1], (C, HID), dtype=jnp.float32) * 0.02
        b1 = jnp.zeros((HID,), dtype=jnp.float32)
        Wg = jax.random.normal(ks[2], (HID, E), dtype=jnp.float32) * 0.02
        bg = jnp.zeros((E,), dtype=jnp.float32)
        Wd = jax.random.normal(ks[3], (E, HID, C), dtype=jnp.float32) * 0.02
        bd = jnp.zeros((E, C), dtype=jnp.float32)
        return {'x': x, 'W1': W1, 'b1': b1, 'Wg': Wg, 'bg': bg, 'Wd': Wd, 'bd': bd}
    _L0_ffn_all = _L0_ffn_setup()
    _L0_ffn_in = {k: v for k, v in _L0_ffn_all.items() if k in ('W1', 'b1', 'Wg', 'bg', 'Wd', 'bd')}
    del _L0_ffn_all
    return {'x': x, 'x_txt': x_txt, 'L0_tok_ln0_g': _L0_tok_in['ln0_g'], 'L0_tok_ln0_b': _L0_tok_in['ln0_b'], 'L0_tok_ln1_g': _L0_tok_in['ln1_g'], 'L0_tok_ln1_b': _L0_tok_in['ln1_b'], 'L0_tok_conv1_w': _L0_tok_in['conv1_w'], 'L0_tok_conv1_b': _L0_tok_in['conv1_b'], 'L0_tok_conv2_w': _L0_tok_in['conv2_w'], 'L0_tok_conv2_b': _L0_tok_in['conv2_b'], 'L0_tok_conv3_w': _L0_tok_in['conv3_w'], 'L0_tok_conv3_b': _L0_tok_in['conv3_b'], 'L0_tok_out_w': _L0_tok_in['out_w'], 'L0_tok_out_b': _L0_tok_in['out_b'], 'L0_txt_emb': _L0_txt_in['emb'], 'L0_txt_Wq': _L0_txt_in['Wq'], 'L0_txt_bq': _L0_txt_in['bq'], 'L0_txt_Wv': _L0_txt_in['Wv'], 'L0_txt_bv': _L0_txt_in['bv'], 'L0_txt_Wo': _L0_txt_in['Wo'], 'L0_txt_bo': _L0_txt_in['bo'], 'L0_txt_W1': _L0_txt_in['W1'], 'L0_txt_b1': _L0_txt_in['b1'], 'L0_txt_W2': _L0_txt_in['W2'], 'L0_txt_b2': _L0_txt_in['b2'], 'L0_txt_ln1_g': _L0_txt_in['ln1_g'], 'L0_txt_ln1_b': _L0_txt_in['ln1_b'], 'L0_txt_ln2_g': _L0_txt_in['ln2_g'], 'L0_txt_ln2_b': _L0_txt_in['ln2_b'], 'L0_txt_fin_g': _L0_txt_in['fin_g'], 'L0_txt_fin_b': _L0_txt_in['fin_b'], 'L0_attn_Wq': _L0_attn_in['Wq'], 'L0_attn_bq': _L0_attn_in['bq'], 'L0_attn_Wk': _L0_attn_in['Wk'], 'L0_attn_bk': _L0_attn_in['bk'], 'L0_attn_Wv': _L0_attn_in['Wv'], 'L0_attn_bv': _L0_attn_in['bv'], 'L0_attn_Wo': _L0_attn_in['Wo'], 'L0_attn_bo': _L0_attn_in['bo'], 'L0_ffn_W1': _L0_ffn_in['W1'], 'L0_ffn_b1': _L0_ffn_in['b1'], 'L0_ffn_Wg': _L0_ffn_in['Wg'], 'L0_ffn_bg': _L0_ffn_in['bg'], 'L0_ffn_Wd': _L0_ffn_in['Wd'], 'L0_ffn_bd': _L0_ffn_in['bd']}

def reference(x, x_txt, L0_tok_ln0_g, L0_tok_ln0_b, L0_tok_ln1_g, L0_tok_ln1_b, L0_tok_conv1_w, L0_tok_conv1_b, L0_tok_conv2_w, L0_tok_conv2_b, L0_tok_conv3_w, L0_tok_conv3_b, L0_tok_out_w, L0_tok_out_b, L0_txt_emb, L0_txt_Wq, L0_txt_bq, L0_txt_Wv, L0_txt_bv, L0_txt_Wo, L0_txt_bo, L0_txt_W1, L0_txt_b1, L0_txt_W2, L0_txt_b2, L0_txt_ln1_g, L0_txt_ln1_b, L0_txt_ln2_g, L0_txt_ln2_b, L0_txt_fin_g, L0_txt_fin_b, L0_attn_Wq, L0_attn_bq, L0_attn_Wk, L0_attn_bk, L0_attn_Wv, L0_attn_bv, L0_attn_Wo, L0_attn_bo, L0_ffn_W1, L0_ffn_b1, L0_ffn_Wg, L0_ffn_bg, L0_ffn_Wd, L0_ffn_bd):
    import jax
    import jax.numpy as jnp

    def _L0_tok_ref(x, ln0_g, ln0_b, ln1_g, ln1_b, conv1_w, conv1_b, conv2_w, conv2_b, conv3_w, conv3_b, out_w, out_b):
        import jax, jax.numpy as jnp
        import numpy as np
        B, T, J, LAT = (128, 128, 64, 64)
        EPS = 1e-05

        def layernorm(x, g, b):
            m = jnp.mean(x, axis=-1, keepdims=True)
            v = jnp.var(x, axis=-1, keepdims=True)
            return (x - m) * jax.lax.rsqrt(v + EPS) * g + b

        def conv2d(x, w, b, pad):
            y = jax.lax.conv_general_dilated(x, w, window_strides=(1, 1), padding=pad, dimension_numbers=('NCHW', 'OIHW', 'NCHW'))
            return y + b[None, :, None, None]
        b, t, j, d = x.shape
        h = layernorm(x.reshape(b, t, j * 3), ln0_g, ln0_b).reshape(b, t, j, 3)
        h = jax.nn.relu(conv2d(h, conv1_w, conv1_b, ((2, 2), (1, 1))))
        h = layernorm(h.reshape(b, t, j * 3), ln0_g, ln0_b).reshape(b, t, j, 3)
        h = jax.nn.relu(conv2d(h, conv2_w, conv2_b, ((2, 2), (0, 0))))
        h = layernorm(h.reshape(b, t, j * 2), ln1_g, ln1_b).reshape(b, t, j, 2)
        h = jax.nn.relu(conv2d(h, conv3_w, conv3_b, ((2, 2), (0, 0))))
        h = h.reshape(b, 2 * t, j)
        res = jnp.concatenate([h[:, :t, :], h[:, t:, :]], axis=2)
        res = layernorm(res, ln1_g, ln1_b)
        return res @ out_w + out_b

    def _L0_txt_ref(tokens, emb, Wq, bq, Wv, bv, Wo, bo, W1, b1, W2, b2, ln1_g, ln1_b, ln2_g, ln2_b, fin_g, fin_b):
        import math
        import jax, jax.numpy as jnp
        import numpy as np
        L, H, D, F, V, S = (4, 8, 64, 256, 100, 512)
        DH = D // H
        EPS = 1e-05

        def positional_encoding(seq_len, d):
            pos = jnp.arange(seq_len, dtype=jnp.float32)[:, None]
            div = jnp.exp(jnp.arange(0, d, 2, dtype=jnp.float32) * (-math.log(10000.0) / d))
            pe = jnp.zeros((seq_len, d), dtype=jnp.float32)
            pe = pe.at[:, 0::2].set(jnp.sin(pos * div))
            pe = pe.at[:, 1::2].set(jnp.cos(pos * div))
            return pe

        def layer_norm(x, g, b):
            mu = jnp.mean(x, axis=-1, keepdims=True)
            var = jnp.mean(jnp.square(x - mu), axis=-1, keepdims=True)
            return (x - mu) * jax.lax.rsqrt(var + EPS) * g + b
        B, Sq = tokens.shape
        x = emb[tokens] + positional_encoding(Sq, D)[None]
        scale = 1.0 / math.sqrt(DH)
        for i in range(L):
            q = (x @ Wq[i] + bq[i]).reshape(B, Sq, H, DH).transpose(0, 2, 1, 3)
            k = (x @ Wv[i] + bv[i]).reshape(B, Sq, H, DH).transpose(0, 2, 1, 3)
            v = (x @ Wv[i] + bv[i]).reshape(B, Sq, H, DH).transpose(0, 2, 1, 3)
            scores = jnp.einsum('bhqd,bhkd->bhqk', q, k) * scale
            attn = jax.nn.softmax(scores, axis=-1)
            o = jnp.einsum('bhqk,bhkd->bhqd', attn, v)
            o = o.transpose(0, 2, 1, 3).reshape(B, Sq, D)
            y = o @ Wo[i] + bo[i]
            x = x + layer_norm(y, ln1_g[i], ln1_b[i])
            h = jax.nn.gelu(x @ W1[i] + b1[i], approximate=False)
            y = h @ W2[i] + b2[i]
            x = x + layer_norm(y, ln2_g[i], ln2_b[i])
        return layer_norm(x, fin_g, fin_b)

    def _L0_attn_ref(x, Wq, bq, Wk, bk, Wv, bv, Wo, bo):
        import jax, jax.numpy as jnp
        import numpy as np
        DIM = 64
        HEADS = 4
        HEAD_DIM = DIM // HEADS
        SCALE = HEAD_DIM ** (-0.5)
        B, N, C = x.shape
        x = jnp.clip(x, -10000.0, 10000.0)

        def heads(t):
            return t.reshape(B, N, HEADS, HEAD_DIM).transpose(0, 2, 1, 3)
        q = heads((x @ Wq.T + bq).astype(jnp.float32))
        k = heads((x @ Wk.T + bk).astype(jnp.float32))
        v = heads((x @ Wv.T + bv).astype(jnp.float32))
        attn = jnp.einsum('bhnd,bhmd->bhnm', q, k) * SCALE
        attn = jax.nn.softmax(attn, axis=-1)
        out = jnp.einsum('bhnm,bhmd->bhnd', attn, v)
        out = out.transpose(0, 2, 1, 3).reshape(B, N, C)
        out = out.astype(jnp.bfloat16).astype(jnp.float32)
        return out @ Wo.T + bo

    def _L0_ffn_ref(x, W1, b1, Wg, bg, Wd, bd):
        import jax, jax.numpy as jnp
        import numpy as np
        C = 64
        HID = 256
        E = 8
        TEMP = 1.0
        orig_shape = x.shape
        xf = x.reshape(-1, orig_shape[-1])
        H = jax.nn.gelu(xf @ W1 + b1, approximate=False)
        probs = jax.nn.softmax((H @ Wg + bg) / TEMP, axis=-1)
        assign = jnp.argmax(probs, axis=-1)
        out = jnp.zeros_like(xf)
        for e in range(Wd.shape[0]):
            y = H @ Wd[e] + bd[e]
            sel = (assign == e)[:, None]
            out = out + jnp.where(sel, probs[:, e:e + 1] * y, 0.0)
        return out.reshape(orig_shape)
    h = _L0_tok_ref(x, L0_tok_ln0_g, L0_tok_ln0_b, L0_tok_ln1_g, L0_tok_ln1_b, L0_tok_conv1_w, L0_tok_conv1_b, L0_tok_conv2_w, L0_tok_conv2_b, L0_tok_conv3_w, L0_tok_conv3_b, L0_tok_out_w, L0_tok_out_b)
    h = jnp.concatenate([h, _L0_txt_ref(x_txt, L0_txt_emb, L0_txt_Wq, L0_txt_bq, L0_txt_Wv, L0_txt_bv, L0_txt_Wo, L0_txt_bo, L0_txt_W1, L0_txt_b1, L0_txt_W2, L0_txt_b2, L0_txt_ln1_g, L0_txt_ln1_b, L0_txt_ln2_g, L0_txt_ln2_b, L0_txt_fin_g, L0_txt_fin_b)], axis=1)
    h = h + _L0_attn_ref(_layernorm(h, axis=-1), L0_attn_Wq, L0_attn_bq, L0_attn_Wk, L0_attn_bk, L0_attn_Wv, L0_attn_bv, L0_attn_Wo, L0_attn_bo)
    h = h + _L0_ffn_ref(_layernorm(h, axis=-1), L0_ffn_W1, L0_ffn_b1, L0_ffn_Wg, L0_ffn_bg, L0_ffn_Wd, L0_ffn_bd)
    return h

_drawn_inputs = setup_inputs


def setup_inputs(seed=0):
    import zlib

    import numpy as np

    out = dict(_drawn_inputs(seed))
    spreads = {'L0_tok_ln0_g': (1.0, 0.2),
     'L0_tok_ln0_b': (0.0, 0.1),
     'L0_tok_ln1_g': (1.0, 0.2),
     'L0_tok_ln1_b': (0.0, 0.1),
     'L0_tok_conv1_b': (0.0, 0.1),
     'L0_tok_conv2_b': (0.0, 0.282),
     'L0_tok_conv3_b': (0.0, 0.1),
     'L0_tok_out_b': (0.0, 0.1),
     'L0_txt_bq': (0.0, 0.8),
     'L0_txt_bv': (0.0, 0.1),
     'L0_txt_bo': (0.0, 0.1),
     'L0_txt_b1': (0.0, 0.1),
     'L0_txt_b2': (0.0, 0.1),
     'L0_txt_ln1_g': (1.0, 0.2),
     'L0_txt_ln1_b': (0.0, 0.1),
     'L0_txt_ln2_g': (1.0, 0.2),
     'L0_txt_ln2_b': (0.0, 0.1),
     'L0_txt_fin_g': (1.0, 0.2),
     'L0_txt_fin_b': (0.0, 0.1),
     'L0_attn_bq': (0.0, 0.436),
     'L0_attn_bk': (0.0, 0.8),
     'L0_attn_bv': (0.0, 0.1),
     'L0_attn_bo': (0.0, 0.1),
     'L0_ffn_b1': (0.0, 0.8),
     'L0_ffn_bg': (0.0, 0.35),
     'L0_ffn_bd': (0.0, 0.529)}
    factors = {'L0_txt_emb': 6.778, 'L0_ffn_W1': 8.0, 'L0_ffn_Wg': 8.0, 'L0_ffn_Wd': 8.0}
    for name, (base, spread) in spreads.items():
        noise = np.random.default_rng([zlib.crc32(name.encode()), seed]).standard_normal(out[name].shape)
        drawn = base * np.exp(spread * noise) if base else spread * noise
        out[name] = jnp.asarray(drawn.astype(out[name].dtype))
    for name, factor in factors.items():
        out[name] = (out[name] * factor).astype(out[name].dtype)
    return out
```

```python
from contextlib import ExitStack

import numpy as np

import concourse.bass as bass
from concourse import mybir

F32 = mybir.dt.float32
F32R = mybir.dt.float32r
BF16 = mybir.dt.bfloat16
I32 = mybir.dt.int32
ALU = mybir.AluOpType
ACT = mybir.ActivationFunctionType
AX = mybir.AxisListType

P = 128
EPS = 1e-5
B = 64
T, J, LAT = 128, 64, 64
QUAD = 4
JP = J + 4


class Count:

    def __init__(self, base):
        self.base, self.k = base, 0

    def up(self, by=1):
        self.k += by
        return self.base + self.k


class Program:

    def __init__(self, nc, ctx, samples):
        self.nc, self.ctx, self.samples = nc, ctx, samples
        self.quads = samples // QUAD

    def sb(self, name, shape, dtype=F32):
        return self.ctx.enter_context(self.nc.sbuf_tensor(name, shape, dtype))

    def psum(self, ctx, name, shape, dtype=F32):
        return ctx.enter_context(self.nc.psum_tensor(name, shape, dtype))

    def sem(self, name):
        return self.ctx.enter_context(self.nc.semaphore(name))


def row(ap):
    return ap.rearrange("(a n) -> a n", a=1)


def on_all_rows(ap, rows=P):
    return row(ap).broadcast_to([rows, ap.shape[0]])



def image_branch(p, x, wts, ident, h_img):
    nc = p.nc
    TAPS = (15, 10, 10)
    KD = (3, 2, 2)
    COLS = (3, 3, 2, 1)
    OUT_HALVES = (1, 1, 2)

    with ExitStack() as ctx:
        def sb(name, shape, dtype=F32):
            return ctx.enter_context(nc.sbuf_tensor(name, shape, dtype))

        def sem(name):
            return p.sem("im_" + name)

        w = [sb(f"im_w{c}", [P, TAPS[c] * OUT_HALVES[c], 2, P], F32R) for c in range(3)]
        bias = [sb(f"im_bias{c}", [P, OUT_HALVES[c]]) for c in range(3)]
        g0_jd, b0_jd = sb("im_g0_jd", [P, 3 * J]), sb("im_b0_jd", [P, 3 * J])
        g0, b0 = sb("im_g0", [P, 3 * J]), sb("im_b0", [P, 3 * J])
        g1_jd, b1_jd = sb("im_g1_jd", [P, 2 * J]), sb("im_b1_jd", [P, 2 * J])
        g1, b1 = sb("im_g1", [P, 2 * J]), sb("im_b1", [P, 2 * J])
        g1_col, b1_col = sb("im_g1_col", [P, 1]), sb("im_b1_col", [P, 1])
        w_out, bias_out = sb("im_w_out", [P, LAT]), sb("im_bias_out", [P, LAT])

        loaded = [sem(f"w_loaded{c}") for c in range(3)]
        small_loaded, zeroed = sem("small_loaded"), sem("zeroed")
        turned, hi_cut, lo_cut = sem("w_turned"), sem("w_hi_cut"), sem("w_lo_cut")

        a_hi = [sb(f"im_a_hi{c}", [P, (2 if c == 0 else 1), QUAD, COLS[c], JP], F32R) for c in range(3)]
        a_lo = [sb(f"im_a_lo{c}", [P, (2 if c == 0 else 1), QUAD, COLS[c], JP], F32R) for c in range(3)]

        with ExitStack() as setup:
            raw = [setup.enter_context(nc.sbuf_tensor(f"im_raw{c}", [P, OUT_HALVES[c], P * TAPS[c]], F32))
                   for c in range(3)]
            turn = [p.psum(setup, f"im_turn{k}", [P, 4, P]) for k in range(4)]
            jobs = [(c, t, h) for c in range(3) for h in range(OUT_HALVES[c]) for t in range(TAPS[c])]
            packs = [[q for q in jobs if q[0] == c] for c in range(3)]
            packs = [q[k:k + 4] for q in packs for k in range(0, len(q), 4)]

            with nc.Block() as block:
                @block.sync
                def _(sp):
                    for c in range(3):
                        sp.dma_start(raw[c][:], wts[f"conv{c + 1}_w"].rearrange("(h o) i a b -> o h (i a b)", o=P))\
                            .then_inc(loaded[c], 16)
                    with nc.allow_non_contiguous_dma(reason="biases and gains as columns"):
                        for c in range(3):
                            sp.dma_start(bias[c][:], wts[f"conv{c + 1}_b"].rearrange("(h o) -> o h", o=P))\
                                .then_inc(small_loaded, 16)
                        sp.dma_start(g1_col[:], wts["ln1_g"].rearrange("(n a) -> n a", a=1)).then_inc(small_loaded, 16)
                        sp.dma_start(b1_col[:], wts["ln1_b"].rearrange("(n a) -> n a", a=1)).then_inc(small_loaded, 16)
                    sp.dma_start(g0_jd[:], on_all_rows(wts["ln0_g"])).then_inc(small_loaded, 16)
                    sp.dma_start(b0_jd[:], on_all_rows(wts["ln0_b"])).then_inc(small_loaded, 16)
                    sp.dma_start(g1_jd[:], on_all_rows(wts["ln1_g"])).then_inc(small_loaded, 16)
                    sp.dma_start(b1_jd[:], on_all_rows(wts["ln1_b"])).then_inc(small_loaded, 16)
                    sp.dma_start(w_out[:], wts["out_w"]).then_inc(small_loaded, 16)
                    sp.dma_start(bias_out[:], on_all_rows(wts["out_b"])).then_inc(small_loaded, 16)

                @block.gpsimd
                def _(pool):
                    for c in range(3):
                        pool.memset(a_hi[c][:].bitcast(F32), 0.0).then_inc(zeroed, 1)
                        pool.memset(a_lo[c][:].bitcast(F32), 0.0).then_inc(zeroed, 1)

                @block.tensor
                def _(pe):
                    for n, pack in enumerate(packs):
                        c = pack[0][0]
                        pe.wait_ge(loaded[c], 16)
                        if n >= 4:
                            pe.wait_ge(lo_cut, n - 3)
                        for k, (c, t, h) in enumerate(pack):
                            src = raw[c][:, h].rearrange("o (i t) -> o t i", t=TAPS[c])[:, t]
                            last = pe.transpose(turn[n % 4][:, k], src, ident[:])
                        last.then_inc(turned, 1)

                def slots(n):
                    c, t, h = packs[n][0]
                    k = h * TAPS[c] + t
                    return w[c], k, len(packs[n])

                @block.scalar
                def _(act):
                    for n in range(len(packs)):
                        dst, k, m = slots(n)
                        act.wait_ge(turned, n + 1)
                        act.activation(dst[:, k:k + m, 0], turn[n % 4][:, 0:m], ACT.Copy).then_inc(hi_cut, 1)

                @block.vector
                def _(dve):
                    for n in range(len(packs)):
                        dst, k, m = slots(n)
                        dve.wait_ge(hi_cut, n + 1)
                        dve.tensor_tensor(dst[:, k:k + m, 1], turn[n % 4][:, 0:m], dst[:, k:k + m, 0].bitcast(F32),
                                          ALU.subtract).then_inc(lo_cut, 1)
                    dve.wait_ge(small_loaded, 11 * 16)
                    for dst, src in ((g0, g0_jd), (b0, b0_jd)):
                        dve.tensor_copy(dst[:].rearrange("p (d j) -> p d j", d=3),
                                        src[:].rearrange("p (j d) -> p d j", d=3))
                    for dst, src in ((g1, g1_jd), (b1, b1_jd)):
                        dve.tensor_copy(dst[:].rearrange("p (d j) -> p d j", d=2),
                                        src[:].rearrange("p (j d) -> p d j", d=2))

        xin = sb("im_x", [P, 2, QUAD, 3 * J])
        act_out = [sb("im_h1", [P, QUAD, 3 * J]), sb("im_h2", [P, QUAD, 2 * J]), sb("im_h3", [P, QUAD, 2 * J])]
        scaled, normed = sb("im_scaled", [P, QUAD, 3 * J]), sb("im_normed", [P, QUAD, 3 * J])
        stats, mean_var = sb("im_stats", [P, QUAD, 6]), sb("im_mean_var", [P, QUAD, 2])
        var_eps, rstd = sb("im_var_eps", [P, QUAD]), sb("im_rstd", [P, QUAD])
        power = sb("im_power", [P, QUAD])
        res = sb("im_res", [P, QUAD, P])
        res_t = sb("im_res_t", [P, QUAD, P])
        c1 = [p.psum(ctx, f"im_c1{k}", [P, 2, 3, J]) for k in range(2)]
        c2 = p.psum(ctx, "im_c2", [P, QUAD, 2, J])
        c3 = p.psum(ctx, "im_c3", [P, 2, QUAD, J])
        turned_res = p.psum(ctx, "im_turned_res", [P, QUAD, P])
        out_rows = p.psum(ctx, "im_out_rows", [P, QUAD, LAT])

        x_loaded = [sem("x_loaded0"), sem("x_loaded1")]
        power_set = sem("power_set")
        dve_step = sem("dve_step")
        var_ready, rstd_ready = sem("var_ready"), sem("rstd_ready")
        normed_ready, hi_ready, lo_ready = sem("normed_ready"), sem("hi_ready"), sem("lo_ready")
        conv_done = [sem(f"conv{c}_done") for c in range(3)]
        relu_done = [sem(f"relu{c}_done") for c in range(3)]
        res_ready, res_turned, res_scaled, out_done, rows_stored = (
            sem("res_ready"), sem("res_turned"), sem("res_scaled"), sem("out_done"), sem("rows_stored"))

        U = p.quads
        assert U % 2 == 0 and U >= 4

        def each_quad(eng, before, step):
            before()
            step(0, 0, True, False)
            step(1, 1, False, False)
            if U > 4:
                with eng.Fori(1, U // 2 - 1) as i:
                    step(i * 2, 0, False, False)
                    step(i * 2 + 1, 1, False, False)
            step(U - 2, 0, False, False)
            step(U - 1, 1, False, True)

        STATS = QUAD
        FULL = STATS + QUAD
        TURN = 3 * FULL + STATS

        def cuts_before(n):
            return n * 3 + 1

        def norms_before(n, first):
            return 1 if first else n * 4

        def steps_before(n, first):
            return FULL if first else n * TURN + (FULL - STATS)

        with nc.Block() as block:
            @block.sync
            def _(sp):
                def load(n, par):
                    sp.dma_start(xin[:, par], x[bass.ds(n * QUAD, QUAD)].rearrange("b t j d -> t b (j d)"))\
                        .then_inc(x_loaded[par], 16)

                def step(n, par, first, last):
                    if not last:
                        if not first:
                            sp.wait_ge(normed_ready, n * 3 - 2)
                        load(n + 1, 1 - par)

                each_quad(sp, lambda: load(0, 0), step)

            @block.vector
            def _(dve):
                def statistics(src, c):
                    for b in range(QUAD):
                        dve.bn_stats(stats[:, b], src[:, b])
                    dve.drain()
                    for b in range(QUAD):
                        dve.bn_aggr(mean_var[:, b], stats[:, b]).then_inc(dve_step, 1)
                    dve.wait_ge(dve_step, c.up(QUAD))
                    dve.tensor_scalar(var_eps[:], mean_var[:, :, 1], EPS, None, ALU.add).then_inc(var_ready, 1)

                def normalise(src, size, gain, shift, c, norms, cuts, first=False, by_column=False):
                    statistics(src, c)
                    for b in range(QUAD):
                        img, to, by = src[:, b], scaled[:, b, 0:size], gain[:]
                        if by_column:
                            img = img.rearrange("p (j d) -> p d j", d=3)
                            to, by = (v.rearrange("p (d j) -> p d j", d=3) for v in (to, by))
                        dve.scalar_tensor_tensor(out=to, in0=img, scalar=mean_var[:, b, 0:1], in1=by,
                                                 op0=ALU.subtract, op1=ALU.mult).then_inc(dve_step, 1)
                    dve.wait_ge(dve_step, c.up(QUAD))
                    dve.wait_ge(rstd_ready, norms.up())
                    if not first:
                        dve.wait_ge(lo_ready, cuts.up() - 1)
                    for b in range(QUAD):
                        last = dve.scalar_tensor_tensor(out=normed[:, b, 0:size], in0=scaled[:, b, 0:size],
                                                        scalar=rstd[:, b:b + 1], in1=shift[:],
                                                        op0=ALU.mult, op1=ALU.add)
                    last.then_inc(normed_ready, 1)

                def last_norm(c, norms):
                    statistics(act_out[2], c)
                    dve.wait_ge(rstd_ready, norms.up())
                    for b in range(QUAD):
                        last = dve.tensor_scalar(res[:, b], act_out[2][:, b], mean_var[:, b, 0:1], rstd[:, b:b + 1],
                                                 ALU.subtract, ALU.mult)
                    last.then_inc(res_ready, 1)

                def store_rows(n):
                    dve.wait_ge(out_done, n + 1)
                    dve.tensor_tensor(h_img[:, bass.ds(n * QUAD, QUAD)], out_rows[:],
                                      bias_out[:].unsqueeze(1).broadcast_to([P, QUAD, LAT]), ALU.add)\
                        .then_inc(rows_stored, 1)

                def first_norm(n, par, c, norms, cuts, first=False):
                    dve.wait_ge(x_loaded[par], (n - par) * 8 + 16)
                    normalise(xin[:, par], 3 * J, g0, b0, c, norms, cuts, first, by_column=True)

                def before():
                    dve.memset(power[:], -0.5).then_inc(power_set, 1)
                    c = Count(0)
                    first_norm(0, 0, c, Count(0), Count(0), True)
                    assert c.k == FULL

                def step(n, par, first, last):
                    c, norms, cuts = Count(steps_before(n, first)), Count(norms_before(n, first)), Count(cuts_before(n))
                    if not last:
                        first_norm(n + 1, 1 - par, c, norms, cuts)
                    dve.wait_ge(relu_done[0], n * 2 + 2)
                    normalise(act_out[0], 3 * J, g0, b0, c, norms, cuts)
                    if not first:
                        dve.wait_ge(relu_done[2], n)
                        last_norm(c, norms)
                    dve.wait_ge(relu_done[1], n + 1)
                    normalise(act_out[1], 2 * J, g1, b1, c, norms, cuts)
                    if not first:
                        store_rows(n - 1)
                    if last:
                        dve.wait_ge(relu_done[2], n + 1)
                        last_norm(c, norms)
                        store_rows(n)
                    else:
                        assert c.k == (TURN - STATS if first else TURN)

                each_quad(dve, before, step)

            @block.gpsimd
            def _(pool):
                def rstd_of(norms):
                    pool.wait_ge(var_ready, norms.up())
                    pool.tensor_tensor(rstd[:], var_eps[:], power[:], ALU.pow).then_inc(rstd_ready, 1)

                def lo_of(c, par, cuts):
                    cols = COLS[c]
                    pool.wait_ge(hi_ready, cuts.up())
                    for b in range(QUAD):
                        last = pool.tensor_tensor(
                            a_lo[c][:, par, b, :, 2:2 + J],
                            normed[:, b, 0:cols * J].rearrange("p (d j) -> p d j", d=cols),
                            a_hi[c][:, par, b, :, 2:2 + J].bitcast(F32), ALU.subtract)
                    last.then_inc(lo_ready, 1)

                def before():
                    pool.wait_ge(power_set, 1)
                    rstd_of(Count(0))
                    lo_of(0, 0, Count(0))

                def step(n, par, first, last):
                    norms, cuts = Count(norms_before(n, first)), Count(cuts_before(n))
                    if not last:
                        rstd_of(norms)
                        lo_of(0, 1 - par, cuts)
                    rstd_of(norms)
                    lo_of(1, 0, cuts)
                    if not first:
                        rstd_of(norms)
                    rstd_of(norms)
                    lo_of(2, 0, cuts)
                    if last:
                        rstd_of(norms)

                each_quad(pool, before, step)

            @block.scalar
            def _(act):
                def hi_of(c, par, cuts):
                    cols = COLS[c]
                    act.wait_ge(normed_ready, cuts.up())
                    for b in range(QUAD):
                        last = act.activation(a_hi[c][:, par, b, :, 2:2 + J],
                                              normed[:, b, 0:cols * J].rearrange("p (d j) -> p d j", d=cols), ACT.Copy)
                    last.then_inc(hi_ready, 1)

                def relu(c, n):
                    if c == 0:
                        for k in range(2):
                            act.wait_ge(conv_done[0], n * 2 + k + 1)
                            act.activation(act_out[0][:, 2 * k:2 * k + 2], c1[k][:].rearrange("p b d j -> p b (d j)"),
                                           ACT.Relu, bias=bias[0][:, 0:1]).then_inc(relu_done[0], 1)
                    elif c == 1:
                        act.wait_ge(conv_done[1], n + 1)
                        act.activation(act_out[1][:], c2[:].rearrange("p b d j -> p b (d j)"), ACT.Relu,
                                       bias=bias[1][:, 0:1]).then_inc(relu_done[1], 1)
                    else:
                        act.wait_ge(conv_done[2], n + 1)
                        for half in range(2):
                            last = act.activation(act_out[2][:, :, half * J:half * J + J], c3[:, half], ACT.Relu,
                                                  bias=bias[2][:, half:half + 1])
                        last.then_inc(relu_done[2], 1)

                def scale_res(n):
                    act.wait_ge(res_turned, n + 1)
                    act.activation(res_t[:], turned_res[:], ACT.Identity, bias=b1_col[:], scale=g1_col[:])\
                        .then_inc(res_scaled, 1)

                def step(n, par, first, last):
                    cuts = Count(cuts_before(n))
                    if not last:
                        hi_of(0, 1 - par, cuts)
                    relu(0, n)
                    hi_of(1, 0, cuts)
                    if not first:
                        relu(2, n - 1)
                    relu(1, n)
                    if not first:
                        scale_res(n - 1)
                    hi_of(2, 0, cuts)
                    if last:
                        relu(2, n)
                        scale_res(n)

                each_quad(act, lambda: hi_of(0, 0, Count(0)), step)

            @block.tensor
            def _(pe):
                def conv(c, par, cuts, n):
                    pe.wait_ge(lo_ready, cuts)
                    hi, lo = a_hi[c][:, par], a_lo[c][:, par]
                    halves = ((0, 2), (2, 4)) if c == 0 else ((0, 4),)
                    for k, (b0_, b1_) in enumerate(halves):
                        for half in range(OUT_HALVES[c]):
                            acc = c1[k][:] if c == 0 else c2[:] if c == 1 else c3[:, half].unsqueeze(2)
                            taps = [(kj, kd) for kd in ((1, 0, 2) if c == 0 else range(2)) for kj in range(5)]
                            for kj, kd in taps:
                                shift = kd - 1 if c == 0 else kd
                                d0 = max(0, -shift) if c == 0 else 0
                                d1 = min(3, 3 - shift) if c == 0 else COLS[c + 1]
                                slot = half * TAPS[c] + kj * KD[c] + kd
                                for part, img in ((0, hi), (1, hi), (0, lo)):
                                    opens = (kj, kd) == taps[0] and part == 0 and img is hi
                                    closes = (kj, kd) == taps[-1] and img is lo
                                    last = pe.matmul(acc[:, :, d0:d1], w[c][:, slot, part],
                                                     img[:, b0_:b1_, d0 + shift:d1 + shift, kj:kj + J],
                                                     start=opens, stop=closes)
                        if c == 0:
                            last.then_inc(conv_done[0], 1)
                    if c:
                        last.then_inc(conv_done[c], 1)

                def project(n):
                    pe.wait_ge(res_ready, n + 1)
                    for b in range(QUAD):
                        last = pe.transpose(turned_res[:, b], res[:, b], ident[:])
                    last.then_inc(res_turned, 1)
                    pe.wait_ge(res_scaled, n + 1)
                    for b in range(QUAD):
                        last = pe.matmul(out_rows[:, b], res_t[:, b], w_out[:], start=True, stop=True)
                    last.then_inc(out_done, 1)

                def step(n, par, first, last):
                    cuts = cuts_before(n)
                    conv(0, par, 1 if first else n * 3 - 1, n)
                    if not first:
                        conv(2, 0, cuts, n - 1)
                    conv(1, 0, cuts + (1 if last else 2), n)
                    if not first:
                        project(n - 1)
                    if last:
                        conv(2, 0, cuts + 2, n)
                        project(n)

                each_quad(pe, lambda: None, step)


def constants(p, ident):
    nc = p.nc
    cleared, made = p.sem("ident_cleared"), p.sem("ident_made")
    with nc.Block() as block:
        @block.gpsimd
        def _(pool):
            pool.memset(ident[:], 0.0).then_inc(cleared, 1)
            pool.wait_ge(cleared, 1)
            pool.affine_select(out=ident[:], in_=ident[:], compare_op=ALU.not_equal, fill=1.0, base=0,
                               pattern=[[-1, P]], channel_multiplier=1).then_inc(made, 1)
            pool.wait_ge(made, 1)



S_TXT = 77
SP_TXT = S_TXT + 1
D = 64
LAYERS, HEADS, FF, VOCAB = 4, 8, 256, 100
DH = D // HEADS

SEC = {}
_at = 0
for _name, _width in (("q", 2 * 2 * P), ("k", 2 * 2 * P), ("v", 2 * D), ("o", 2 * D), ("ff1", 2 * FF)):
    SEC[_name] = (_at, _at + _width)
    _at += _width
W_COLS = _at
ROWS_OF = ("bv", "bo", "ln1_g", "ln1_b", "b2", "ln2_g", "ln2_b")
GROUP = 32
HPT = P // GROUP
TENSORS = HEADS // HPT


def place_heads(dve, dst, src, head_dim, group, done):
    for copy in range(3):
        dve.tensor_copy(
            dst.rearrange("p l (j r) -> p l j r", r=group)[:, :, :, copy * head_dim:(copy + 1) * head_dim],
            src.rearrange("p l (j c) -> p l j c", c=head_dim)).then_inc(done, 1)


def text_branch(p, tokens, pos, wts, ident, h_txt):
    nc, S = p.nc, p.samples
    U = p.quads
    R = S_TXT
    QW = QUAD * SP_TXT
    SCALE = 1.0 / float(np.sqrt(DH))

    with ExitStack() as ctx:
        def sb(name, shape, dtype=F32):
            return ctx.enter_context(nc.sbuf_tensor("tx_" + name, shape, dtype))

        def sem(name):
            return p.sem("tx_" + name)

        w_all = sb("w_all", [P, LAYERS, W_COLS], F32R)
        w2_all = sb("w2_all", [P, LAYERS, 2, D])
        rows_all = sb("rows_all", [R, LAYERS, len(ROWS_OF), D])
        cols_all = sb("cols_all", [P, LAYERS, 10])
        fin_g, fin_b = sb("fin_g", [R, D]), sb("fin_b", [R, D])
        row_in_group, lo_rows = sb("row_in_group", [P, 1]), sb("lo_rows", [P, 2])
        head_rows = sb("head_rows", [P, HPT])
        V = sb("V", [R, 2, QUAD, HEADS, DH + 1])
        xT = sb("xT", [P, QUAD, SP_TXT], F32R)
        xTf = sb("xTf", [P, 2, QUAD, SP_TXT], F32R)
        oT = sb("oT", [P, QUAD, SP_TXT], F32R)
        QP = sb("QP", [P, 2, TENSORS, SP_TXT], F32R)
        mpad = sb("mpad", [R, TENSORS, P], F32R)
        power = sb("power", [P, QUAD])

        with ExitStack() as setup:
            def tmp(name, shape, dtype=F32):
                return setup.enter_context(nc.sbuf_tensor("tx_" + name, shape, dtype))

            raw = {m: tmp("raw_" + m, [P, LAYERS, FF if m == "W1" else D]) for m in ("Wq", "Wv", "Wo", "W1")}
            q_hi, q_lo = tmp("q_hi", [P, LAYERS, D], F32R), tmp("q_lo", [P, LAYERS, D], F32R)
            row_index = tmp("row_index", [P, 1], I32)
            steps = tmp("steps", [P, 5])
            word = tmp("word", [VOCAB, 1], I32)
            word_f = tmp("word_f", [VOCAB, 1])
            toks = tmp("toks", [VOCAB, S * R], I32)
            emb = tmp("emb", [VOCAB, D])
            pos_sb = tmp("pos", [R, D])
            hot = tmp("hot", [VOCAB, 2, QUAD, R])
            emb_rows = [p.psum(setup, f"tx_emb_rows{k}", [P, QUAD, D]) for k in range(2)]

            w_loaded, small_loaded = sem("w_loaded"), sem("small_loaded")
            tok_loaded = sem("tok_loaded")
            cleared, indexed, masks, cut, placed = (
                sem("cleared"), sem("indexed"), sem("masks"), sem("w_cut"), sem("w_placed"))
            ones_set, hot_made, embedded, summed = (
                sem("ones_set"), sem("hot_made"), sem("embedded"), sem("pos_added"))

            with nc.Block() as block:
                @block.sync
                def _(sp):
                    for m in raw:
                        for half in range(2):
                            sp.dma_start(raw[m][half * D:(half + 1) * D], wts[m].rearrange("l i o -> i l o"))\
                                .then_inc(w_loaded, 16)
                    sp.dma_start(w2_all[:], wts["W2"].rearrange("l (k i) o -> i l k o", i=P)).then_inc(w_loaded, 16)
                    for k, m in enumerate(ROWS_OF):
                        src = wts[m].rearrange("(a l) d -> a l d", a=1).broadcast_to([R, LAYERS, D])
                        sp.dma_start(rows_all[:, :, k], src).then_inc(small_loaded, 16)
                    sp.dma_start(fin_g[:], on_all_rows(wts["fin_g"], R)).then_inc(small_loaded, 16)
                    sp.dma_start(fin_b[:], on_all_rows(wts["fin_b"], R)).then_inc(small_loaded, 16)

                @block.scalar
                def _(act):
                    act.dma_start(toks[:], tokens.rearrange("(a b) t -> a (b t)", a=1).broadcast_to([VOCAB, S * R]))\
                        .then_inc(tok_loaded, 16)
                    act.dma_start(emb[:], wts["emb"]).then_inc(tok_loaded, 16)
                    act.dma_start(pos_sb[:], pos).then_inc(tok_loaded, 16)
                    act.wait_ge(ones_set, 3)
                    with nc.allow_non_contiguous_dma(reason="biases as columns, beside the heads' rows"):
                        for k in range(2):
                            act.dma_start(cols_all[:, :, 8 + k], wts["b1"][:, k * P:(k + 1) * P].rearrange("l i -> i l"))\
                                .then_inc(small_loaded, 16)
                        for at, m in ((0, "bq"), (4, "bv")):
                            for h in range(HEADS):
                                t, j = h // HPT, h % HPT
                                src = wts[m][:, h * DH:(h + 1) * DH].rearrange("l c -> c l")
                                for copy in range(3):
                                    r = GROUP * j + DH * copy
                                    act.dma_start(cols_all[r:r + DH, :, at + t], src).then_inc(small_loaded, 16)
                N_SMALL = len(ROWS_OF) + 2 + 2 + 2 * HEADS * 3

                @block.gpsimd
                def _(pool):
                    pool.memset(V[:], 1.0).then_inc(cleared, 1)
                    pool.memset(power[:], -0.5).then_inc(cleared, 1)
                    for t in (xT, xTf, oT, QP, mpad):
                        pool.memset(t[:].bitcast(F32), 0.0).then_inc(cleared, 1)
                    pool.memset(head_rows[:], 0.0).then_inc(cleared, 1)
                    pool.wait_ge(cleared, 8)
                    for j in range(HPT):
                        rows = slice(GROUP * j, GROUP * (j + 1))
                        pool.memset(head_rows[rows, j:j + 1], 1.0).then_inc(indexed, 1)
                        pool.wait_ge(indexed, 2 * j + 1)
                        pool.iota(row_index[rows], pattern=[[0, 1]], base=0, channel_multiplier=1).then_inc(indexed, 1)
                        pool.wait_ge(indexed, 2 * j + 2)
                    pool.iota(word[:], pattern=[[0, 1]], base=0, channel_multiplier=1).then_inc(indexed, 1)

                @block.vector
                def _(dve):
                    sec = {m: w_all[:, :, a:b] for m, (a, b) in SEC.items()}
                    dve.memset(sec["q"].bitcast(F32), 0.0).then_inc(masks, 1)
                    dve.memset(sec["k"].bitcast(F32), 0.0).then_inc(masks, 1)
                    dve.memset(cols_all[:], 0.0).then_inc(ones_set, 1)
                    dve.wait_ge(indexed, 2 * HPT + 1)
                    dve.tensor_copy(row_in_group[:], row_index[:]).then_inc(masks, 1)
                    dve.tensor_copy(word_f[:], word[:]).then_inc(masks, 1)
                    dve.wait_ge(masks, 4)
                    for k, edge in enumerate((DH, 2 * DH, 3 * DH, 3 * DH + 2)):
                        dve.tensor_scalar(steps[:, k:k + 1], row_in_group[:], float(edge), None, ALU.is_ge)\
                            .then_inc(masks, 1)
                    dve.wait_ge(masks, 8)
                    dve.tensor_tensor(lo_rows[:, 0:1], steps[:, 1:2], steps[:, 2:3], ALU.subtract).then_inc(masks, 1)
                    dve.tensor_tensor(lo_rows[:, 1:2], steps[:, 0:1], steps[:, 1:2], ALU.subtract).then_inc(masks, 1)
                    dve.tensor_tensor(steps[:, 4:5], steps[:, 2:3], steps[:, 3:4], ALU.subtract).then_inc(masks, 1)
                    dve.wait_ge(masks, 11)
                    dve.wait_ge(ones_set, 1)
                    dve.tensor_copy(cols_all[:, :, 4:6], steps[:, 4:5].unsqueeze(1).broadcast_to([P, LAYERS, 2]))\
                        .then_inc(ones_set, 2)
                    dve.wait_ge(w_loaded, 9 * 16)
                    pairs = [(raw["Wq"][:], q_hi[:], q_lo[:]),
                             (raw["Wv"][:], sec["v"][:, :, 0:D], sec["v"][:, :, D:]),
                             (raw["Wo"][:], sec["o"][:, :, 0:D], sec["o"][:, :, D:]),
                             (raw["W1"][:], sec["ff1"][:, :, 0:FF], sec["ff1"][:, :, FF:])]
                    for src, hi, lo in pairs:
                        dve.tensor_copy(hi, src).then_inc(cut, 1)
                    dve.wait_ge(cut, 4)
                    for src, hi, lo in pairs:
                        dve.tensor_tensor(lo, src, hi.bitcast(F32), ALU.subtract).then_inc(cut, 1)
                    dve.wait_ge(cut, 8)
                    for part in range(2):
                        a, b = part * 2 * P, (part + 1) * 2 * P
                        place_heads(dve, sec["q"][:, :, a:b], (q_lo if part else q_hi)[:].bitcast(F32), DH, GROUP, placed)
                        place_heads(dve, sec["k"][:, :, a:b],
                                    sec["v"][:, :, part * D:(part + 1) * D].bitcast(F32), DH, GROUP, placed)
                    dve.wait_ge(small_loaded, N_SMALL * 16)
                    for at, who in ((0, 0), (4, 1)):
                        dve.tensor_scalar(cols_all[:, :, at + 2:at + 4], cols_all[:, :, at:at + 2],
                                          lo_rows[:, who:who + 1], None, ALU.mult)
                    dve.wait_ge(tok_loaded, 48)

                    def quad(n, par, first):
                        if not first:
                            dve.wait_ge(embedded, n - 1)
                        dve.tensor_scalar(hot[:, par].rearrange("v b t -> v (b t)"),
                                          toks[:, bass.ds(n * (QUAD * R), QUAD * R)], word_f[:, 0:1], None,
                                          ALU.is_equal).then_inc(hot_made, 1)
                        dve.wait_ge(embedded, n + 1)
                        dve.tensor_tensor(h_txt[:, bass.ds(n * QUAD, QUAD)], emb_rows[par][0:R],
                                          pos_sb[:].unsqueeze(1).broadcast_to([R, QUAD, D]), ALU.add)\
                            .then_inc(summed, 1)

                    quad(0, 0, True)
                    quad(1, 1, True)
                    with dve.Fori(1, U // 2) as i:
                        quad(i * 2, 0, False)
                        quad(i * 2 + 1, 1, False)

                @block.tensor
                def _(pe):
                    def quad(n, par, first):
                        if not first:
                            pe.wait_ge(summed, n - 1)
                        pe.wait_ge(hot_made, n + 1)
                        for b in range(QUAD):
                            last = pe.matmul(emb_rows[par][0:R, b], hot[:, par, b], emb[:], start=True, stop=True)
                        last.then_inc(embedded, 1)

                    quad(0, 0, True)
                    quad(1, 1, True)
                    with pe.Fori(1, U // 2) as i:
                        quad(i * 2, 0, False)
                        quad(i * 2 + 1, 1, False)

        w = sb("w", [P, W_COLS], F32R)
        w2 = sb("w2", [P, 2, D])
        rows = sb("rows", [R, len(ROWS_OF), D])
        cols = sb("cols", [P, 10])
        xs = sb("xs", [R, QUAD, 2 * D], F32R)
        qk_lo = sb("qk_lo", [P, 2, QW], F32R)
        KF = sb("KF", [P, TENSORS, QW], F32R)
        QF = sb("QF", [P, 2, TENSORS, QUAD, SP_TXT], F32R)
        KB = sb("KB", [P, 2, TENSORS, HPT, QW], F32R)
        mneg = sb("mneg", [R, HEADS])
        PT = sb("PT", [R, 2, TENSORS, HPT * SP_TXT])
        rsum = sb("rsum", [R, QUAD, HEADS])
        o_rows = sb("o_rows", [R, QUAD, D])
        os_ = sb("os", [R, QUAD, 2 * D], F32R)
        y = sb("y", [R, QUAD, D])
        yg = sb("yg", [R, QUAD, D])
        x_shift = sb("x_shift", [R, QUAD, D])
        stats, mean_var = sb("stats", [R, QUAD, 6]), sb("mean_var", [R, QUAD, 2])
        var_eps, rstd = sb("var_eps", [R, QUAD]), sb("rstd", [R, QUAD])
        HT = sb("HT", [P, 2, 2, QW])

        w_set = sem("w_set")
        x_hi, x_cut, x_turned, xT_set = sem("x_hi"), sem("x_cut"), sem("x_turned"), sem("xT_set")
        projected, lo_part, qk_cut, k_split = sem("projected"), sem("lo_part"), sem("qk_cut"), sem("k_split")
        v_made, v_set = sem("v_made"), sem("v_set")
        scored, max_found, max_hi, max_set, max_turned, q_set = (
            sem("scored"), sem("max_found"), sem("max_hi"), sem("max_set"), sem("max_turned"), sem("q_set"))
        scored_t, exped, weighed = sem("scored_t"), sem("exped"), sem("weighed")
        sums_inv, o_set, o_hi, o_cut, o_turned, oT_set = (
            sem("sums_inv"), sem("o_set"), sem("o_hi"), sem("o_cut"), sem("o_turned"), sem("oT_set"))
        y_made, y_set, y_aggr, y_var, y_rstd, y_gain, shifted, x_new = (
            sem("y_made"), sem("y_set"), sem("y_aggr"), sem("y_var"), sem("y_rstd"),
            sem("y_gain"), sem("x_shifted"), sem("x_new"))
        f_hi, f_cut, f_turned, fT_set, f_up, f_gelu = (
            sem("f_hi"), sem("f_cut"), sem("f_turned"), sem("fT_set"), sem("f_up"), sem("f_gelu"))

        scores = p.psum(ctx, "tx_scores", [P, 2, 512])
        scores_t = p.psum(ctx, "tx_scores_t", [P, 2, 512])
        maxT = p.psum(ctx, "tx_maxT", [P, TENSORS, SP_TXT])
        outs = p.psum(ctx, "tx_outs", [P, QUAD, HEADS, DH + 1])
        work = [p.psum(ctx, f"tx_work{k}", [P, 512]) for k in range(2)]

        def sec(m, part, a=0, b=None):
            lo, hi = SEC[m]
            half = (hi - lo) // 2
            return w[:, lo + part * half + a:lo + part * half + (half if b is None else b)]

        def of(m):
            return rows[:, ROWS_OF.index(m)].unsqueeze(1).broadcast_to([R, QUAD, D])

        def quads(n):
            return h_txt[:, bass.ds(n * QUAD, QUAD)]

        def turns(eng, body):
            body(0, 0, True, False, False)
            body(1, 1, False, False, False)
            if U > 4:
                with eng.Fori(1, U // 2 - 1) as i:
                    body(i * 2, 0, False, False, False)
                    body(i * 2 + 1, 1, False, False, False)
            body(U - 2, 0, False, True, False)
            body(U - 1, 1, False, True, True)

        def norm_at(l, g, ff):
            return l * (2 * U) + (U if ff else 0) + g

        def ln_stats(dve, n, y_psum, bias):
            dve.wait_ge(y_made, n + 1)
            dve.tensor_tensor(y[:], y_psum, of(bias), ALU.add).then_inc(y_set, 1)
            dve.wait_ge(y_set, n + 1)
            for b in range(QUAD):
                dve.bn_stats(stats[:, b], y[:, b])
            dve.drain()
            for b in range(QUAD):
                last = dve.bn_aggr(mean_var[:, b], stats[:, b])
            last.then_inc(y_aggr, 1)
            dve.wait_ge(y_aggr, n + 1)
            dve.tensor_scalar(var_eps[:], mean_var[:, :, 1], EPS, None, ALU.add).then_inc(y_var, 1)

        def ln_gain(dve, n, gain):
            for b in range(QUAD):
                last = dve.scalar_tensor_tensor(out=yg[:, b], in0=y[:, b], scalar=mean_var[:, b, 0:1],
                                                in1=rows[:, ROWS_OF.index(gain)], op0=ALU.subtract, op1=ALU.mult)
            last.then_inc(y_gain, 1)

        def ln_sum(dve, n, g):
            dve.wait_ge(y_gain, n + 1)
            dve.wait_ge(y_rstd, n + 1)
            dve.wait_ge(shifted, n + 1)
            for b in range(QUAD):
                last = dve.scalar_tensor_tensor(out=quads(g)[:, b], in0=yg[:, b], scalar=rstd[:, b:b + 1],
                                                in1=x_shift[:, b], op0=ALU.mult, op1=ALU.add)
            last.then_inc(x_new, 1)

        def ln_rstd(pool, n):
            pool.wait_ge(y_var, n + 1)
            pool.tensor_tensor(rstd[:], var_eps[:], power[0:R], ALU.pow).then_inc(y_rstd, 1)

        def ln_shift(pool, n, g, shift, wait):
            if wait:
                pool.wait_ge(x_new, n)
            pool.tensor_tensor(x_shift[:], quads(g), of(shift), ALU.add).then_inc(shifted, 1)

        with nc.Block() as block:
            @block.vector
            def _(dve):
                def set_weights(l):
                    dve.tensor_copy(w[:], w_all[:, bass.ds(l, 1)].rearrange("p a n -> p (a n)").bitcast(F32)).then_inc(w_set, 1)
                    dve.tensor_copy(w2[:], w2_all[:, bass.ds(l, 1)].rearrange("p a k n -> p (a k) n")).then_inc(w_set, 1)
                    dve.tensor_copy(rows[:], rows_all[:, bass.ds(l, 1)].rearrange("p a k n -> p (a k) n")).then_inc(w_set, 1)
                    dve.tensor_copy(cols[:], cols_all[:, bass.ds(l, 1)].rearrange("p a n -> p (a n)")).then_inc(w_set, 1)
                    dve.wait_ge(w_set, l * 4 + 4)

                def cut_qk(n, i, par):
                    t, is_q = i % 2, i // 2
                    dst = QF[:, par, t].rearrange("p b s -> p (b s)") if is_q else KF[:, t]
                    dve.wait_ge(lo_part, n * 4 + i + 1)
                    dve.scalar_tensor_tensor(out=dst, in0=work[(i + 1) % 2][:, 0:QW],
                                             scalar=cols[:, (0 if is_q else 4) + t:(1 if is_q else 5) + t],
                                             in1=qk_lo[:, i % 2].bitcast(F32), op0=ALU.add, op1=ALU.subtract)\
                        .then_inc(qk_cut, 1)

                def set_v(n, par):
                    dve.wait_ge(v_made, n + 1)
                    bias = of("bv").rearrange("p b (h c) -> p b h c", h=HEADS)
                    src = work[1][0:R, 0:QUAD * D].rearrange("p (b h c) -> p b h c", b=QUAD, h=HEADS)
                    dve.tensor_tensor(V[:, par, :, :, 0:DH], src, bias, ALU.add).then_inc(v_set, 1)

                def find_max(nb):
                    dve.wait_ge(scored, nb + 1)
                    dve.tensor_reduce(mneg[:].rearrange("p (t j) -> p t j", t=TENSORS),
                                      scores[0:R, :, 0:HPT * SP_TXT].rearrange("p t (j s) -> p t j s", j=HPT)[:, :, :, 0:R],
                                      AX.X, ALU.max, negate=True).then_inc(max_found, 1)
                    dve.wait_ge(max_found, nb + 1)
                    lanes = mpad[:].rearrange("p t (j r) -> p t j r", r=GROUP)
                    m = mneg[:].rearrange("p (t j) -> p t j", t=TENSORS)
                    dve.tensor_copy(lanes[:, :, :, 3 * DH], m).then_inc(max_hi, 1)
                    dve.wait_ge(max_hi, nb + 1)
                    dve.tensor_tensor(lanes[:, :, :, 3 * DH + 1], m, lanes[:, :, :, 3 * DH].bitcast(F32),
                                      ALU.subtract).then_inc(max_set, 1)

                def join_max(nb, par, b):
                    dve.wait_ge(max_turned, nb + 1)
                    dve.tensor_tensor(QP[:, b % 2, :, 0:R], maxT[:, :, 0:R], QF[:, par, :, b, 0:R].bitcast(F32),
                                      ALU.add).then_inc(q_set, 1)

                def normalise_o(n):
                    dve.wait_ge(weighed, n * QUAD + QUAD)
                    dve.reciprocal(rsum[:], outs[0:R, :, :, DH]).then_inc(sums_inv, 1)
                    dve.wait_ge(sums_inv, n + 1)
                    dve.tensor_tensor(o_rows[:].rearrange("p b (h c) -> p b h c", h=HEADS), outs[0:R, :, :, 0:DH],
                                      rsum[:].unsqueeze(3).broadcast_to([R, QUAD, HEADS, DH]), ALU.mult)\
                        .then_inc(o_set, 1)

                y_rows = work[1][0:R, 0:QUAD * D].rearrange("p (b d) -> p b d", b=QUAD)

                with dve.Fori(0, LAYERS) as l:
                    set_weights(l)
                    for i in range(4):
                        cut_qk(l * U, i, 0)
                    set_v(l * U, 0)
                    find_max(l * U * QUAD)
                    join_max(l * U * QUAD, 0, 0)

                    def attention(g, par, first, last2, last):
                        n = l * U + g
                        ln = norm_at(l, g - 1, False)
                        for b in range(QUAD):
                            if b < QUAD - 1:
                                find_max(n * QUAD + b + 1)
                                join_max(n * QUAD + b + 1, par, b + 1)
                            elif not last:
                                find_max(n * QUAD + QUAD)
                                join_max(n * QUAD + QUAD, 1 - par, 0)
                            if b == 0:
                                if not first:
                                    normalise_o(n - 1)
                                if not last:
                                    cut_qk(n + 1, 0, 1 - par)
                                    cut_qk(n + 1, 1, 1 - par)
                            if b == 1 and not last:
                                cut_qk(n + 1, 2, 1 - par)
                                cut_qk(n + 1, 3, 1 - par)
                            if b == 2:
                                if not last:
                                    set_v(n + 1, 1 - par)
                                if not first:
                                    ln_stats(dve, ln, y_rows, "bo")
                                    ln_gain(dve, ln, "ln1_g")
                            if b == 3 and not first:
                                ln_sum(dve, ln, g - 1)
                        if last:
                            ln = norm_at(l, g, False)
                            normalise_o(n)
                            ln_stats(dve, ln, y_rows, "bo")
                            ln_gain(dve, ln, "ln1_g")
                            ln_sum(dve, ln, g)

                    turns(dve, attention)

                    def feed_forward(g, par, first, last2, last):
                        ln = norm_at(l, g, True)
                        ln_stats(dve, ln, y_rows, "b2")
                        ln_gain(dve, ln, "ln2_g")
                        ln_sum(dve, ln, g)

                    turns(dve, feed_forward)

            @block.gpsimd
            def _(pool):
                def cut(rows_f32, split, hi_ready, done, n):
                    pool.wait_ge(hi_ready, n + 1)
                    pool.tensor_tensor(split[:, :, D:], rows_f32, split[:, :, 0:D].bitcast(F32), ALU.subtract)\
                        .then_inc(done, 1)

                def split_k(n, par):
                    for t in range(TENSORS):
                        pool.wait_ge(qk_cut, n * 4 + t + 1)
                        pool.tensor_tensor(KB[:, par, t], KF[:, t].bitcast(F32).unsqueeze(1).broadcast_to([P, HPT, QW]),
                                           head_rows[:].unsqueeze(2).broadcast_to([P, HPT, QW]), ALU.mult)\
                            .then_inc(k_split, 1)

                with pool.Fori(0, LAYERS) as l:
                    pool.wait_ge(w_set, l * 4 + 4)
                    cut(quads(0), xs, x_hi, x_cut, l * U)
                    split_k(l * U, 0)
                    cut(quads(1), xs, x_hi, x_cut, l * U + 1)

                    def attention(g, par, first, last2, last):
                        n = l * U + g
                        ln = norm_at(l, g - 1, False)
                        if not first:
                            cut(o_rows[:], os_, o_hi, o_cut, n - 1)
                            ln_shift(pool, ln, g - 1, "ln1_b", not (isinstance(g, int) and g == 1))
                        if not last:
                            split_k(n + 1, 1 - par)
                        if not first:
                            ln_rstd(pool, ln)
                        if not last2:
                            cut(quads(g + 2), xs, x_hi, x_cut, n + 2)
                        if last:
                            ln = norm_at(l, g, False)
                            cut(o_rows[:], os_, o_hi, o_cut, n)
                            ln_shift(pool, ln, g, "ln1_b", True)
                            ln_rstd(pool, ln)

                    turns(pool, attention)
                    cut(quads(0), xs, f_hi, f_cut, l * U)
                    cut(quads(1), xs, f_hi, f_cut, l * U + 1)

                    def feed_forward(g, par, first, last2, last):
                        n, ln = l * U + g, norm_at(l, g, True)
                        if not last2:
                            cut(quads(g + 2), xs, f_hi, f_cut, n + 2)
                        ln_shift(pool, ln, g, "ln2_b", True)
                        ln_rstd(pool, ln)

                    turns(pool, feed_forward)

            @block.scalar
            def _(act):
                def hi(rows_f32, split, done):
                    act.activation(split[:, :, 0:D], rows_f32, ACT.Copy).then_inc(done, 1)

                def set_turned(dst, turned, done, n):
                    act.wait_ge(turned, n + 1)
                    act.activation(dst[:, :, 0:R], work[0][:, 0:QUAD * R].rearrange("p (b s) -> p b s", b=QUAD), ACT.Copy)\
                        .then_inc(done, 1)

                def part_lo(n, i):
                    t, is_q = i % 2, i // 2
                    at = (2 if is_q else 6) + t
                    act.wait_ge(projected, n * 4 + i + 1)
                    act.activation(qk_lo[:, i % 2], work[(i + 1) % 2][:, 0:QW], ACT.Identity,
                                   bias=cols[:, at:at + 1], scale=lo_rows[:, 1 - is_q:2 - is_q]).then_inc(lo_part, 1)

                def exp(nb, b):
                    act.wait_ge(scored_t, nb + 1)
                    act.activation(PT[:, b % 2], scores_t[0:R, :, 0:HPT * SP_TXT], ACT.Exp, scale=SCALE)\
                        .then_inc(exped, 1)

                def gelu(n, par):
                    act.wait_ge(f_up, n + 1)
                    for half in range(2):
                        src = (scores_t if par else scores)[:, half, 0:QW]
                        last = act.activation(HT[:, par, half], src, ACT.Gelu, bias=cols[:, 8 + half:9 + half])
                    last.then_inc(f_gelu, 1)

                with act.Fori(0, LAYERS) as l:
                    act.wait_ge(w_set, l * 4 + 4)
                    hi(quads(0), xs, x_hi)
                    set_turned(xT, x_turned, xT_set, l * U)
                    for i in range(4):
                        part_lo(l * U, i)
                    hi(quads(1), xs, x_hi)

                    def attention(g, par, first, last2, last):
                        n = l * U + g
                        for b in range(QUAD):
                            if b == 0 and not last:
                                set_turned(xT, x_turned, xT_set, n + 1)
                            exp(n * QUAD + b, b)
                            if b == 0:
                                if not last:
                                    part_lo(n + 1, 0)
                                    part_lo(n + 1, 1)
                                if not first:
                                    act.wait_ge(o_set, n)
                                    hi(o_rows[:], os_, o_hi)
                            if b == 1:
                                if not last:
                                    part_lo(n + 1, 2)
                                    part_lo(n + 1, 3)
                                if not first:
                                    set_turned(oT, o_turned, oT_set, n - 1)
                        if not last2:
                            hi(quads(g + 2), xs, x_hi)
                        if last:
                            act.wait_ge(o_set, n + 1)
                            hi(o_rows[:], os_, o_hi)
                            set_turned(oT, o_turned, oT_set, n)

                    turns(act, attention)
                    act.wait_ge(x_new, norm_at(l, 0, False) + 1)
                    hi(quads(0), xs, f_hi)
                    set_turned(xTf[:, 0], f_turned, fT_set, l * U)
                    gelu(l * U, 0)
                    act.wait_ge(x_new, norm_at(l, 1, False) + 1)
                    hi(quads(1), xs, f_hi)
                    set_turned(xTf[:, 1], f_turned, fT_set, l * U + 1)

                    def feed_forward(g, par, first, last2, last):
                        n = l * U + g
                        if not last2:
                            act.wait_ge(x_new, norm_at(l, g + 2, False) + 1)
                            hi(quads(g + 2), xs, f_hi)
                        if not last:
                            gelu(n + 1, 1 - par)
                        if not last2:
                            set_turned(xTf[:, par], f_turned, fT_set, n + 2)

                    turns(act, feed_forward)

            @block.tensor
            def _(pe):
                def turn(src, ready, done, n):
                    pe.wait_ge(ready, n + 1)
                    for b in range(QUAD):
                        last = pe.transpose(work[0][:, b * R:(b + 1) * R], src[:, b].bitcast(F32), ident[0:R, 0:R])
                    last.then_inc(done, 1)

                def project(n, i):
                    t, m = i % 2, "q" if i // 2 else "k"
                    if i >= 2:
                        pe.wait_ge(qk_cut, n * 4 + i - 1)
                    for part in range(2):
                        last = pe.matmul(work[(i + 1) % 2][:, 0:QW], sec(m, part, t * P, (t + 1) * P),
                                         xT[:].rearrange("p b s -> p (b s)"), start=part == 0, stop=part == 1)
                    last.then_inc(projected, 1)

                def project_v(n):
                    pe.wait_ge(qk_cut, n * 4 + 3)
                    for b in range(QUAD):
                        for part in range(2):
                            last = pe.matmul(work[1][0:R, b * D:(b + 1) * D], xT[:, b, 0:R], sec("v", part),
                                             start=part == 0, stop=part == 1)
                    last.then_inc(v_made, 1)

                def score(n, par, b):
                    if b == 0:
                        pe.wait_ge(k_split, n * 2 + 2)
                        pe.wait_ge(qk_cut, n * 4 + 4)
                    for t in range(TENSORS):
                        k = KB[:, par, t].rearrange("p j (b s) -> p j b s", b=QUAD)[:, :, b]
                        last = pe.matmul(scores[0:R, t, 0:HPT * SP_TXT], QF[:, par, t, b, 0:R], k, start=True, stop=True)
                    last.then_inc(scored, 1)

                def turn_max(nb):
                    pe.wait_ge(max_set, nb + 1)
                    for t in range(TENSORS):
                        last = pe.transpose(maxT[:, t, 0:R], mpad[:, t].bitcast(F32), ident[0:R, 0:R])
                    last.then_inc(max_turned, 1)

                def score_t(n, par, b, fresh):
                    nb = n * QUAD + b
                    pe.wait_ge(q_set, nb + 1)
                    if not fresh:
                        pe.wait_ge(exped, nb)
                    for t in range(TENSORS):
                        for j in range(HPT):
                            k = KB[:, par, t, j].rearrange("p (b s) -> p b s", b=QUAD)[:, b, 0:R]
                            last = pe.matmul(scores_t[0:R, t, j * SP_TXT:(j + 1) * SP_TXT], k, QP[:, b % 2, t],
                                             start=True, stop=True)
                    last.then_inc(scored_t, 1)

                def weigh(n, par, b, fresh):
                    pe.wait_ge(exped, n * QUAD + b + 1)
                    if b == 0:
                        pe.wait_ge(v_set, n + 1)
                        if not fresh:
                            pe.wait_ge(o_set, n)
                    for h in range(HEADS):
                        t, j = h // HPT, h % HPT
                        last = pe.matmul(outs[0:R, b, h], PT[:, b % 2, t, j * SP_TXT:j * SP_TXT + R], V[:, par, b, h],
                                         start=True, stop=True)
                    last.then_inc(weighed, 1)

                def project_o(n, ln, bank_ready):
                    pe.wait_ge(oT_set, n + 1)
                    pe.wait_ge(*bank_ready)
                    for b in range(QUAD):
                        for part in range(2):
                            last = pe.matmul(work[1][0:R, b * D:(b + 1) * D], oT[:, b, 0:R], sec("o", part),
                                             start=part == 0, stop=part == 1)
                    last.then_inc(y_made, 1)

                def up(n, par):
                    pe.wait_ge(fT_set, n + 1)
                    for half in range(2):
                        for part in range(2):
                            last = pe.matmul((scores_t if par else scores)[:, half, 0:QW],
                                             sec("ff1", part, half * P, (half + 1) * P),
                                             xTf[:, par].rearrange("p b s -> p (b s)"), start=part == 0, stop=part == 1)
                    last.then_inc(f_up, 1)

                def down(n, ln, par):
                    pe.wait_ge(f_gelu, n + 1)
                    pe.wait_ge(y_set, ln)
                    for b in range(QUAD):
                        for half in range(2):
                            last = pe.matmul(work[1][0:R, b * D:(b + 1) * D],
                                             HT[:, par, half].rearrange("p (b s) -> p b s", b=QUAD)[:, b, 0:R],
                                             w2[:, half], start=half == 0, stop=half == 1)
                    last.then_inc(y_made, 1)

                with pe.Fori(0, LAYERS) as l:
                    pe.wait_ge(w_set, l * 4 + 4)
                    turn(xs, x_cut, x_turned, l * U)
                    pe.wait_ge(xT_set, l * U + 1)
                    for i in range(4):
                        project(l * U, i)
                    project_v(l * U)
                    score(l * U, 0, 0)
                    turn_max(l * U * QUAD)

                    def attention(g, par, first, last2, last):
                        n = l * U + g
                        ln = norm_at(l, g - 1, False)
                        for b in range(QUAD):
                            if b == 0 and not last:
                                turn(xs, x_cut, x_turned, n + 1)
                            score_t(n, par, b, first and b == 0)
                            if b < QUAD - 1:
                                score(n, par, b + 1)
                            elif not last:
                                score(n + 1, 1 - par, 0)
                            if b > 0:
                                weigh(n, par, b - 1, first)
                            elif not first:
                                weigh(n - 1, 1 - par, QUAD - 1, True)
                            if b < QUAD - 1:
                                turn_max(n * QUAD + b + 1)
                            elif not last:
                                turn_max(n * QUAD + QUAD)
                            if b == 0 and not last:
                                pe.wait_ge(xT_set, n + 2)
                                if first or isinstance(g, int) and g == 1:
                                    pe.wait_ge(v_set, n + 1)
                                else:
                                    pe.wait_ge(y_set, ln)
                                project(n + 1, 0)
                                project(n + 1, 1)
                            if b == 1:
                                if not last:
                                    project(n + 1, 2)
                                    project(n + 1, 3)
                                    if not first:
                                        pe.wait_ge(qk_cut, n * 4 + 8)
                                if not first:
                                    turn(os_, o_cut, o_turned, n - 1)
                            if b == 2:
                                if not last:
                                    project_v(n + 1)
                                if not first:
                                    project_o(n - 1, ln, (y_set, ln) if last else (v_set, n + 2))
                        if last:
                            weigh(n, par, QUAD - 1, True)
                            turn(os_, o_cut, o_turned, n)
                            project_o(n, norm_at(l, g, False), (y_set, ln + 1))

                    turns(pe, attention)
                    turn(xs, f_cut, f_turned, l * U)
                    up(l * U, 0)
                    turn(xs, f_cut, f_turned, l * U + 1)

                    def feed_forward(g, par, first, last2, last):
                        n = l * U + g
                        if not last:
                            up(n + 1, 1 - par)
                        down(n, norm_at(l, g, True), par)
                        if not last2:
                            turn(xs, f_cut, f_turned, n + 2)

                    turns(pe, feed_forward)

        end_aggr, end_var, end_rstd, end_scaled, end_done = (
            sem("end_aggr"), sem("end_var"), sem("end_rstd"), sem("end_scaled"), sem("end_done"))

        def over_quads(eng, body):
            body(0, 0, True)
            body(1, 1, True)
            with eng.Fori(1, U // 2) as i:
                body(i * 2, 0, False)
                body(i * 2 + 1, 1, False)

        with nc.Block() as block:
            @block.vector
            def _(dve):
                def quad(n, par, first):
                    q = quads(n)
                    for b in range(QUAD):
                        dve.bn_stats(stats[:, b], q[:, b])
                    dve.drain()
                    for b in range(QUAD):
                        last = dve.bn_aggr(mean_var[:, b], stats[:, b])
                    last.then_inc(end_aggr, 1)
                    dve.wait_ge(end_aggr, n + 1)
                    dve.tensor_scalar(var_eps[:], mean_var[:, :, 1], EPS, None, ALU.add).then_inc(end_var, 1)
                    for b in range(QUAD):
                        last = dve.scalar_tensor_tensor(out=yg[:, b], in0=q[:, b], scalar=mean_var[:, b, 0:1],
                                                        in1=fin_g[:], op0=ALU.subtract, op1=ALU.mult)
                    last.then_inc(end_scaled, 1)
                    dve.wait_ge(end_scaled, n + 1)
                    dve.wait_ge(end_rstd, n + 1)
                    for b in range(QUAD):
                        last = dve.scalar_tensor_tensor(out=q[:, b], in0=yg[:, b], scalar=rstd[:, b:b + 1],
                                                        in1=fin_b[:], op0=ALU.mult, op1=ALU.add)
                    last.then_inc(end_done, 1)

                over_quads(dve, quad)

            @block.gpsimd
            def _(pool):
                def quad(n, par, first):
                    pool.wait_ge(end_var, n + 1)
                    pool.tensor_tensor(rstd[:], var_eps[:], power[0:R], ALU.pow).then_inc(end_rstd, 1)

                over_quads(pool, quad)



SEQ = T + S_TXT
SEQP = SEQ + 1
TILES = ((0, T), (T, S_TXT))
A_HEADS = 4
A_DH = D // A_HEADS
A_GROUP = 64
A_HPT = P // A_GROUP
A_TENSORS = A_HEADS // A_HPT
A_HALF = A_TENSORS * P
CLIP = 10000.0
EXPERTS = 8


def live(n):
    return not isinstance(n, int) or 0 <= n < B


def due(value):
    return not isinstance(value, int) or value > 0


def set_stats(dve, rows_of, mean_var, stats, var_eps, aggregated, var_ready, m):
    for t, (_, n) in enumerate(TILES):
        dve.bn_stats(stats[0:n, t], rows_of(m, t))
    dve.drain()
    for t, (_, n) in enumerate(TILES):
        last = dve.bn_aggr(mean_var[0:n, t], stats[0:n, t])
    last.then_inc(aggregated, 1)
    dve.wait_ge(aggregated, m + 1)
    dve.tensor_scalar(var_eps[:], mean_var[:, :, 1], EPS, None, ALU.add).then_inc(var_ready, 1)


def fusion_attention(p, wts, ident, rows_of):
    nc = p.nc
    SCALE = 1.0 / float(np.sqrt(A_DH))

    with ExitStack() as ctx:
        def sb(name, shape, dtype=F32):
            return ctx.enter_context(nc.sbuf_tensor("at_" + name, shape, dtype))

        def sem(name):
            return p.sem("at_" + name)

        wq, wk = sb("wq", [P, 2, A_HALF], F32R), sb("wk", [P, 2, A_HALF], F32R)
        wv, wo = sb("wv", [P, 2, D], F32R), sb("wo", [D + 1, 2, D], F32R)
        bv = sb("bv", [P, D])
        cols = sb("cols", [P, 8])
        lo_rows, head_rows = sb("lo_rows", [P, 2]), sb("head_rows", [P, A_HPT])
        power = sb("power", [P, 2])

        stats, mean_var = sb("stats", [P, 2, 6]), sb("mean_var", [P, 2, 2])
        var_eps, rstd = sb("var_eps", [P, 2]), sb("rstd", [P, 2])
        z, zc = sb("z", [P, 2, D]), sb("zc", [P, 2, D])
        xs = sb("xs", [P, 2, 2 * D], F32R)
        xT = sb("xT", [P, SEQP], F32R)
        qk_lo = sb("qk_lo", [P, 2, SEQP], F32R)
        KF = sb("KF", [P, A_TENSORS, SEQP], F32R)
        QF = sb("QF", [P, 2, A_TENSORS, SEQP], F32R)
        KB = sb("KB", [P, 2, A_TENSORS, A_HPT, SEQP], F32R)
        QP = sb("QP", [P, 2, A_TENSORS, SEQP], F32R)
        mneg = sb("mneg", [P, 2, A_HEADS])
        mpad = sb("mpad", [P, 2, A_TENSORS, P], F32R)
        PT = sb("PT", [P, 2, A_TENSORS, A_HPT * SEQP])
        V = sb("V", [P, 2, 2, A_HEADS, A_DH + 1])
        rsum = sb("rsum", [P, 2, A_HEADS])
        o_rows = sb("o_rows", [P, 2, 2, P], BF16)
        oT = sb("oT", [D + 1, SEQP], F32R)
        ident_bf = sb("ident_bf", [P, P], BF16)

        scores = p.psum(ctx, "at_scores", [P, 2, 512])
        scores_t = p.psum(ctx, "at_scores_t", [P, 2, 512])
        maxT = p.psum(ctx, "at_maxT", [P, A_TENSORS, SEQP])
        outs = p.psum(ctx, "at_outs", [P, 2, A_HEADS, A_DH + 1])
        work = [p.psum(ctx, f"at_work{k}", [P, 512]) for k in range(2)]

        with ExitStack() as setup:
            def tmp(name, shape, dtype=F32):
                return setup.enter_context(nc.sbuf_tensor("at_" + name, shape, dtype))

            MATS = ("Wq", "Wk", "Wv", "Wo")
            raw = tmp("raw", [D, len(MATS), 2 * D])
            hi, lo = tmp("hi", [P, len(MATS), D], F32R), tmp("lo", [P, len(MATS), D], F32R)
            bo = tmp("bo", [D + 1, D])
            row_index = tmp("row_index", [P, 1], I32)
            row_in_group = tmp("row_in_group", [P, 1])
            steps = tmp("steps", [P, 5])
            w_loaded, cols_loaded, cleared, indexed, masks, ones_set = (
                sem("w_loaded"), sem("cols_loaded"), sem("cleared"), sem("indexed"), sem("masks"), sem("ones_set"))
            turned, w_hi, w_lo, placed = sem("w_turned"), sem("w_hi"), sem("w_lo"), sem("w_placed")
            turn = work[0][:, 0:len(MATS) * D].rearrange("p (m o) -> p m o", m=len(MATS))

            with nc.Block() as block:
                @block.sync
                def _(sp):
                    for k, m in enumerate(MATS):
                        for half in range(2):
                            sp.dma_start(raw[:, k, half * D:(half + 1) * D], wts[m]).then_inc(w_loaded, 16)
                    sp.dma_start(bv[:], on_all_rows(wts["bv"])).then_inc(w_loaded, 16)
                    sp.dma_start(bo[D:D + 1], row(wts["bo"])).then_inc(w_loaded, 16)

                @block.scalar
                def _(act):
                    act.wait_ge(ones_set, 3)
                    with nc.allow_non_contiguous_dma(reason="biases as columns, beside the heads' rows"):
                        for at, m in ((0, "bq"), (4, "bk")):
                            for h in range(A_HEADS):
                                t, j = h // A_HPT, h % A_HPT
                                src = wts[m][h * A_DH:(h + 1) * A_DH].rearrange("(n a) -> n a", a=1)
                                for copy in range(3):
                                    r = A_GROUP * j + A_DH * copy
                                    act.dma_start(cols[r:r + A_DH, at + t:at + t + 1], src).then_inc(cols_loaded, 16)
                    act.wait_ge(turned, 1)
                    act.activation(hi[:], turn, ACT.Copy).then_inc(w_hi, 1)
                N_COLS = 2 * A_HEADS * 3

                @block.gpsimd
                def _(pool):
                    pool.memset(V[:], 1.0).then_inc(cleared, 1)
                    pool.memset(power[:], -0.5).then_inc(cleared, 1)
                    for t in (xT, QP, mpad):
                        pool.memset(t[:].bitcast(F32), 0.0).then_inc(cleared, 1)
                    pool.memset(oT[:].bitcast(F32), 1.0).then_inc(cleared, 1)
                    for t in (mneg, z, mean_var, head_rows, o_rows):
                        pool.memset(t[:], 0.0).then_inc(cleared, 1)
                    pool.tensor_copy(ident_bf[:], ident[:]).then_inc(cleared, 1)
                    pool.wait_ge(cleared, 12)
                    for j in range(A_HPT):
                        rows = slice(A_GROUP * j, A_GROUP * (j + 1))
                        pool.memset(head_rows[rows, j:j + 1], 1.0).then_inc(indexed, 1)
                        pool.wait_ge(indexed, 2 * j + 1)
                        pool.iota(row_index[rows], pattern=[[0, 1]], base=0, channel_multiplier=1).then_inc(indexed, 1)
                        pool.wait_ge(indexed, 2 * j + 2)

                @block.tensor
                def _(pe):
                    pe.wait_ge(w_loaded, 10 * 16)
                    for k in range(len(MATS)):
                        last = pe.transpose(turn[:, k], raw[:, k], ident[0:D, 0:D])
                    last.then_inc(turned, 1)

                @block.vector
                def _(dve):
                    dve.memset(wq[:].bitcast(F32), 0.0).then_inc(masks, 1)
                    dve.memset(wk[:].bitcast(F32), 0.0).then_inc(masks, 1)
                    dve.memset(cols[:], 0.0).then_inc(ones_set, 1)
                    dve.memset(outs[:], 1.0).then_inc(masks, 1)
                    dve.wait_ge(indexed, 2 * A_HPT)
                    dve.tensor_copy(row_in_group[:], row_index[:]).then_inc(masks, 1)
                    dve.wait_ge(masks, 4)
                    for k, edge in enumerate((A_DH, 2 * A_DH, 3 * A_DH, 3 * A_DH + 2)):
                        dve.tensor_scalar(steps[:, k:k + 1], row_in_group[:], float(edge), None, ALU.is_ge)\
                            .then_inc(masks, 1)
                    dve.wait_ge(masks, 8)
                    dve.tensor_tensor(lo_rows[:, 0:1], steps[:, 1:2], steps[:, 2:3], ALU.subtract).then_inc(masks, 1)
                    dve.tensor_tensor(lo_rows[:, 1:2], steps[:, 0:1], steps[:, 1:2], ALU.subtract).then_inc(masks, 1)
                    dve.tensor_tensor(steps[:, 4:5], steps[:, 2:3], steps[:, 3:4], ALU.subtract).then_inc(masks, 1)
                    dve.wait_ge(masks, 11)
                    dve.wait_ge(ones_set, 1)
                    dve.tensor_copy(cols[:, 4:6], steps[:, 4:5].broadcast_to([P, 2])).then_inc(ones_set, 2)
                    dve.wait_ge(w_hi, 1)
                    dve.tensor_tensor(lo[:], turn, hi[:].bitcast(F32), ALU.subtract).then_inc(w_lo, 1)
                    dve.tensor_copy(wo[D:D + 1, 0], bo[D:D + 1]).then_inc(w_lo, 1)
                    dve.wait_ge(w_lo, 2)
                    for part, src in ((0, hi), (1, lo)):
                        for k, dst in ((0, wq), (1, wk)):
                            place_heads(dve, dst[:, part:part + 1], src[:, k:k + 1].bitcast(F32), A_DH, A_GROUP, placed)
                        dve.tensor_copy(wv[:, part], src[:, 2].bitcast(F32))
                        dve.tensor_copy(wo[0:D, part], src[0:D, 3].bitcast(F32))
                    dve.tensor_tensor(wo[D:D + 1, 1], bo[D:D + 1], wo[D:D + 1, 0].bitcast(F32), ALU.subtract)
                    dve.wait_ge(cols_loaded, N_COLS * 16)
                    for at, who in ((0, 0), (4, 1)):
                        dve.tensor_scalar(cols[:, at + 2:at + 4], cols[:, at:at + 2], lo_rows[:, who:who + 1],
                                          None, ALU.mult)

        aggregated, var_ready, rstd_ready, normed, z_ready, x_hi, x_cut, x_turned, xT_set = (
            sem("aggregated"), sem("var_ready"), sem("rstd_ready"), sem("normed"), sem("z_ready"), sem("x_hi"),
            sem("x_cut"), sem("x_turned"), sem("xT_set"))
        projected, lo_part, qk_cut, k_split, v_made, v_set = (
            sem("projected"), sem("lo_part"), sem("qk_cut"), sem("k_split"), sem("v_made"), sem("v_set"))
        scored, max_found, max_hi, max_set, max_turned, q_set = (
            sem("scored"), sem("max_found"), sem("max_hi"), sem("max_set"), sem("max_turned"), sem("q_set"))
        scored_t, exped, weighed, sums_inv, o_set, o_turned, oT_set, y_made, y_added = (
            sem("scored_t"), sem("exped"), sem("weighed"), sem("sums_inv"), sem("o_set"), sem("o_turned"),
            sem("oT_set"), sem("y_made"), sem("y_added"))

        def each_step(eng, step):
            for n in range(-3, 2):
                step(n, n % 2)
            with eng.Fori(1, B // 2 - 2) as i:
                step(i * 2, 0)
                step(i * 2 + 1, 1)
            for n in range(B - 4, B + 1):
                step(n, n % 2)

        with nc.Block() as block:
            @block.vector
            def _(dve):
                def find_max(m, tile):
                    n = TILES[tile][1]
                    dve.wait_ge(scored, m * 2 + (tile + 1))
                    dve.tensor_reduce(mneg[0:n, tile].rearrange("p (t j) -> p t j", t=A_TENSORS),
                                      scores[0:n, :, 0:A_HPT * SEQP].rearrange("p t (j s) -> p t j s", j=A_HPT)[:, :, :, 0:SEQ],
                                      AX.X, ALU.max, negate=True).then_inc(max_found, 1)

                def set_max(m):
                    lanes = mpad[:].rearrange("p a t (j r) -> p (a t) j r", r=A_GROUP)
                    v = mneg[:].rearrange("p a (t j) -> p (a t) j", t=A_TENSORS)
                    dve.wait_ge(max_found, m * 2 + 2)
                    dve.tensor_copy(lanes[:, :, :, 3 * A_DH], v).then_inc(max_hi, 1)
                    dve.wait_ge(max_hi, m + 1)
                    dve.tensor_tensor(lanes[:, :, :, 3 * A_DH + 1], v, lanes[:, :, :, 3 * A_DH].bitcast(F32),
                                      ALU.subtract).then_inc(max_set, 1)

                def join_max(m, par):
                    dve.wait_ge(max_turned, m + 1)
                    if due(m * 2 - 2):
                        dve.wait_ge(scored_t, m * 2 - 2)
                    dve.tensor_tensor(QP[:, par, :, 0:SEQ], maxT[:, :, 0:SEQ], QF[:, par, :, 0:SEQ].bitcast(F32),
                                      ALU.add).then_inc(q_set, 1)

                def cut_qk(m, i, par):
                    t, is_q = i % 2, i // 2
                    dst = QF[:, par, t] if is_q else KF[:, t]
                    dve.wait_ge(lo_part, m * 4 + (i + 1))
                    if i == 0 and due(m * 2):
                        dve.wait_ge(k_split, m * 2)
                    dve.scalar_tensor_tensor(out=dst, in0=work[(i + 1) % 2][:, 0:SEQP],
                                             scalar=cols[:, (0 if is_q else 4) + t:(1 if is_q else 5) + t],
                                             in1=qk_lo[:, i % 2].bitcast(F32), op0=ALU.add, op1=ALU.subtract)\
                        .then_inc(qk_cut, 1)

                def set_v(m, par):
                    dve.wait_ge(v_made, m + 1)
                    if due(m - 1):
                        dve.wait_ge(weighed, m - 1)
                    for tile, (_, n) in enumerate(TILES):
                        last = dve.tensor_tensor(
                            V[0:n, par, tile, :, 0:A_DH],
                            work[1][0:n, tile * D:(tile + 1) * D].rearrange("p (h c) -> p h c", h=A_HEADS),
                            bv[0:n].rearrange("p (h c) -> p h c", h=A_HEADS), ALU.add)
                    last.then_inc(v_set, 1)

                def norm_z(m):
                    dve.wait_ge(rstd_ready, m + 1)
                    for tile, (_, n) in enumerate(TILES):
                        last = dve.tensor_scalar(z[0:n, tile], rows_of(m, tile), mean_var[0:n, tile, 0:1],
                                                 rstd[0:n, tile:tile + 1], ALU.subtract, ALU.mult)
                    last.then_inc(normed, 1)
                    dve.wait_ge(normed, m + 1)
                    if due(m):
                        dve.wait_ge(x_cut, m)
                    dve.tensor_scalar(zc[:], z[:], -CLIP, CLIP, ALU.max, ALU.min).then_inc(z_ready, 1)

                def normalise_o(m, par):
                    dve.wait_ge(weighed, m + 1)
                    if due(m - 1):
                        dve.wait_ge(o_turned, m - 1)
                    dve.reciprocal(rsum[:], outs[:, :, :, A_DH]).then_inc(sums_inv, 1)
                    dve.wait_ge(sums_inv, m + 1)
                    dve.tensor_tensor(o_rows[:, par, :, 0:D].rearrange("p a (h c) -> p a h c", h=A_HEADS), outs[:, :, :, 0:A_DH],
                                      rsum[:].unsqueeze(3).broadcast_to([P, 2, A_HEADS, A_DH]), ALU.mult)\
                        .then_inc(o_set, 1)

                def add_y(m):
                    dve.wait_ge(y_made, m + 1)
                    for tile, (_, n) in enumerate(TILES):
                        last = dve.tensor_tensor(rows_of(m, tile), rows_of(m, tile),
                                                 work[1][0:n, tile * D:(tile + 1) * D], ALU.add)
                    last.then_inc(y_added, 1)

                def step(n, par):
                    if live(n + 3):
                        set_stats(dve, rows_of, mean_var, stats, var_eps, aggregated, var_ready, n + 3)
                    if live(n + 1):
                        find_max(n + 1, 0)
                    if live(n + 2):
                        cut_qk(n + 2, 0, par)
                        cut_qk(n + 2, 1, par)
                    if live(n + 1):
                        find_max(n + 1, 1)
                        set_max(n + 1)
                    if live(n + 3):
                        norm_z(n + 3)
                    if live(n + 1):
                        join_max(n + 1, 1 - par)
                    if live(n + 2):
                        cut_qk(n + 2, 2, par)
                        cut_qk(n + 2, 3, par)
                        set_v(n + 2, par)
                    if live(n):
                        normalise_o(n, par)
                    if live(n - 1):
                        add_y(n - 1)

                each_step(dve, step)

            @block.gpsimd
            def _(pool):
                def step(n, par):
                    if live(n + 3):
                        pool.wait_ge(var_ready, n + 4)
                        pool.tensor_tensor(rstd[:], var_eps[:], power[:], ALU.pow).then_inc(rstd_ready, 1)
                    if live(n + 2):
                        m = n + 2
                        if due(m * 2 - 2):
                            pool.wait_ge(scored_t, m * 2 - 2)
                        for t in range(A_TENSORS):
                            pool.wait_ge(qk_cut, m * 4 + (t + 1))
                            pool.tensor_tensor(KB[:, par, t],
                                               KF[:, t].bitcast(F32).unsqueeze(1).broadcast_to([P, A_HPT, SEQP]),
                                               head_rows[:].unsqueeze(2).broadcast_to([P, A_HPT, SEQP]), ALU.mult)\
                                .then_inc(k_split, 1)
                    if live(n + 3):
                        pool.wait_ge(x_hi, n + 4)
                        pool.tensor_tensor(xs[:, :, D:], zc[:], xs[:, :, 0:D].bitcast(F32), ALU.subtract)\
                            .then_inc(x_cut, 1)

                each_step(pool, step)

            @block.scalar
            def _(act):
                def exp(m, tile):
                    n = TILES[tile][1]
                    act.wait_ge(scored_t, m * 2 + (tile + 1))
                    if tile == 0 and due(m):
                        act.wait_ge(weighed, m)
                    act.activation(PT[0:n, tile], scores_t[0:n, :, 0:A_HPT * SEQP], ACT.Exp, scale=SCALE)\
                        .then_inc(exped, 1)

                def part_lo(m, i):
                    t, is_q = i % 2, i // 2
                    at = (2 if is_q else 6) + t
                    act.wait_ge(projected, m * 4 + (i + 1))
                    if due(m * 4 + (i - 1)):
                        act.wait_ge(qk_cut, m * 4 + (i - 1))
                    act.activation(qk_lo[:, i % 2], work[(i + 1) % 2][:, 0:SEQP], ACT.Identity,
                                   bias=cols[:, at:at + 1], scale=lo_rows[:, 1 - is_q:2 - is_q]).then_inc(lo_part, 1)

                def step(n, par):
                    if live(n):
                        exp(n, 0)
                    if live(n + 2):
                        act.wait_ge(x_turned, n + 3)
                        if due(n + 2):
                            act.wait_ge(v_made, n + 2)
                        act.activation(xT[:, 0:SEQ], work[0][:, 0:SEQ], ACT.Copy).then_inc(xT_set, 1)
                    if live(n):
                        exp(n, 1)
                    if live(n + 2):
                        for i in range(4):
                            part_lo(n + 2, i)
                    if live(n - 1):
                        act.wait_ge(o_turned, n)
                        if due(n - 1):
                            act.wait_ge(y_made, n - 1)
                        act.activation(oT[0:D, 0:SEQ], work[0][:].bitcast(BF16)[0:D, 0:SEQ], ACT.Copy).then_inc(oT_set, 1)
                    if live(n + 3):
                        act.wait_ge(z_ready, n + 4)
                        if due(n + 3):
                            act.wait_ge(x_turned, n + 3)
                        act.activation(xs[:, :, 0:D], zc[:], ACT.Copy).then_inc(x_hi, 1)

                each_step(act, step)

            @block.tensor
            def _(pe):
                def score(m, par, tile):
                    at, n = TILES[tile]
                    if tile == 0:
                        pe.wait_ge(k_split, m * 2 + 2)
                        pe.wait_ge(qk_cut, m * 4 + 4)
                    if due(m * 2 + tile):
                        pe.wait_ge(max_found, m * 2 + tile)
                    for t in range(A_TENSORS):
                        last = pe.matmul(scores[0:n, t, 0:A_HPT * SEQP], QF[:, par, t, at:at + n],
                                         KB[:, par, t].rearrange("p j s -> p (j s)"), start=True, stop=True)
                    last.then_inc(scored, 1)

                def score_t(m, par, tile):
                    at, n = TILES[tile]
                    if tile == 0:
                        pe.wait_ge(q_set, m + 1)
                    if due(m * 2 + tile):
                        pe.wait_ge(exped, m * 2 + tile)
                    for t in range(A_TENSORS):
                        for j in range(A_HPT):
                            last = pe.matmul(scores_t[0:n, t, j * SEQP:(j + 1) * SEQP], KB[:, par, t, j, at:at + n],
                                             QP[:, par, t], start=True, stop=True)
                    last.then_inc(scored_t, 1)

                def turn_x(m):
                    pe.wait_ge(x_cut, m + 1)
                    if due(m):
                        pe.wait_ge(qk_cut, m * 4)
                    if due(m - 3):
                        pe.wait_ge(oT_set, m - 3)
                    for tile, (at, n) in enumerate(TILES):
                        last = pe.transpose(work[0][:, at:at + n], xs[0:n, tile].bitcast(F32), ident[0:n, 0:n])
                    last.then_inc(x_turned, 1)

                def project(m, i):
                    t, wgt = i % 2, wq if i // 2 else wk
                    if i == 0:
                        pe.wait_ge(xT_set, m + 1)
                        if due(m):
                            pe.wait_ge(v_set, m)
                        if due(m - 3):
                            pe.wait_ge(y_added, m - 3)
                    if i >= 2:
                        pe.wait_ge(qk_cut, m * 4 + (i - 1))
                    for part in range(2):
                        last = pe.matmul(work[(i + 1) % 2][:, 0:SEQP], wgt[:, part, t * P:(t + 1) * P], xT[:],
                                         start=part == 0, stop=part == 1)
                    last.then_inc(projected, 1)

                def project_v(m):
                    pe.wait_ge(qk_cut, m * 4 + 3)
                    for tile, (at, n) in enumerate(TILES):
                        for part in range(2):
                            last = pe.matmul(work[1][0:n, tile * D:(tile + 1) * D], xT[:, at:at + n], wv[:, part],
                                             start=part == 0, stop=part == 1)
                    last.then_inc(v_made, 1)

                def weigh(m, par):
                    pe.wait_ge(exped, m * 2 + 2)
                    pe.wait_ge(v_set, m + 1)
                    if due(m):
                        pe.wait_ge(o_set, m)
                    for tile, (at, n) in enumerate(TILES):
                        for h in range(A_HEADS):
                            t, j = h // A_HPT, h % A_HPT
                            for keys, (_, kn) in enumerate(TILES):
                                last = pe.matmul(outs[0:n, tile, h],
                                                 PT[0:kn, keys, t, j * SEQP + at:j * SEQP + at + n],
                                                 V[0:kn, par, keys, h], start=keys == 0, stop=keys == 1)
                    last.then_inc(weighed, 1)

                def turn_max(m):
                    pe.wait_ge(max_set, m + 1)
                    for tile, (at, n) in enumerate(TILES):
                        for t in range(A_TENSORS):
                            last = pe.transpose(maxT[:, t, at:at + n], mpad[0:n, tile, t].bitcast(F32), ident[0:n, 0:n])
                    last.then_inc(max_turned, 1)

                def turn_o(m, par):
                    pe.wait_ge(o_set, m + 1)
                    if live(m + 3):
                        pe.wait_ge(qk_cut, m * 4 + 16)
                    elif due(m):
                        pe.wait_ge(oT_set, m)
                    for tile, (at, n) in enumerate(TILES):
                        last = pe.transpose(work[0][:].bitcast(BF16)[:, at:at + n], o_rows[0:n, par, tile],
                                            ident_bf[0:n, 0:n])
                    last.then_inc(o_turned, 1)

                def project_o(m):
                    pe.wait_ge(oT_set, m + 1)
                    if live(m + 3):
                        pe.wait_ge(v_set, m + 4)
                    else:
                        pe.wait_ge(y_added, m)
                    for tile, (at, n) in enumerate(TILES):
                        for part in range(2):
                            last = pe.matmul(work[1][0:n, tile * D:(tile + 1) * D], oT[:, at:at + n], wo[:, part],
                                             start=part == 0, stop=part == 1)
                    last.then_inc(y_made, 1)

                def step(n, par):
                    if live(n):
                        score_t(n, par, 0)
                    if live(n + 2):
                        turn_x(n + 2)
                    if live(n + 1):
                        score(n + 1, 1 - par, 0)
                    if live(n):
                        score_t(n, par, 1)
                    if live(n + 2):
                        project(n + 2, 0)
                        project(n + 2, 1)
                    if live(n + 1):
                        score(n + 1, 1 - par, 1)
                    if live(n):
                        weigh(n, par)
                    if live(n + 1):
                        turn_max(n + 1)
                    if live(n + 2):
                        project(n + 2, 2)
                        project(n + 2, 3)
                        project_v(n + 2)
                    if live(n - 1):
                        turn_o(n - 1, 1 - par)
                        project_o(n - 1)

                each_step(pe, step)


def experts(p, wts, ident, rows_of, out):
    nc = p.nc
    HALVES = FF // P
    WIDE = EXPERTS * D
    G = 4

    with ExitStack() as ctx:
        def sb(name, shape, dtype=F32):
            return ctx.enter_context(nc.sbuf_tensor("ex_" + name, shape, dtype))

        def sem(name):
            return p.sem("ex_" + name)

        w1 = sb("w1", [P, 2, FF], F32R)
        wd = sb("wd", [P, 2, HALVES, WIDE + EXPERTS], F32R)
        b1 = sb("b1", [P, HALVES])
        biases, ones = sb("biases", [33, WIDE + EXPERTS], F32R), sb("ones", [33, P], F32R)
        rank, power = sb("rank", [P, EXPERTS]), sb("power", [P, 2])

        stats, mean_var = sb("stats", [P, 2, 6]), sb("mean_var", [P, 2, 2])
        var_eps, rstd = sb("var_eps", [P, 2]), sb("rstd", [P, 2])
        z = sb("z", [P, 2, D])
        xs = sb("xs", [P, 2, 2 * D], F32R)
        xT = sb("xT", [P, 2, SEQP], F32R)
        H = sb("H", [P, 2, HALVES, SEQP])
        H_hi = sb("H_hi", [P, 2 * G, HALVES, SEQP], F32R)
        H_lo = sb("H_lo", [P, 2 * G, HALVES, SEQP], F32R)
        top, less = sb("top", [P, 2 * G]), sb("less", [P, 2 * G, EXPERTS])
        e_less, e_sum = sb("e_less", [P, 2 * G, EXPERTS]), sb("e_sum", [P, 2 * G])
        prob = sb("prob", [P, 2 * G])
        first, chosen = sb("first", [P, 2 * G]), sb("chosen", [P, 2 * G, EXPERTS])
        gate = sb("gate", [P, 2 * G, EXPERTS])
        weighted = sb("weighted", [P, 2, EXPERTS, D])
        summed = sb("summed", [P, 2, D])

        turned_x = p.psum(ctx, "ex_turned_x", [P, 512])
        up_rows = p.psum(ctx, "ex_up", [P, HALVES, SEQP])
        logits = p.psum(ctx, "ex_logits", [P, 2 * G, EXPERTS])
        y = [p.psum(ctx, f"ex_y{k}", [P, EXPERTS, D]) for k in range(4)]

        with ExitStack() as setup:
            def tmp(name, shape, dtype=F32):
                return setup.enter_context(nc.sbuf_tensor("ex_" + name, shape, dtype))

            w1_raw = tmp("w1_raw", [P, FF])
            wd_raw = tmp("wd_raw", [P, HALVES, WIDE + EXPERTS])
            b_raw, b_hi = tmp("b_raw", [33, WIDE + EXPERTS]), tmp("b_hi", [33, WIDE + EXPERTS], F32R)
            w_loaded, cleared, w_hi, set_up = sem("w_loaded"), sem("cleared"), sem("w_hi"), sem("set_up")

            with nc.Block() as block:
                @block.sync
                def _(sp):
                    for half in range(2):
                        sp.dma_start(w1_raw[half * D:(half + 1) * D], wts["W1"]).then_inc(w_loaded, 16)
                    for half in range(HALVES):
                        rows = slice(half * P, (half + 1) * P)
                        sp.dma_start(wd_raw[:, half, 0:WIDE].rearrange("p (e d) -> p e d", e=EXPERTS),
                                     wts["Wd"][:, rows].rearrange("e i d -> i e d")).then_inc(w_loaded, 16)
                        sp.dma_start(wd_raw[:, half, WIDE:], wts["Wg"][rows]).then_inc(w_loaded, 16)
                        with nc.allow_non_contiguous_dma(reason="bias as columns"):
                            sp.dma_start(b1[:, half:half + 1], wts["b1"][rows].rearrange("(n a) -> n a", a=1))\
                                .then_inc(w_loaded, 16)
                    sp.wait_ge(cleared, 1)
                    for r in (0, 32):
                        sp.dma_start(b_raw[r:r + 1, 0:WIDE], row(wts["bd"].rearrange("e d -> (e d)"))).then_inc(w_loaded, 16)
                        sp.dma_start(b_raw[r:r + 1, WIDE:], row(wts["bg"])).then_inc(w_loaded, 16)

                @block.gpsimd
                def _(pool):
                    pool.memset(b_raw[:], 0.0).then_inc(cleared, 1)
                    pool.memset(biases[:].bitcast(F32), 0.0).then_inc(cleared, 1)
                    pool.memset(ones[:].bitcast(F32), 1.0)
                    pool.memset(power[:], -0.5)
                    pool.memset(xT[:].bitcast(F32), 0.0)
                    pool.memset(z[:], 0.0)
                    pool.memset(mean_var[:], 0.0)
                    for e in range(EXPERTS):
                        pool.memset(rank[:, e:e + 1], float(EXPERTS - e))

                @block.vector
                def _(dve):
                    dve.memset(logits[:], 0.0)
                    dve.wait_ge(w_loaded, 12 * 16)
                    dve.tensor_copy(w1[:, 0], w1_raw[:]).then_inc(w_hi, 1)
                    dve.tensor_copy(wd[:, 0], wd_raw[:]).then_inc(w_hi, 1)
                    dve.tensor_copy(b_hi[:], b_raw[:]).then_inc(w_hi, 1)
                    dve.wait_ge(w_hi, 3)
                    dve.tensor_tensor(w1[:, 1], w1_raw[:], w1[:, 0].bitcast(F32), ALU.subtract)
                    dve.tensor_tensor(wd[:, 1], wd_raw[:], wd[:, 0].bitcast(F32), ALU.subtract)
                    dve.wait_ge(cleared, 2)
                    dve.tensor_copy(biases[0:1], b_hi[0:1].bitcast(F32))
                    dve.tensor_tensor(biases[32:33], b_raw[32:33], b_hi[32:33].bitcast(F32), ALU.subtract)

        aggregated, var_ready, rstd_ready, z_ready, x_hi, x_cut, x_turned, xT_set = (
            sem("aggregated"), sem("var_ready"), sem("rstd_ready"), sem("z_ready"), sem("x_hi"),
            sem("x_cut"), sem("x_turned"), sem("xT_set"))
        up_done, gelu_done, h_hi, h_cut = sem("up_done"), sem("gelu_done"), sem("h_hi"), sem("h_cut")
        gated, gate_step, gate_exp, gate_sum, gate_set = (
            sem("gated"), sem("gate_step"), sem("gate_exp"), sem("gate_sum"), sem("gate_set"))
        y_made, y_weighted, y_summed, added, stored = (
            sem("y_made"), sem("y_weighted"), sem("y_summed"), sem("added"), sem("stored"))
        GATE_STEPS = 6

        def each_step(eng, step):
            for n in range(-6, 8):
                step(n, n % 8)
            with eng.Fori(1, B // 8 - 1) as i:
                for k in range(8):
                    step(i * 8 + k, k)
            for n in range(B - 8, B):
                step(n, n % 8)

        with nc.Block() as block:
            @block.sync
            def _(sp):
                def step(n, k):
                    if k % 2 == 1 and live(n):
                        sp.wait_ge(added, n * 2 + 2)
                        for tile, (at, rows) in enumerate(TILES):
                            sp.dma_start(out[bass.ds(n - 1, 2), at:at + rows].rearrange("b s d -> s b d"),
                                         rows_of(n - 1, tile, 2)).then_inc(stored, 16)

                each_step(sp, step)
                sp.wait_ge(stored, B * 16)

            @block.vector
            def _(dve):
                def choose(q):
                    wide = [P, 2 * G, EXPERTS]
                    base = q * GATE_STEPS
                    dve.wait_ge(gated, q * G + G)
                    dve.tensor_reduce(top[:], logits[:], AX.X, ALU.max).then_inc(gate_step, 1)
                    dve.wait_ge(gate_step, base + 1)
                    dve.tensor_tensor(less[:], logits[:], top[:].unsqueeze(2).broadcast_to(wide), ALU.subtract)\
                        .then_inc(gate_sum, 1)
                    dve.wait_ge(gate_sum, q + 1)
                    dve.scalar_tensor_tensor(out=chosen[:], in0=less[:], scalar=0.0,
                                             in1=rank[:].unsqueeze(1).broadcast_to(wide), op0=ALU.is_ge, op1=ALU.mult)\
                        .then_inc(gate_step, 1)
                    dve.wait_ge(gate_step, base + 2)
                    dve.tensor_reduce(first[:], chosen[:], AX.X, ALU.max).then_inc(gate_step, 1)
                    dve.wait_ge(gate_exp, q + 1)
                    dve.tensor_reduce(e_sum[:], e_less[:], AX.X, ALU.add).then_inc(gate_step, 1)
                    dve.wait_ge(gate_step, base + 4)
                    dve.reciprocal(prob[:], e_sum[:]).then_inc(gate_step, 1)
                    dve.tensor_tensor(chosen[:], chosen[:], first[:].unsqueeze(2).broadcast_to(wide), ALU.is_equal)\
                        .then_inc(gate_step, 1)
                    dve.wait_ge(gate_step, base + 6)
                    dve.tensor_tensor(gate[:], chosen[:], prob[:].unsqueeze(2).broadcast_to(wide), ALU.mult)\
                        .then_inc(gate_set, 1)
                    dve.wait_ge(gate_set, q + 1)

                def combine(m, b, par, tile):
                    n = TILES[tile][1]
                    dve.wait_ge(y_made, m * 2 + (tile + 1))
                    dve.tensor_tensor(weighted[0:n, tile], y[2 * par + tile][0:n],
                                      gate[0:n, 2 * b + tile].unsqueeze(2).broadcast_to([n, EXPERTS, D]), ALU.mult)\
                        .then_inc(y_weighted, 1)
                    dve.wait_ge(y_weighted, m * 2 + (tile + 1))
                    dve.tensor_reduce(summed[0:n, tile], weighted[0:n, tile].rearrange("p e d -> p d e"), AX.X, ALU.add)\
                        .then_inc(y_summed, 1)
                    dve.wait_ge(y_summed, m * 2 + (tile + 1))
                    dve.tensor_tensor(rows_of(m, tile), rows_of(m, tile), summed[0:n, tile], ALU.add).then_inc(added, 1)

                def step(n, k):
                    b, par = k % G, k % 2
                    if live(n + 6):
                        set_stats(dve, rows_of, mean_var, stats, var_eps, aggregated, var_ready, n + 6)
                    if live(n):
                        combine(n, b, par, 0)
                    if live(n + 6):
                        m = n + 6
                        dve.wait_ge(rstd_ready, m + 1)
                        if due(m):
                            dve.wait_ge(x_cut, m)
                        for tile, (_, rows) in enumerate(TILES):
                            last = dve.tensor_scalar(z[0:rows, tile], rows_of(m, tile), mean_var[0:rows, tile, 0:1],
                                                     rstd[0:rows, tile:tile + 1], ALU.subtract, ALU.mult)
                        last.then_inc(z_ready, 1)
                    if live(n):
                        combine(n, b, par, 1)
                    if b == G - 1 and live(n + 4):
                        choose((n + 4 - b) // G if isinstance(n, int) else q_of(n, k))

                def q_of(n, k):
                    return QREG[0] * 2 + (k // G + 1)

                QREG = [None]
                for n in range(-6, 8):
                    step(n, n % 8)
                with dve.Fori(1, B // 8 - 1) as i:
                    QREG[0] = i
                    for k in range(8):
                        step(i * 8 + k, k)
                for n in range(B - 8, B):
                    step(n, n % 8)

            @block.gpsimd
            def _(pool):
                def step(n, k):
                    if live(n + 6):
                        pool.wait_ge(var_ready, n + 7)
                        pool.tensor_tensor(rstd[:], var_eps[:], power[:], ALU.pow).then_inc(rstd_ready, 1)
                    if live(n + 4):
                        m, slot = n + 4, (k + 4) % 8
                        pool.wait_ge(h_hi, m + 1)
                        pool.tensor_tensor(H_lo[:, slot], H[:, k % 2], H_hi[:, slot].bitcast(F32), ALU.subtract)\
                            .then_inc(h_cut, 1)
                    if live(n + 6):
                        pool.wait_ge(x_hi, n + 7)
                        pool.tensor_tensor(xs[:, :, D:], z[:], xs[:, :, 0:D].bitcast(F32), ALU.subtract)\
                            .then_inc(x_cut, 1)

                each_step(pool, step)

            @block.scalar
            def _(act):
                def step(n, k, q):
                    if live(n + 4):
                        m, slot = n + 4, (k + 4) % 8
                        act.wait_ge(up_done, m + 1)
                        if due(m - 1):
                            act.wait_ge(h_cut, m - 1)
                        for half in range(HALVES):
                            last = act.activation(H[:, k % 2, half], up_rows[:, half], ACT.Gelu, bias=b1[:, half:half + 1])
                        last.then_inc(gelu_done, 1)
                        act.wait_ge(gelu_done, m + 1)
                        if due(m * 2 - 14):
                            act.wait_ge(y_made, m * 2 - 14)
                        act.activation(H_hi[:, slot], H[:, k % 2], ACT.Copy).then_inc(h_hi, 1)
                    if live(n + 5):
                        m = n + 5
                        act.wait_ge(x_turned, m + 1)
                        if due(m - 1):
                            act.wait_ge(up_done, m - 1)
                        act.activation(xT[:, (k + 5) % 2, 0:SEQ], turned_x[:, 0:SEQ], ACT.Copy).then_inc(xT_set, 1)
                    if live(n + 6):
                        m = n + 6
                        act.wait_ge(z_ready, m + 1)
                        if due(m):
                            act.wait_ge(x_turned, m)
                        act.activation(xs[:, :, 0:D], z[:], ACT.Copy).then_inc(x_hi, 1)
                    if k % G == G - 1 and live(n + 4):
                        act.wait_ge(gate_sum, q + 1)
                        act.activation(e_less[:], less[:], ACT.Exp).then_inc(gate_exp, 1)

                for n in range(-6, 8):
                    step(n, n % 8, (n + 4) // G)
                with act.Fori(1, B // 8 - 1) as i:
                    for k in range(8):
                        step(i * 8 + k, k, i * 2 + (k // G + 1))
                for n in range(B - 8, B):
                    step(n, n % 8, (n + 4) // G)

            @block.tensor
            def _(pe):
                def products(acc, slot, at, n, a, b):
                    pe.matmul(acc, ones[:, 0:n], biases[:, a:b], start=True, stop=False)
                    for half in range(HALVES):
                        for h, part in ((H_hi, 0), (H_hi, 1), (H_lo, 0)):
                            closes = half == HALVES - 1 and h is H_lo
                            last = pe.matmul(acc, h[:, slot, half, at:at + n], wd[:, part, half, a:b],
                                             start=False, stop=closes)
                    return last

                def run_experts(m, slot, par, tile):
                    at, n = TILES[tile]
                    if due(m * 2 - 3 + tile):
                        pe.wait_ge(y_weighted, m * 2 - 3 + tile)
                    acc = y[2 * par + tile][0:n].rearrange("p e d -> p (e d)")
                    products(acc, slot, at, n, 0, WIDE).then_inc(y_made, 1)

                def step(n, k, q):
                    if live(n + 4):
                        m = n + 4
                        pe.wait_ge(xT_set, m + 1)
                        if due(m):
                            pe.wait_ge(gelu_done, m)
                        for half in range(HALVES):
                            for part in range(2):
                                last = pe.matmul(up_rows[:, half], w1[:, part, half * P:(half + 1) * P], xT[:, k % 2],
                                                 start=part == 0, stop=part == 1)
                        last.then_inc(up_done, 1)
                    if live(n):
                        run_experts(n, k, k % 2, 0)
                    if live(n + 5):
                        m = n + 5
                        pe.wait_ge(x_cut, m + 1)
                        if due(m):
                            pe.wait_ge(xT_set, m)
                        for tile, (at, rows) in enumerate(TILES):
                            last = pe.transpose(turned_x[:, at:at + rows], xs[0:rows, tile].bitcast(F32),
                                                ident[0:rows, 0:rows])
                        last.then_inc(x_turned, 1)
                    if live(n):
                        run_experts(n, k, k % 2, 1)
                    if live(n + 4):
                        m, slot, b = n + 4, (k + 4) % 8, k % G
                        pe.wait_ge(h_cut, m + 1)
                        if b == 0 and due(q):
                            pe.wait_ge(gate_sum, q)
                        for tile, (at, rows) in enumerate(TILES):
                            last = products(logits[0:rows, 2 * b + tile], slot, at, rows, WIDE, WIDE + EXPERTS)
                        last.then_inc(gated, 1)

                for n in range(-6, 8):
                    step(n, n % 8, (n + 4) // G)
                with pe.Fori(1, B // 8 - 1) as i:
                    for k in range(8):
                        step(i * 8 + k, k, i * 2 + (k // G + 1))
                for n in range(B - 8, B):
                    step(n, n % 8, (n + 4) // G)



IMAGE_WEIGHTS = ("ln0_g", "ln0_b", "ln1_g", "ln1_b", "conv1_w", "conv1_b", "conv2_w", "conv2_b", "conv3_w",
                 "conv3_b", "out_w", "out_b")
TEXT_WEIGHTS = ("emb", "Wq", "bq", "Wv", "bv", "Wo", "bo", "W1", "b1", "W2", "b2", "ln1_g", "ln1_b", "ln2_g",
                "ln2_b", "fin_g", "fin_b")
ATTENTION_WEIGHTS = ("Wq", "bq", "Wk", "bk", "Wv", "bv", "Wo", "bo")
EXPERT_WEIGHTS = ("W1", "b1", "Wg", "bg", "Wd", "bd")


def early_fusion_embed(nc, x, x_txt, pos, weights, out):
    def of(prefix, names):
        return {name: weights[prefix + name] for name in names}

    with ExitStack() as ctx:
        p = Program(nc, ctx, B)
        ident = p.sb("ident", [P, P])
        h_img, h_txt = p.sb("h_img", [T, B, LAT]), p.sb("h_txt", [S_TXT, B, D])

        def rows_of(n, tile, count=None):
            h = h_txt if tile else h_img
            v = h[:, bass.ds(n, count or 1)]
            return v if count else v.rearrange("p a d -> p (a d)")

        constants(p, ident)
        image_branch(p, x, of("L0_tok_", IMAGE_WEIGHTS), ident, h_img)
        text_branch(p, x_txt, pos, of("L0_txt_", TEXT_WEIGHTS), ident, h_txt)
        fusion_attention(p, of("L0_attn_", ATTENTION_WEIGHTS), ident, rows_of)
        experts(p, of("L0_ffn_", EXPERT_WEIGHTS), ident, rows_of, out)


def positional_table():
    at = np.arange(S_TXT, dtype=np.float32)[:, None]
    freq = np.exp(np.arange(0, D, 2, dtype=np.float32) * np.float32(-np.log(10000.0) / D))
    table = np.zeros((S_TXT, D), np.float32)
    table[:, 0::2], table[:, 1::2] = np.sin(at * freq), np.cos(at * freq)
    return table


def kernel(**inputs):
    import concourse.bacc as _bacc
    from concourse import mybir as _mybir
    from concourse.bass_utils import run_bass_kernel_spmd as _run

    nc = _bacc.Bacc("TRN2", target_bir_lowering=False, num_devices=1)
    arrays = {name: np.ascontiguousarray(a) for name, a in inputs.items()}
    arrays["pos"] = positional_table()
    dram = {name: nc.dram_tensor(name, a.shape, _mybir.dt.from_np(a.dtype), kind="ExternalInput").ap()
            for name, a in arrays.items()}
    out = nc.dram_tensor("out", (B, T + S_TXT, D), F32, kind="ExternalOutput").ap()
    weights = {name: ap for name, ap in dram.items() if name.startswith("L0_")}
    early_fusion_embed(nc, dram["x"], dram["x_txt"], dram["pos"], weights, out)
    r = _run(nc, [arrays], core_ids=[0])
    return r.results[0]["out"]
```

```python
from contextlib import ExitStack

import numpy as np

import concourse.bass as bass
from concourse import mybir

F32 = mybir.dt.float32
F32R = mybir.dt.float32r
BF16 = mybir.dt.bfloat16
I32 = mybir.dt.int32
ALU = mybir.AluOpType
ACT = mybir.ActivationFunctionType
AX = mybir.AxisListType

P = 128
EPS = 1e-5
B = 64
T, J, LAT = 128, 64, 64
QUAD = 4
JP = J + 4


class Count:

    def __init__(self, base):
        self.base, self.k = base, 0

    def up(self, by=1):
        self.k += by
        return self.base + self.k


class Program:

    def __init__(self, nc, ctx, samples):
        self.nc, self.ctx, self.samples = nc, ctx, samples
        self.quads = samples // QUAD

    def sb(self, name, shape, dtype=F32):
        return self.ctx.enter_context(self.nc.sbuf_tensor(name, shape, dtype))

    def psum(self, ctx, name, shape, dtype=F32):
        return ctx.enter_context(self.nc.psum_tensor(name, shape, dtype))

    def sem(self, name):
        return self.ctx.enter_context(self.nc.semaphore(name))


def row(ap):
    return ap.rearrange("(a n) -> a n", a=1)


def on_all_rows(ap, rows=P):
    return row(ap).broadcast_to([rows, ap.shape[0]])



def image_branch(p, x, wts, ident, h_img, later_loads):
    nc = p.nc
    TAPS = (15, 10, 10)
    KD = (3, 2, 2)
    COLS = (3, 3, 2, 1)
    OUT_HALVES = (1, 1, 2)

    with ExitStack() as ctx:
        def sb(name, shape, dtype=F32):
            return ctx.enter_context(nc.sbuf_tensor(name, shape, dtype))

        def sem(name):
            return p.sem("im_" + name)

        w = [sb(f"im_w{c}", [P, TAPS[c] * OUT_HALVES[c], 2, P], F32R) for c in range(3)]
        bias = [sb(f"im_bias{c}", [P, OUT_HALVES[c]]) for c in range(3)]
        g0_jd, b0_jd = sb("im_g0_jd", [P, 3 * J]), sb("im_b0_jd", [P, 3 * J])
        g0, b0 = sb("im_g0", [P, 3 * J]), sb("im_b0", [P, 3 * J])
        g1_jd, b1_jd = sb("im_g1_jd", [P, 2 * J]), sb("im_b1_jd", [P, 2 * J])
        g1, b1 = sb("im_g1", [P, 2 * J]), sb("im_b1", [P, 2 * J])
        g1_col, b1_col = sb("im_g1_col", [P, 1]), sb("im_b1_col", [P, 1])
        w_out, bias_out = sb("im_w_out", [P, LAT]), sb("im_bias_out", [P, LAT])

        loaded = [sem(f"w_loaded{c}") for c in range(3)]
        small_loaded, zeroed = sem("small_loaded"), sem("zeroed")
        turned, hi_cut, lo_cut = sem("w_turned"), sem("w_hi_cut"), sem("w_lo_cut")

        a_hi = [sb(f"im_a_hi{c}", [P, (2 if c == 0 else 1), QUAD, COLS[c], JP], F32R) for c in range(3)]
        a_lo = [sb(f"im_a_lo{c}", [P, (2 if c == 0 else 1), QUAD, COLS[c], JP], F32R) for c in range(3)]

        with ExitStack() as setup:
            raw = [setup.enter_context(nc.sbuf_tensor(f"im_raw{c}", [P, OUT_HALVES[c], P * TAPS[c]], F32))
                   for c in range(3)]
            turn = [p.psum(setup, f"im_turn{k}", [P, 4, P]) for k in range(4)]
            jobs = [(c, t, h) for c in range(3) for h in range(OUT_HALVES[c]) for t in range(TAPS[c])]
            packs = [[q for q in jobs if q[0] == c] for c in range(3)]
            packs = [q[k:k + 4] for q in packs for k in range(0, len(q), 4)]

            with nc.Block() as block:
                @block.sync
                def _(sp):
                    for c in range(3):
                        sp.dma_start(raw[c][:], wts[f"conv{c + 1}_w"].rearrange("(h o) i a b -> o h (i a b)", o=P))\
                            .then_inc(loaded[c], 16)
                    with nc.allow_non_contiguous_dma(reason="biases and gains as columns"):
                        for c in range(3):
                            sp.dma_start(bias[c][:], wts[f"conv{c + 1}_b"].rearrange("(h o) -> o h", o=P))\
                                .then_inc(small_loaded, 16)
                        sp.dma_start(g1_col[:], wts["ln1_g"].rearrange("(n a) -> n a", a=1)).then_inc(small_loaded, 16)
                        sp.dma_start(b1_col[:], wts["ln1_b"].rearrange("(n a) -> n a", a=1)).then_inc(small_loaded, 16)
                    sp.dma_start(g0_jd[:], on_all_rows(wts["ln0_g"])).then_inc(small_loaded, 16)
                    sp.dma_start(b0_jd[:], on_all_rows(wts["ln0_b"])).then_inc(small_loaded, 16)
                    sp.dma_start(g1_jd[:], on_all_rows(wts["ln1_g"])).then_inc(small_loaded, 16)
                    sp.dma_start(b1_jd[:], on_all_rows(wts["ln1_b"])).then_inc(small_loaded, 16)
                    sp.dma_start(w_out[:], wts["out_w"]).then_inc(small_loaded, 16)
                    sp.dma_start(bias_out[:], on_all_rows(wts["out_b"])).then_inc(small_loaded, 16)

                @block.gpsimd
                def _(pool):
                    for c in range(3):
                        pool.memset(a_hi[c][:].bitcast(F32), 0.0).then_inc(zeroed, 1)
                        pool.memset(a_lo[c][:].bitcast(F32), 0.0).then_inc(zeroed, 1)

                @block.tensor
                def _(pe):
                    for n, pack in enumerate(packs):
                        c = pack[0][0]
                        pe.wait_ge(loaded[c], 16)
                        if n >= 4:
                            pe.wait_ge(lo_cut, n - 3)
                        for k, (c, t, h) in enumerate(pack):
                            src = raw[c][:, h].rearrange("o (i t) -> o t i", t=TAPS[c])[:, t]
                            last = pe.transpose(turn[n % 4][:, k], src, ident[:])
                        last.then_inc(turned, 1)

                def slots(n):
                    c, t, h = packs[n][0]
                    k = h * TAPS[c] + t
                    return w[c], k, len(packs[n])

                @block.scalar
                def _(act):
                    for n in range(len(packs)):
                        dst, k, m = slots(n)
                        act.wait_ge(turned, n + 1)
                        act.activation(dst[:, k:k + m, 0], turn[n % 4][:, 0:m], ACT.Copy).then_inc(hi_cut, 1)

                @block.vector
                def _(dve):
                    for n in range(len(packs)):
                        dst, k, m = slots(n)
                        dve.wait_ge(hi_cut, n + 1)
                        dve.tensor_tensor(dst[:, k:k + m, 1], turn[n % 4][:, 0:m], dst[:, k:k + m, 0].bitcast(F32),
                                          ALU.subtract).then_inc(lo_cut, 1)
                    dve.wait_ge(small_loaded, 11 * 16)
                    for dst, src in ((g0, g0_jd), (b0, b0_jd)):
                        dve.tensor_copy(dst[:].rearrange("p (d j) -> p d j", d=3),
                                        src[:].rearrange("p (j d) -> p d j", d=3))
                    for dst, src in ((g1, g1_jd), (b1, b1_jd)):
                        dve.tensor_copy(dst[:].rearrange("p (d j) -> p d j", d=2),
                                        src[:].rearrange("p (j d) -> p d j", d=2))

        xin = sb("im_x", [P, 2, QUAD, 3 * J])
        act_out = [sb("im_h1", [P, QUAD, 3 * J]), sb("im_h2", [P, QUAD, 2 * J]), sb("im_h3", [P, QUAD, 2 * J])]
        scaled, normed = sb("im_scaled", [P, QUAD, 3 * J]), sb("im_normed", [P, QUAD, 3 * J])
        stats, mean_var = sb("im_stats", [P, QUAD, 6]), sb("im_mean_var", [P, QUAD, 2])
        var_eps, rstd = sb("im_var_eps", [P, QUAD]), sb("im_rstd", [P, QUAD])
        power = sb("im_power", [P, QUAD])
        res = sb("im_res", [P, QUAD, P])
        res_t = sb("im_res_t", [P, QUAD, P])
        c1 = [p.psum(ctx, f"im_c1{k}", [P, 2, 3, J]) for k in range(2)]
        c2 = p.psum(ctx, "im_c2", [P, QUAD, 2, J])
        c3 = p.psum(ctx, "im_c3", [P, 2, QUAD, J])
        turned_res = p.psum(ctx, "im_turned_res", [P, QUAD, P])
        out_rows = p.psum(ctx, "im_out_rows", [P, QUAD, LAT])

        x_loaded = [sem("x_loaded0"), sem("x_loaded1")]
        power_set = sem("power_set")
        dve_step = sem("dve_step")
        var_ready, rstd_ready = sem("var_ready"), sem("rstd_ready")
        normed_ready, hi_ready, lo_ready = sem("normed_ready"), sem("hi_ready"), sem("lo_ready")
        conv_done = [sem(f"conv{c}_done") for c in range(3)]
        relu_done = [sem(f"relu{c}_done") for c in range(3)]
        res_ready, res_turned, res_scaled, out_done, rows_stored = (
            sem("res_ready"), sem("res_turned"), sem("res_scaled"), sem("out_done"), sem("rows_stored"))

        U = p.quads
        assert U % 2 == 0 and U >= 4

        def each_quad(eng, before, step):
            before()
            step(0, 0, True, False)
            step(1, 1, False, False)
            if U > 4:
                with eng.Fori(1, U // 2 - 1) as i:
                    step(i * 2, 0, False, False)
                    step(i * 2 + 1, 1, False, False)
            step(U - 2, 0, False, False)
            step(U - 1, 1, False, True)

        STATS = QUAD
        FULL = STATS + QUAD
        TURN = 3 * FULL + STATS

        def cuts_before(n):
            return n * 3 + 1

        def norms_before(n, first):
            return 1 if first else n * 4

        def steps_before(n, first):
            return FULL if first else n * TURN + (FULL - STATS)

        with nc.Block() as block:
            @block.sync
            def _(sp):
                def load(n, par):
                    sp.dma_start(xin[:, par], x[bass.ds(n * QUAD, QUAD)].rearrange("b t j d -> t b (j d)"))\
                        .then_inc(x_loaded[par], 16)

                def step(n, par, first, last):
                    if not last:
                        if not first:
                            sp.wait_ge(normed_ready, n * 3 - 2)
                        load(n + 1, 1 - par)
                    if first:
                        for inputs in later_loads:
                            inputs.load(sp)

                each_quad(sp, lambda: load(0, 0), step)

            @block.vector
            def _(dve):
                def statistics(src, c):
                    for b in range(QUAD):
                        dve.bn_stats(stats[:, b], src[:, b])
                    dve.drain()
                    for b in range(QUAD):
                        dve.bn_aggr(mean_var[:, b], stats[:, b]).then_inc(dve_step, 1)
                    dve.wait_ge(dve_step, c.up(QUAD))
                    dve.tensor_scalar(var_eps[:], mean_var[:, :, 1], EPS, None, ALU.add).then_inc(var_ready, 1)

                def normalise(src, size, gain, shift, c, norms, cuts, first=False, by_column=False):
                    statistics(src, c)
                    for b in range(QUAD):
                        img, to, by = src[:, b], scaled[:, b, 0:size], gain[:]
                        if by_column:
                            img = img.rearrange("p (j d) -> p d j", d=3)
                            to, by = (v.rearrange("p (d j) -> p d j", d=3) for v in (to, by))
                        dve.scalar_tensor_tensor(out=to, in0=img, scalar=mean_var[:, b, 0:1], in1=by,
                                                 op0=ALU.subtract, op1=ALU.mult).then_inc(dve_step, 1)
                    dve.wait_ge(dve_step, c.up(QUAD))
                    dve.wait_ge(rstd_ready, norms.up())
                    if not first:
                        dve.wait_ge(lo_ready, cuts.up() - 1)
                    for b in range(QUAD):
                        last = dve.scalar_tensor_tensor(out=normed[:, b, 0:size], in0=scaled[:, b, 0:size],
                                                        scalar=rstd[:, b:b + 1], in1=shift[:],
                                                        op0=ALU.mult, op1=ALU.add)
                    last.then_inc(normed_ready, 1)

                def last_norm(c, norms):
                    statistics(act_out[2], c)
                    dve.wait_ge(rstd_ready, norms.up())
                    for b in range(QUAD):
                        last = dve.tensor_scalar(res[:, b], act_out[2][:, b], mean_var[:, b, 0:1], rstd[:, b:b + 1],
                                                 ALU.subtract, ALU.mult)
                    last.then_inc(res_ready, 1)

                def store_rows(n):
                    dve.wait_ge(out_done, n + 1)
                    dve.tensor_tensor(h_img[:, bass.ds(n * QUAD, QUAD)], out_rows[:],
                                      bias_out[:].unsqueeze(1).broadcast_to([P, QUAD, LAT]), ALU.add)\
                        .then_inc(rows_stored, 1)

                def first_norm(n, par, c, norms, cuts, first=False):
                    dve.wait_ge(x_loaded[par], (n - par) * 8 + 16)
                    normalise(xin[:, par], 3 * J, g0, b0, c, norms, cuts, first, by_column=True)

                def before():
                    dve.memset(power[:], -0.5).then_inc(power_set, 1)
                    c = Count(0)
                    first_norm(0, 0, c, Count(0), Count(0), True)
                    assert c.k == FULL

                def step(n, par, first, last):
                    c, norms, cuts = Count(steps_before(n, first)), Count(norms_before(n, first)), Count(cuts_before(n))
                    if not last:
                        first_norm(n + 1, 1 - par, c, norms, cuts)
                    dve.wait_ge(relu_done[0], n * 2 + 2)
                    normalise(act_out[0], 3 * J, g0, b0, c, norms, cuts)
                    if not first:
                        dve.wait_ge(relu_done[2], n)
                        last_norm(c, norms)
                    dve.wait_ge(relu_done[1], n + 1)
                    normalise(act_out[1], 2 * J, g1, b1, c, norms, cuts)
                    if not first:
                        store_rows(n - 1)
                    if last:
                        dve.wait_ge(relu_done[2], n + 1)
                        last_norm(c, norms)
                        store_rows(n)
                    else:
                        assert c.k == (TURN - STATS if first else TURN)

                each_quad(dve, before, step)

            @block.gpsimd
            def _(pool):
                def rstd_of(norms):
                    pool.wait_ge(var_ready, norms.up())
                    pool.tensor_tensor(rstd[:], var_eps[:], power[:], ALU.pow).then_inc(rstd_ready, 1)

                def lo_of(c, par, cuts):
                    cols = COLS[c]
                    pool.wait_ge(hi_ready, cuts.up())
                    for b in range(QUAD):
                        last = pool.tensor_tensor(
                            a_lo[c][:, par, b, :, 2:2 + J],
                            normed[:, b, 0:cols * J].rearrange("p (d j) -> p d j", d=cols),
                            a_hi[c][:, par, b, :, 2:2 + J].bitcast(F32), ALU.subtract)
                    last.then_inc(lo_ready, 1)

                def before():
                    pool.wait_ge(power_set, 1)
                    rstd_of(Count(0))
                    lo_of(0, 0, Count(0))

                def step(n, par, first, last):
                    norms, cuts = Count(norms_before(n, first)), Count(cuts_before(n))
                    if not last:
                        rstd_of(norms)
                        lo_of(0, 1 - par, cuts)
                    rstd_of(norms)
                    lo_of(1, 0, cuts)
                    if not first:
                        rstd_of(norms)
                    rstd_of(norms)
                    lo_of(2, 0, cuts)
                    if last:
                        rstd_of(norms)

                each_quad(pool, before, step)

            @block.scalar
            def _(act):
                def hi_of(c, par, cuts):
                    cols = COLS[c]
                    act.wait_ge(normed_ready, cuts.up())
                    for b in range(QUAD):
                        last = act.activation(a_hi[c][:, par, b, :, 2:2 + J],
                                              normed[:, b, 0:cols * J].rearrange("p (d j) -> p d j", d=cols), ACT.Copy)
                    last.then_inc(hi_ready, 1)

                def relu(c, n):
                    if c == 0:
                        for k in range(2):
                            act.wait_ge(conv_done[0], n * 2 + k + 1)
                            act.activation(act_out[0][:, 2 * k:2 * k + 2], c1[k][:].rearrange("p b d j -> p b (d j)"),
                                           ACT.Relu, bias=bias[0][:, 0:1]).then_inc(relu_done[0], 1)
                    elif c == 1:
                        act.wait_ge(conv_done[1], n + 1)
                        act.activation(act_out[1][:], c2[:].rearrange("p b d j -> p b (d j)"), ACT.Relu,
                                       bias=bias[1][:, 0:1]).then_inc(relu_done[1], 1)
                    else:
                        act.wait_ge(conv_done[2], n + 1)
                        for half in range(2):
                            last = act.activation(act_out[2][:, :, half * J:half * J + J], c3[:, half], ACT.Relu,
                                                  bias=bias[2][:, half:half + 1])
                        last.then_inc(relu_done[2], 1)

                def scale_res(n):
                    act.wait_ge(res_turned, n + 1)
                    act.activation(res_t[:], turned_res[:], ACT.Identity, bias=b1_col[:], scale=g1_col[:])\
                        .then_inc(res_scaled, 1)

                def step(n, par, first, last):
                    cuts = Count(cuts_before(n))
                    if not last:
                        hi_of(0, 1 - par, cuts)
                    relu(0, n)
                    hi_of(1, 0, cuts)
                    if not first:
                        relu(2, n - 1)
                    relu(1, n)
                    if not first:
                        scale_res(n - 1)
                    hi_of(2, 0, cuts)
                    if last:
                        relu(2, n)
                        scale_res(n)

                each_quad(act, lambda: hi_of(0, 0, Count(0)), step)

            @block.tensor
            def _(pe):
                def conv(c, par, cuts, n):
                    pe.wait_ge(lo_ready, cuts)
                    hi, lo = a_hi[c][:, par], a_lo[c][:, par]
                    halves = ((0, 2), (2, 4)) if c == 0 else ((0, 4),)
                    for k, (b0_, b1_) in enumerate(halves):
                        for half in range(OUT_HALVES[c]):
                            acc = c1[k][:] if c == 0 else c2[:] if c == 1 else c3[:, half].unsqueeze(2)
                            taps = [(kj, kd) for kd in ((1, 0, 2) if c == 0 else range(2)) for kj in range(5)]
                            for kj, kd in taps:
                                shift = kd - 1 if c == 0 else kd
                                d0 = max(0, -shift) if c == 0 else 0
                                d1 = min(3, 3 - shift) if c == 0 else COLS[c + 1]
                                slot = half * TAPS[c] + kj * KD[c] + kd
                                for part, img in ((0, hi), (1, hi), (0, lo)):
                                    opens = (kj, kd) == taps[0] and part == 0 and img is hi
                                    closes = (kj, kd) == taps[-1] and img is lo
                                    last = pe.matmul(acc[:, :, d0:d1], w[c][:, slot, part],
                                                     img[:, b0_:b1_, d0 + shift:d1 + shift, kj:kj + J],
                                                     start=opens, stop=closes)
                        if c == 0:
                            last.then_inc(conv_done[0], 1)
                    if c:
                        last.then_inc(conv_done[c], 1)

                def project(n):
                    pe.wait_ge(res_ready, n + 1)
                    for b in range(QUAD):
                        last = pe.transpose(turned_res[:, b], res[:, b], ident[:])
                    last.then_inc(res_turned, 1)
                    pe.wait_ge(res_scaled, n + 1)
                    for b in range(QUAD):
                        last = pe.matmul(out_rows[:, b], res_t[:, b], w_out[:], start=True, stop=True)
                    last.then_inc(out_done, 1)

                def step(n, par, first, last):
                    cuts = cuts_before(n)
                    conv(0, par, 1 if first else n * 3 - 1, n)
                    if not first:
                        conv(2, 0, cuts, n - 1)
                    conv(1, 0, cuts + (1 if last else 2), n)
                    if not first:
                        project(n - 1)
                    if last:
                        conv(2, 0, cuts + 2, n)
                        project(n)

                each_quad(pe, lambda: None, step)


def constants(p, ident, clear):
    nc = p.nc
    cleared, made = p.sem("ident_cleared"), p.sem("ident_made")
    with nc.Block() as block:
        @block.gpsimd
        def _(pool):
            for t in clear:
                pool.memset(t[:], 0.0)
            pool.memset(ident[:], 0.0).then_inc(cleared, 1)
            pool.wait_ge(cleared, 1)
            pool.affine_select(out=ident[:], in_=ident[:], compare_op=ALU.not_equal, fill=1.0, base=0,
                               pattern=[[-1, P]], channel_multiplier=1).then_inc(made, 1)
            pool.wait_ge(made, 1)



S_TXT = 77
SP_TXT = S_TXT + 1
D = 64
LAYERS, HEADS, FF, VOCAB = 4, 8, 256, 100
DH = D // HEADS

SEC = {}
_at = 0
for _name, _width in (("q", 2 * 2 * P), ("k", 2 * 2 * P), ("v", 2 * D), ("o", 2 * D), ("ff1", 2 * FF)):
    SEC[_name] = (_at, _at + _width)
    _at += _width
W_COLS = _at
ROWS_OF = ("bv", "bo", "ln1_g", "ln1_b", "b2", "ln2_g", "ln2_b")
GROUP = 32
HPT = P // GROUP
TENSORS = HEADS // HPT


def place_heads(dve, dst, src, head_dim, group, done):
    for copy in range(3):
        dve.tensor_copy(
            dst.rearrange("p l (j r) -> p l j r", r=group)[:, :, :, copy * head_dim:(copy + 1) * head_dim],
            src.rearrange("p l (j c) -> p l j c", c=head_dim)).then_inc(done, 1)


class TextInputs:

    def __init__(self, p, tokens, pos, wts):
        self.nc, self.wts, self.dram_tokens, self.dram_pos = p.nc, wts, tokens, pos

        def sb(name, shape, dtype=F32):
            return p.sb("tx_" + name, shape, dtype)

        self.raw = {m: sb("raw_" + m, [P, LAYERS, FF if m == "W1" else D]) for m in ("Wq", "Wv", "Wo", "W1")}
        self.w2_all = sb("w2_all", [P, LAYERS, 2, D])
        self.rows_all = sb("rows_all", [S_TXT, LAYERS, len(ROWS_OF), D])
        self.cols_all = sb("cols_all", [P, LAYERS, 10])
        self.fin_g, self.fin_b = sb("fin_g", [S_TXT, D]), sb("fin_b", [S_TXT, D])
        self.toks = sb("toks", [VOCAB, p.samples * S_TXT], I32)
        self.emb, self.pos = sb("emb", [VOCAB, D]), sb("pos", [S_TXT, D])
        self.w_loaded, self.small_loaded, self.tok_loaded = p.sem("tx_w_loaded"), p.sem("tx_small_loaded"), p.sem("tx_tok_loaded")
        self.N_W = 2 * len(self.raw) + 1
        self.N_SMALL = len(ROWS_OF) + 2 + 2 + 2 * HEADS * 3
        self.N_TOK = 3

    def load(self, q):
        nc, wts = self.nc, self.wts
        q.dma_start(self.toks[:], self.dram_tokens.rearrange("(a b) t -> a (b t)", a=1)
                    .broadcast_to([VOCAB, self.toks.shape[1]])).then_inc(self.tok_loaded, 16)
        q.dma_start(self.emb[:], wts["emb"]).then_inc(self.tok_loaded, 16)
        q.dma_start(self.pos[:], self.dram_pos).then_inc(self.tok_loaded, 16)
        for m in self.raw:
            for half in range(2):
                q.dma_start(self.raw[m][half * D:(half + 1) * D], wts[m].rearrange("l i o -> i l o"))\
                    .then_inc(self.w_loaded, 16)
        q.dma_start(self.w2_all[:], wts["W2"].rearrange("l (k i) o -> i l k o", i=P)).then_inc(self.w_loaded, 16)
        for k, m in enumerate(ROWS_OF):
            src = wts[m].rearrange("(a l) d -> a l d", a=1).broadcast_to([S_TXT, LAYERS, D])
            q.dma_start(self.rows_all[:, :, k], src).then_inc(self.small_loaded, 16)
        q.dma_start(self.fin_g[:], on_all_rows(wts["fin_g"], S_TXT)).then_inc(self.small_loaded, 16)
        q.dma_start(self.fin_b[:], on_all_rows(wts["fin_b"], S_TXT)).then_inc(self.small_loaded, 16)
        with nc.allow_non_contiguous_dma(reason="biases as columns, beside the heads' rows"):
            for k in range(2):
                q.dma_start(self.cols_all[:, :, 8 + k], wts["b1"][:, k * P:(k + 1) * P].rearrange("l i -> i l"))\
                    .then_inc(self.small_loaded, 16)
            for at, m in ((0, "bq"), (4, "bv")):
                for h in range(HEADS):
                    t, j = h // HPT, h % HPT
                    src = wts[m][:, h * DH:(h + 1) * DH].rearrange("l c -> c l")
                    for copy in range(3):
                        r = GROUP * j + DH * copy
                        q.dma_start(self.cols_all[r:r + DH, :, at + t], src).then_inc(self.small_loaded, 16)


def text_branch(p, inputs, ident, h_txt):
    nc, S = p.nc, p.samples
    U = p.quads
    R = S_TXT
    QW = QUAD * SP_TXT
    SCALE = 1.0 / float(np.sqrt(DH))

    with ExitStack() as ctx:
        def sb(name, shape, dtype=F32):
            return ctx.enter_context(nc.sbuf_tensor("tx_" + name, shape, dtype))

        def sem(name):
            return p.sem("tx_" + name)

        w_all = sb("w_all", [P, LAYERS, W_COLS], F32R)
        w2_all, rows_all, cols_all, fin_g, fin_b = (
            inputs.w2_all, inputs.rows_all, inputs.cols_all, inputs.fin_g, inputs.fin_b)
        row_in_group, lo_rows = sb("row_in_group", [P, 1]), sb("lo_rows", [P, 2])
        head_rows = sb("head_rows", [P, HPT])
        V = sb("V", [P, 2, QUAD, HEADS, DH + 1])
        xT = sb("xT", [P, QUAD, SP_TXT], F32R)
        xTf = sb("xTf", [P, 2, QUAD, SP_TXT], F32R)
        oT = sb("oT", [P, QUAD, SP_TXT], F32R)
        QP = sb("QP", [P, 2, TENSORS, SP_TXT], F32R)
        mpad = sb("mpad", [R, TENSORS, P], F32R)
        power = sb("power", [P, QUAD])

        with ExitStack() as setup:
            def tmp(name, shape, dtype=F32):
                return setup.enter_context(nc.sbuf_tensor("tx_" + name, shape, dtype))

            raw, toks, emb, pos_sb = inputs.raw, inputs.toks, inputs.emb, inputs.pos
            q_hi, q_lo = tmp("q_hi", [P, LAYERS, D], F32R), tmp("q_lo", [P, LAYERS, D], F32R)
            row_index = tmp("row_index", [P, 1], I32)
            steps = tmp("steps", [P, 5])
            word = tmp("word", [VOCAB, 1], I32)
            word_f = tmp("word_f", [VOCAB, 1])
            hot = tmp("hot", [VOCAB, 2, QUAD, R])
            emb_rows = [p.psum(setup, f"tx_emb_rows{k}", [P, QUAD, D]) for k in range(2)]

            cleared, indexed, masks, cut, placed = (
                sem("cleared"), sem("indexed"), sem("masks"), sem("w_cut"), sem("w_placed"))
            ones_set, hot_made, embedded, summed = (
                sem("ones_set"), sem("hot_made"), sem("embedded"), sem("pos_added"))

            with nc.Block() as block:
                @block.gpsimd
                def _(pool):
                    pool.memset(V[:], 1.0).then_inc(cleared, 1)
                    pool.memset(power[:], -0.5).then_inc(cleared, 1)
                    for t in (xT, xTf, oT, QP, mpad):
                        pool.memset(t[:].bitcast(F32), 0.0).then_inc(cleared, 1)
                    pool.memset(head_rows[:], 0.0).then_inc(cleared, 1)
                    pool.wait_ge(cleared, 8)
                    for j in range(HPT):
                        rows = slice(GROUP * j, GROUP * (j + 1))
                        pool.memset(head_rows[rows, j:j + 1], 1.0).then_inc(indexed, 1)
                        pool.wait_ge(indexed, 2 * j + 1)
                        pool.iota(row_index[rows], pattern=[[0, 1]], base=0, channel_multiplier=1).then_inc(indexed, 1)
                        pool.wait_ge(indexed, 2 * j + 2)
                    pool.iota(word[:], pattern=[[0, 1]], base=0, channel_multiplier=1).then_inc(indexed, 1)

                @block.vector
                def _(dve):
                    sec = {m: w_all[:, :, a:b] for m, (a, b) in SEC.items()}
                    dve.memset(sec["q"].bitcast(F32), 0.0).then_inc(masks, 1)
                    dve.memset(sec["k"].bitcast(F32), 0.0).then_inc(masks, 1)
                    dve.wait_ge(indexed, 2 * HPT + 1)
                    dve.tensor_copy(row_in_group[:], row_index[:]).then_inc(masks, 1)
                    dve.tensor_copy(word_f[:], word[:]).then_inc(masks, 1)
                    dve.wait_ge(masks, 4)
                    for k, edge in enumerate((DH, 2 * DH, 3 * DH, 3 * DH + 1)):
                        dve.tensor_scalar(steps[:, k:k + 1], row_in_group[:], float(edge), None, ALU.is_ge)\
                            .then_inc(masks, 1)
                    dve.wait_ge(masks, 8)
                    dve.tensor_tensor(lo_rows[:, 0:1], steps[:, 1:2], steps[:, 2:3], ALU.subtract).then_inc(masks, 1)
                    dve.tensor_tensor(lo_rows[:, 1:2], steps[:, 0:1], steps[:, 1:2], ALU.subtract).then_inc(masks, 1)
                    dve.tensor_tensor(steps[:, 4:5], steps[:, 2:3], steps[:, 3:4], ALU.subtract).then_inc(masks, 1)
                    dve.wait_ge(masks, 11)
                    dve.wait_ge(inputs.small_loaded, inputs.N_SMALL * 16)
                    dve.tensor_tensor(cols_all[:, :, 4:6], cols_all[:, :, 4:6],
                                      steps[:, 4:5].unsqueeze(1).broadcast_to([P, LAYERS, 2]), ALU.add)\
                        .then_inc(ones_set, 1)
                    dve.wait_ge(inputs.w_loaded, inputs.N_W * 16)
                    pairs = [(raw["Wq"][:], q_hi[:], q_lo[:]),
                             (raw["Wv"][:], sec["v"][:, :, 0:D], sec["v"][:, :, D:]),
                             (raw["Wo"][:], sec["o"][:, :, 0:D], sec["o"][:, :, D:]),
                             (raw["W1"][:], sec["ff1"][:, :, 0:FF], sec["ff1"][:, :, FF:])]
                    for src, hi, lo in pairs:
                        dve.tensor_copy(hi, src).then_inc(cut, 1)
                    dve.wait_ge(cut, 4)
                    for src, hi, lo in pairs:
                        dve.tensor_tensor(lo, src, hi.bitcast(F32), ALU.subtract).then_inc(cut, 1)
                    dve.wait_ge(cut, 8)
                    for part in range(2):
                        a, b = part * 2 * P, (part + 1) * 2 * P
                        place_heads(dve, sec["q"][:, :, a:b], (q_lo if part else q_hi)[:].bitcast(F32), DH, GROUP, placed)
                        place_heads(dve, sec["k"][:, :, a:b],
                                    sec["v"][:, :, part * D:(part + 1) * D].bitcast(F32), DH, GROUP, placed)
                    dve.wait_ge(ones_set, 1)
                    for at, who in ((0, 0), (4, 1)):
                        dve.tensor_scalar(cols_all[:, :, at + 2:at + 4], cols_all[:, :, at:at + 2],
                                          lo_rows[:, who:who + 1], None, ALU.mult)
                    dve.wait_ge(inputs.tok_loaded, inputs.N_TOK * 16)

                    def quad(n, par, first):
                        if not first:
                            dve.wait_ge(embedded, n - 1)
                        dve.tensor_scalar(hot[:, par].rearrange("v b t -> v (b t)"),
                                          toks[:, bass.ds(n * (QUAD * R), QUAD * R)], word_f[:, 0:1], None,
                                          ALU.is_equal).then_inc(hot_made, 1)
                        dve.wait_ge(embedded, n + 1)
                        dve.tensor_tensor(h_txt[:, bass.ds(n * QUAD, QUAD)], emb_rows[par][0:R],
                                          pos_sb[:].unsqueeze(1).broadcast_to([R, QUAD, D]), ALU.add)\
                            .then_inc(summed, 1)

                    quad(0, 0, True)
                    quad(1, 1, True)
                    with dve.Fori(1, U // 2) as i:
                        quad(i * 2, 0, False)
                        quad(i * 2 + 1, 1, False)

                @block.tensor
                def _(pe):
                    def quad(n, par, first):
                        if not first:
                            pe.wait_ge(summed, n - 1)
                        pe.wait_ge(hot_made, n + 1)
                        for b in range(QUAD):
                            last = pe.matmul(emb_rows[par][0:R, b], hot[:, par, b], emb[:], start=True, stop=True)
                        last.then_inc(embedded, 1)

                    quad(0, 0, True)
                    quad(1, 1, True)
                    with pe.Fori(1, U // 2) as i:
                        quad(i * 2, 0, False)
                        quad(i * 2 + 1, 1, False)

        w = sb("w", [P, W_COLS], F32R)
        w2 = sb("w2", [P, 2, D])
        rows = sb("rows", [R, len(ROWS_OF), D])
        cols = sb("cols", [P, 10])
        xs = sb("xs", [R, QUAD, 2 * D], F32R)
        qk_lo = sb("qk_lo", [P, 2, QW], F32R)
        KF = sb("KF", [P, TENSORS, QW], F32R)
        QF = sb("QF", [P, 2, TENSORS, QUAD, SP_TXT], F32R)
        KB = sb("KB", [P, 2, TENSORS, HPT, QW], F32R)
        PT = sb("PT", [P, 2, TENSORS, HPT * SP_TXT])
        oU = sb("oU", [P, TENSORS, SP_TXT])
        rsum = sb("rsum", [R, HEADS])
        o_rows = sb("o_rows", [R, 2, QUAD, D])
        os_ = sb("os", [R, QUAD, 2 * D], F32R)
        y = sb("y", [R, QUAD, D])
        yg = sb("yg", [R, QUAD, D])
        x_shift = sb("x_shift", [R, QUAD, D])
        stats, mean_var = sb("stats", [R, QUAD, 6]), sb("mean_var", [R, QUAD, 2])
        var_eps, rstd = sb("var_eps", [R, QUAD]), sb("rstd", [R, QUAD])
        HT = sb("HT", [P, 2, 2, QW])

        w_set = sem("w_set")
        x_hi, x_cut, x_turned, xT_set = sem("x_hi"), sem("x_cut"), sem("x_turned"), sem("xT_set")
        projected, lo_part, qk_cut, k_split = sem("projected"), sem("lo_part"), sem("qk_cut"), sem("k_split")
        v_made, v_set = sem("v_made"), sem("v_set")
        scored, max_set, max_turned, q_set = sem("scored"), sem("max_set"), sem("max_turned"), sem("q_set")
        scored_t, exped, weighed = sem("scored_t"), sem("exped"), sem("weighed")
        out_copied, outs_turned, outs_cleared = sem("out_copied"), sem("outs_turned"), sem("outs_cleared")
        sums_inv, o_set, o_hi, o_cut, o_turned, oT_set = (
            sem("sums_inv"), sem("o_set"), sem("o_hi"), sem("o_cut"), sem("o_turned"), sem("oT_set"))
        y_made, y_set, y_aggr, y_var, y_rstd, y_gain, shifted, x_new = (
            sem("y_made"), sem("y_set"), sem("y_aggr"), sem("y_var"), sem("y_rstd"),
            sem("y_gain"), sem("x_shifted"), sem("x_new"))
        f_hi, f_cut, f_turned, fT_set, f_up, f_gelu = (
            sem("f_hi"), sem("f_cut"), sem("f_turned"), sem("fT_set"), sem("f_up"), sem("f_gelu"))

        scores = p.psum(ctx, "tx_scores", [P, 2, 512])
        scores_t = p.psum(ctx, "tx_scores_t", [P, 2, 512])
        maxT = p.psum(ctx, "tx_maxT", [P, TENSORS, SP_TXT])
        out_bank = p.psum(ctx, "tx_out_bank", [P, 512])
        outT = out_bank[:, 0:TENSORS * SP_TXT].rearrange("p (t s) -> p t s", t=TENSORS)
        outs = out_bank[0:R, 256:256 + TENSORS * P].rearrange("p (t j r) -> p t j r", t=TENSORS, j=HPT)
        work = [p.psum(ctx, f"tx_work{k}", [P, 512]) for k in range(2)]

        def sec(m, part, a=0, b=None):
            lo, hi = SEC[m]
            half = (hi - lo) // 2
            return w[:, lo + part * half + a:lo + part * half + (half if b is None else b)]

        def of(m):
            return rows[:, ROWS_OF.index(m)].unsqueeze(1).broadcast_to([R, QUAD, D])

        def quads(n):
            return h_txt[:, bass.ds(n * QUAD, QUAD)]

        def turns(eng, body):
            body(0, 0, True, False, False)
            body(1, 1, False, False, False)
            if U > 4:
                with eng.Fori(1, U // 2 - 1) as i:
                    body(i * 2, 0, False, False, False)
                    body(i * 2 + 1, 1, False, False, False)
            body(U - 2, 0, False, True, False)
            body(U - 1, 1, False, True, True)

        def norm_at(l, g, ff):
            return l * (2 * U) + (U if ff else 0) + g

        def ln_stats(dve, n, y_psum, bias):
            dve.wait_ge(y_made, n + 1)
            dve.tensor_tensor(y[:], y_psum, of(bias), ALU.add).then_inc(y_set, 1)
            dve.wait_ge(y_set, n + 1)
            for b in range(QUAD):
                dve.bn_stats(stats[:, b], y[:, b])
            dve.drain()
            for b in range(QUAD):
                last = dve.bn_aggr(mean_var[:, b], stats[:, b])
            last.then_inc(y_aggr, 1)
            dve.wait_ge(y_aggr, n + 1)
            dve.tensor_scalar(var_eps[:], mean_var[:, :, 1], EPS, None, ALU.add).then_inc(y_var, 1)

        def ln_gain(dve, n, gain):
            for b in range(QUAD):
                last = dve.scalar_tensor_tensor(out=yg[:, b], in0=y[:, b], scalar=mean_var[:, b, 0:1],
                                                in1=rows[:, ROWS_OF.index(gain)], op0=ALU.subtract, op1=ALU.mult)
            last.then_inc(y_gain, 1)

        def ln_sum(dve, n, g):
            dve.wait_ge(y_gain, n + 1)
            dve.wait_ge(y_rstd, n + 1)
            dve.wait_ge(shifted, n + 1)
            for b in range(QUAD):
                last = dve.scalar_tensor_tensor(out=quads(g)[:, b], in0=yg[:, b], scalar=rstd[:, b:b + 1],
                                                in1=x_shift[:, b], op0=ALU.mult, op1=ALU.add)
            last.then_inc(x_new, 1)

        def ln_rstd(pool, n):
            pool.wait_ge(y_var, n + 1)
            pool.tensor_tensor(rstd[:], var_eps[:], power[0:R], ALU.pow).then_inc(y_rstd, 1)

        def ln_shift(pool, n, g, shift, wait):
            if wait:
                pool.wait_ge(x_new, n)
            pool.tensor_tensor(x_shift[:], quads(g), of(shift), ALU.add).then_inc(shifted, 1)

        with nc.Block() as block:
            @block.vector
            def _(dve):
                def set_weights(l):
                    dve.tensor_copy(w[:], w_all[:, bass.ds(l, 1)].rearrange("p a n -> p (a n)").bitcast(F32)).then_inc(w_set, 1)
                    dve.tensor_copy(w2[:], w2_all[:, bass.ds(l, 1)].rearrange("p a k n -> p (a k) n")).then_inc(w_set, 1)
                    dve.tensor_copy(rows[:], rows_all[:, bass.ds(l, 1)].rearrange("p a k n -> p (a k) n")).then_inc(w_set, 1)
                    dve.tensor_copy(cols[:], cols_all[:, bass.ds(l, 1)].rearrange("p a n -> p (a n)")).then_inc(w_set, 1)
                    dve.wait_ge(w_set, l * 4 + 4)

                def cut_qk(n, i, par):
                    t, is_q = i % 2, i // 2
                    dst = QF[:, par, t].rearrange("p b s -> p (b s)") if is_q else KF[:, t]
                    dve.wait_ge(lo_part, n * 4 + i + 1)
                    dve.scalar_tensor_tensor(out=dst, in0=work[(i + 1) % 2][:, 0:QW],
                                             scalar=cols[:, (0 if is_q else 4) + t:(1 if is_q else 5) + t],
                                             in1=qk_lo[:, i % 2].bitcast(F32), op0=ALU.add, op1=ALU.subtract)\
                        .then_inc(qk_cut, 1)

                def set_v(n, par):
                    dve.wait_ge(v_made, n + 1)
                    bias = of("bv").rearrange("p b (h c) -> p b h c", h=HEADS)
                    src = work[1][0:R, 0:QUAD * D].rearrange("p (b h c) -> p b h c", b=QUAD, h=HEADS)
                    dve.tensor_tensor(V[0:R, par, :, :, 0:DH], src, bias, ALU.add).then_inc(v_set, 1)

                def find_max(nb):
                    dve.wait_ge(scored, nb + 1)
                    dve.tensor_reduce(mpad[:].rearrange("p t (j r) -> p t j r", r=GROUP)[:, :, :, 3 * DH],
                                      scores[0:R, :, 0:HPT * SP_TXT].rearrange("p t (j s) -> p t j s", j=HPT)[:, :, :, 0:R],
                                      AX.X, ALU.max, negate=True).then_inc(max_set, 1)

                def join_max(nb, par, b):
                    dve.wait_ge(max_turned, nb + 1)
                    dve.tensor_tensor(QP[:, b % 2, :, 0:R], maxT[:, :, 0:R], QF[:, par, :, b, 0:R].bitcast(F32),
                                      ALU.add).then_inc(q_set, 1)

                def normalise_o(nb, par, b):
                    dve.wait_ge(outs_turned, nb + 1)
                    dve.reciprocal(rsum[:].rearrange("p (t j) -> p t j", t=TENSORS), outs[:, :, :, DH]).then_inc(sums_inv, 1)
                    dve.wait_ge(sums_inv, nb + 1)
                    dve.tensor_tensor(o_rows[:, par, b].rearrange("p (t j c) -> p t j c", t=TENSORS, j=HPT),
                                      outs[:, :, :, 0:DH],
                                      rsum[:].rearrange("p (t j) -> p t j", t=TENSORS).unsqueeze(3)
                                      .broadcast_to([R, TENSORS, HPT, DH]), ALU.mult).then_inc(o_set, 1)

                y_rows = work[1][0:R, 0:QUAD * D].rearrange("p (b d) -> p b d", b=QUAD)

                dve.memset(out_bank[:], 0.0).then_inc(outs_cleared, 1)
                dve.memset(PT[:], 0.0).then_inc(outs_cleared, 1)
                with dve.Fori(0, LAYERS) as l:
                    set_weights(l)
                    for i in range(4):
                        cut_qk(l * U, i, 0)
                    set_v(l * U, 0)
                    find_max(l * U * QUAD)
                    join_max(l * U * QUAD, 0, 0)

                    def attention(g, par, first, last2, last):
                        n = l * U + g
                        second_on = not isinstance(g, int) or g > 1
                        ln = norm_at(l, g - 1, False)
                        for b in range(QUAD):
                            more = b < QUAD - 1 or not last
                            if more:
                                find_max(n * QUAD + (b + 1))
                            if b == 2 and not last:
                                set_v(n + 1, 1 - par)
                            if more:
                                if b < QUAD - 1:
                                    join_max(n * QUAD + (b + 1), par, b + 1)
                                else:
                                    join_max(n * QUAD + QUAD, 1 - par, 0)
                            if b:
                                normalise_o(n * QUAD + (b - 1), par, b - 1)
                            elif not first:
                                normalise_o(n * QUAD - 1, 1 - par, QUAD - 1)
                            if b == 0 and not last:
                                cut_qk(n + 1, 0, 1 - par)
                                cut_qk(n + 1, 1, 1 - par)
                            if b == 1 and not last:
                                cut_qk(n + 1, 2, 1 - par)
                                cut_qk(n + 1, 3, 1 - par)
                            if b == 0 and second_on:
                                ln_gain(dve, ln - 1, "ln1_g")
                            if b == 1 and second_on:
                                ln_sum(dve, ln - 1, g - 2)
                            if b == 3 and not first:
                                ln_stats(dve, ln, y_rows, "bo")
                        if last:
                            ln_gain(dve, ln, "ln1_g")
                            ln_sum(dve, ln, g - 1)
                            ln = norm_at(l, g, False)
                            normalise_o(n * QUAD + (QUAD - 1), par, QUAD - 1)
                            ln_stats(dve, ln, y_rows, "bo")
                            ln_gain(dve, ln, "ln1_g")
                            ln_sum(dve, ln, g)

                    turns(dve, attention)

                    def feed_forward(g, par, first, last2, last):
                        ln = norm_at(l, g, True)
                        ln_stats(dve, ln, y_rows, "b2")
                        ln_gain(dve, ln, "ln2_g")
                        ln_sum(dve, ln, g)

                    turns(dve, feed_forward)

            @block.gpsimd
            def _(pool):
                def cut(rows_f32, split, hi_ready, done, n):
                    pool.wait_ge(hi_ready, n + 1)
                    pool.tensor_tensor(split[:, :, D:], rows_f32, split[:, :, 0:D].bitcast(F32), ALU.subtract)\
                        .then_inc(done, 1)

                def split_k(n, par):
                    for t in range(TENSORS):
                        pool.wait_ge(qk_cut, n * 4 + t + 1)
                        pool.tensor_tensor(KB[:, par, t], KF[:, t].bitcast(F32).unsqueeze(1).broadcast_to([P, HPT, QW]),
                                           head_rows[:].unsqueeze(2).broadcast_to([P, HPT, QW]), ALU.mult)\
                            .then_inc(k_split, 1)

                with pool.Fori(0, LAYERS) as l:
                    pool.wait_ge(w_set, l * 4 + 4)
                    cut(quads(0), xs, x_hi, x_cut, l * U)
                    split_k(l * U, 0)
                    cut(quads(1), xs, x_hi, x_cut, l * U + 1)

                    def attention(g, par, first, last2, last):
                        n = l * U + g
                        ln = norm_at(l, g - 1, False)
                        if not first:
                            cut(o_rows[:, 1 - par], os_, o_hi, o_cut, n - 1)
                        if not last:
                            split_k(n + 1, 1 - par)
                        if not first:
                            ln_shift(pool, ln, g - 1, "ln1_b", not (isinstance(g, int) and g == 1))
                        if not last2:
                            cut(quads(g + 2), xs, x_hi, x_cut, n + 2)
                        if not first:
                            ln_rstd(pool, ln)
                        if last:
                            ln = norm_at(l, g, False)
                            cut(o_rows[:, par], os_, o_hi, o_cut, n)
                            ln_shift(pool, ln, g, "ln1_b", True)
                            ln_rstd(pool, ln)

                    turns(pool, attention)
                    cut(quads(0), xs, f_hi, f_cut, l * U)
                    cut(quads(1), xs, f_hi, f_cut, l * U + 1)

                    def feed_forward(g, par, first, last2, last):
                        n, ln = l * U + g, norm_at(l, g, True)
                        if not last2:
                            cut(quads(g + 2), xs, f_hi, f_cut, n + 2)
                        ln_shift(pool, ln, g, "ln2_b", True)
                        ln_rstd(pool, ln)

                    turns(pool, feed_forward)

            @block.scalar
            def _(act):
                def hi(rows_f32, split, done):
                    act.activation(split[:, :, 0:D], rows_f32, ACT.Copy).then_inc(done, 1)

                def set_turned(dst, turned, done, n):
                    act.wait_ge(turned, n + 1)
                    act.activation(dst[:, :, 0:R], work[0][:, 0:QUAD * R].rearrange("p (b s) -> p b s", b=QUAD), ACT.Copy)\
                        .then_inc(done, 1)

                def part_lo(n, i):
                    t, is_q = i % 2, i // 2
                    at = (2 if is_q else 6) + t
                    act.wait_ge(projected, n * 4 + i + 1)
                    act.activation(qk_lo[:, i % 2], work[(i + 1) % 2][:, 0:QW], ACT.Identity,
                                   bias=cols[:, at:at + 1], scale=lo_rows[:, 1 - is_q:2 - is_q]).then_inc(lo_part, 1)

                def exp(nb, b, fresh):
                    act.wait_ge(scored_t, nb + 1)
                    if not fresh:
                        act.wait_ge(weighed, nb - 1)
                    act.activation(PT[0:R, b % 2], scores_t[0:R, :, 0:HPT * SP_TXT], ACT.Exp, scale=SCALE)\
                        .then_inc(exped, 1)

                def copy_outs(nb):
                    act.wait_ge(weighed, nb + 1)
                    act.activation(oU[:], outT, ACT.Copy).then_inc(out_copied, 1)

                def gelu(n, par):
                    act.wait_ge(f_up, n + 1)
                    for half in range(2):
                        src = (scores_t if par else scores)[:, half, 0:QW]
                        last = act.activation(HT[:, par, half], src, ACT.Gelu, bias=cols[:, 8 + half:9 + half])
                    last.then_inc(f_gelu, 1)

                with act.Fori(0, LAYERS) as l:
                    act.wait_ge(w_set, l * 4 + 4)
                    hi(quads(0), xs, x_hi)
                    set_turned(xT, x_turned, xT_set, l * U)
                    for i in range(4):
                        part_lo(l * U, i)
                    hi(quads(1), xs, x_hi)

                    def attention(g, par, first, last2, last):
                        n = l * U + g
                        for b in range(QUAD):
                            exp(n * QUAD + b, b, first and b < 2)
                            if b == 0 and not last:
                                set_turned(xT, x_turned, xT_set, n + 1)
                            if b or not first:
                                copy_outs(n * QUAD + (b - 1))
                            if b == 0 and not last:
                                part_lo(n + 1, 0)
                                part_lo(n + 1, 1)
                            if b == 1 and not last:
                                part_lo(n + 1, 2)
                                part_lo(n + 1, 3)
                            if b == 0 and not first:
                                act.wait_ge(o_set, n * QUAD)
                                hi(o_rows[:, 1 - par], os_, o_hi)
                            if b == 2 and not last2:
                                hi(quads(g + 2), xs, x_hi)
                            if b == 2 and not first:
                                set_turned(oT, o_turned, oT_set, n - 1)
                        if last:
                            copy_outs(n * QUAD + (QUAD - 1))
                            act.wait_ge(o_set, n * QUAD + QUAD)
                            hi(o_rows[:, par], os_, o_hi)
                            set_turned(oT, o_turned, oT_set, n)

                    turns(act, attention)
                    act.wait_ge(x_new, norm_at(l, 0, False) + 1)
                    hi(quads(0), xs, f_hi)
                    set_turned(xTf[:, 0], f_turned, fT_set, l * U)
                    gelu(l * U, 0)
                    act.wait_ge(x_new, norm_at(l, 1, False) + 1)
                    hi(quads(1), xs, f_hi)
                    set_turned(xTf[:, 1], f_turned, fT_set, l * U + 1)

                    def feed_forward(g, par, first, last2, last):
                        n = l * U + g
                        if not last2:
                            act.wait_ge(x_new, norm_at(l, g + 2, False) + 1)
                            hi(quads(g + 2), xs, f_hi)
                        if not last:
                            gelu(n + 1, 1 - par)
                        if not last2:
                            set_turned(xTf[:, par], f_turned, fT_set, n + 2)

                    turns(act, feed_forward)

            @block.tensor
            def _(pe):
                def turn(src, ready, done, n):
                    pe.wait_ge(ready, n + 1)
                    for b in range(QUAD):
                        last = pe.transpose(work[0][:, b * R:(b + 1) * R], src[:, b].bitcast(F32), ident[0:R, 0:R])
                    last.then_inc(done, 1)

                def project(n, i):
                    t, m = i % 2, "q" if i // 2 else "k"
                    if i >= 2:
                        pe.wait_ge(qk_cut, n * 4 + i - 1)
                    for part in range(2):
                        last = pe.matmul(work[(i + 1) % 2][:, 0:QW], sec(m, part, t * P, (t + 1) * P),
                                         xT[:].rearrange("p b s -> p (b s)"), start=part == 0, stop=part == 1)
                    last.then_inc(projected, 1)

                def project_v(n):
                    pe.wait_ge(qk_cut, n * 4 + 3)
                    for b in range(QUAD):
                        for part in range(2):
                            last = pe.matmul(work[1][0:R, b * D:(b + 1) * D], xT[:, b, 0:R], sec("v", part),
                                             start=part == 0, stop=part == 1)
                    last.then_inc(v_made, 1)

                def score(n, par, b):
                    if b == 0:
                        pe.wait_ge(k_split, n * 2 + 2)
                        pe.wait_ge(qk_cut, n * 4 + 4)
                    for t in range(TENSORS):
                        k = KB[:, par, t].rearrange("p j (b s) -> p j b s", b=QUAD)[:, :, b]
                        last = pe.matmul(scores[0:R, t, 0:HPT * SP_TXT], QF[:, par, t, b, 0:R], k, start=True, stop=True)
                    last.then_inc(scored, 1)

                def turn_max(nb):
                    pe.wait_ge(max_set, nb + 1)
                    for t in range(TENSORS):
                        last = pe.transpose(maxT[:, t, 0:R], mpad[:, t].bitcast(F32), ident[0:R, 0:R])
                    last.then_inc(max_turned, 1)

                def score_t(n, par, b, fresh):
                    nb = n * QUAD + b
                    pe.wait_ge(q_set, nb + 1)
                    if not fresh:
                        pe.wait_ge(exped, nb)
                    for t in range(TENSORS):
                        for j in range(HPT):
                            k = KB[:, par, t, j].rearrange("p (b s) -> p b s", b=QUAD)[:, b, 0:R]
                            last = pe.matmul(scores_t[0:R, t, j * SP_TXT:(j + 1) * SP_TXT], k, QP[:, b % 2, t],
                                             start=True, stop=True)
                    last.then_inc(scored_t, 1)

                def weigh(nb, n, par, b, fresh):
                    pe.wait_ge(exped, nb + 1)
                    if b == 0:
                        pe.wait_ge(v_set, n + 1)
                    if not fresh:
                        pe.wait_ge(o_set, nb)
                    for t in range(TENSORS):
                        for j in range(HPT):
                            last = pe.matmul(outT[32 * j:32 * j + DH + 1, t], V[:, par, b, t * HPT + j],
                                             PT[:, b % 2, t, j * SP_TXT:(j + 1) * SP_TXT], start=True, stop=True)
                    last.then_inc(weighed, 1)

                def turn_outs(nb):
                    pe.wait_ge(out_copied, nb + 1)
                    for t in range(TENSORS):
                        last = pe.transpose(out_bank[0:R, 256 + t * P:256 + (t + 1) * P], oU[:, t, 0:R], ident[:])
                    last.then_inc(outs_turned, 1)

                def project_o(n, ln, bank_ready):
                    pe.wait_ge(oT_set, n + 1)
                    pe.wait_ge(*bank_ready)
                    for b in range(QUAD):
                        for part in range(2):
                            last = pe.matmul(work[1][0:R, b * D:(b + 1) * D], oT[:, b, 0:R], sec("o", part),
                                             start=part == 0, stop=part == 1)
                    last.then_inc(y_made, 1)

                def up(n, par):
                    pe.wait_ge(fT_set, n + 1)
                    for half in range(2):
                        for part in range(2):
                            last = pe.matmul((scores_t if par else scores)[:, half, 0:QW],
                                             sec("ff1", part, half * P, (half + 1) * P),
                                             xTf[:, par].rearrange("p b s -> p (b s)"), start=part == 0, stop=part == 1)
                    last.then_inc(f_up, 1)

                def down(n, ln, par):
                    pe.wait_ge(f_gelu, n + 1)
                    pe.wait_ge(y_set, ln)
                    for b in range(QUAD):
                        for half in range(2):
                            last = pe.matmul(work[1][0:R, b * D:(b + 1) * D],
                                             HT[:, par, half].rearrange("p (b s) -> p b s", b=QUAD)[:, b, 0:R],
                                             w2[:, half], start=half == 0, stop=half == 1)
                    last.then_inc(y_made, 1)

                pe.wait_ge(outs_cleared, 2)
                with pe.Fori(0, LAYERS) as l:
                    pe.wait_ge(w_set, l * 4 + 4)
                    turn(xs, x_cut, x_turned, l * U)
                    pe.wait_ge(xT_set, l * U + 1)
                    for i in range(4):
                        project(l * U, i)
                    project_v(l * U)
                    score(l * U, 0, 0)
                    turn_max(l * U * QUAD)

                    def attention(g, par, first, last2, last):
                        n = l * U + g
                        ln = norm_at(l, g - 1, False)
                        for b in range(QUAD):
                            more = b < QUAD - 1 or not last
                            score_t(n, par, b, first and b == 0)
                            if b < QUAD - 1:
                                score(n, par, b + 1)
                            elif not last:
                                score(n + 1, 1 - par, 0)
                            if b > 0:
                                weigh(n * QUAD + (b - 1), n, par, b - 1, first and b == 1)
                            elif not first:
                                weigh(n * QUAD - 1, n - 1, 1 - par, QUAD - 1, False)
                            if b == 0 and not last:
                                turn(xs, x_cut, x_turned, n + 1)
                            if b == 1 and not last:
                                project(n + 1, 2)
                                project(n + 1, 3)
                            if b == 2 and not last:
                                project_v(n + 1)
                            if b == 3 and not first:
                                project_o(n - 1, ln, (y_set, ln) if last else (v_set, n + 2))
                            if more:
                                turn_max(n * QUAD + (b + 1))
                            if b or not first:
                                turn_outs(n * QUAD + (b - 1))
                            if b == 0 and not last:
                                pe.wait_ge(xT_set, n + 2)
                                if first or isinstance(g, int) and g == 1:
                                    pe.wait_ge(v_set, n + 1)
                                else:
                                    pe.wait_ge(y_set, ln)
                                project(n + 1, 0)
                                project(n + 1, 1)
                            if b == 2 and not first:
                                if not last:
                                    pe.wait_ge(qk_cut, n * 4 + 8)
                                turn(os_, o_cut, o_turned, n - 1)
                        if last:
                            weigh(n * QUAD + (QUAD - 1), n, par, QUAD - 1, False)
                            turn_outs(n * QUAD + (QUAD - 1))
                            turn(os_, o_cut, o_turned, n)
                            project_o(n, norm_at(l, g, False), (y_set, ln + 1))

                    turns(pe, attention)
                    turn(xs, f_cut, f_turned, l * U)
                    up(l * U, 0)
                    turn(xs, f_cut, f_turned, l * U + 1)

                    def feed_forward(g, par, first, last2, last):
                        n = l * U + g
                        if not last:
                            up(n + 1, 1 - par)
                        down(n, norm_at(l, g, True), par)
                        if not last2:
                            turn(xs, f_cut, f_turned, n + 2)

                    turns(pe, feed_forward)

        end_aggr, end_var, end_rstd, end_scaled, end_done = (
            sem("end_aggr"), sem("end_var"), sem("end_rstd"), sem("end_scaled"), sem("end_done"))

        def over_quads(eng, body):
            body(0, 0, True)
            body(1, 1, True)
            with eng.Fori(1, U // 2) as i:
                body(i * 2, 0, False)
                body(i * 2 + 1, 1, False)

        with nc.Block() as block:
            @block.vector
            def _(dve):
                def quad(n, par, first):
                    q = quads(n)
                    for b in range(QUAD):
                        dve.bn_stats(stats[:, b], q[:, b])
                    dve.drain()
                    for b in range(QUAD):
                        last = dve.bn_aggr(mean_var[:, b], stats[:, b])
                    last.then_inc(end_aggr, 1)
                    dve.wait_ge(end_aggr, n + 1)
                    dve.tensor_scalar(var_eps[:], mean_var[:, :, 1], EPS, None, ALU.add).then_inc(end_var, 1)
                    for b in range(QUAD):
                        last = dve.scalar_tensor_tensor(out=yg[:, b], in0=q[:, b], scalar=mean_var[:, b, 0:1],
                                                        in1=fin_g[:], op0=ALU.subtract, op1=ALU.mult)
                    last.then_inc(end_scaled, 1)
                    dve.wait_ge(end_scaled, n + 1)
                    dve.wait_ge(end_rstd, n + 1)
                    for b in range(QUAD):
                        last = dve.scalar_tensor_tensor(out=q[:, b], in0=yg[:, b], scalar=rstd[:, b:b + 1],
                                                        in1=fin_b[:], op0=ALU.mult, op1=ALU.add)
                    last.then_inc(end_done, 1)

                over_quads(dve, quad)

            @block.gpsimd
            def _(pool):
                def quad(n, par, first):
                    pool.wait_ge(end_var, n + 1)
                    pool.tensor_tensor(rstd[:], var_eps[:], power[0:R], ALU.pow).then_inc(end_rstd, 1)

                over_quads(pool, quad)



SEQ = T + S_TXT
SEQP = SEQ + 1
TILES = ((0, T), (T, S_TXT))
A_HEADS = 4
A_DH = D // A_HEADS
A_GROUP = 64
A_HPT = P // A_GROUP
A_TENSORS = A_HEADS // A_HPT
A_HALF = A_TENSORS * P
CLIP = 10000.0
EXPERTS = 8


def live(n):
    return not isinstance(n, int) or 0 <= n < B


def due(value):
    return not isinstance(value, int) or value > 0


def set_stats(dve, rows_of, mean_var, stats, var_eps, aggregated, var_ready, m):
    for t, (_, n) in enumerate(TILES):
        dve.bn_stats(stats[0:n, t], rows_of(m, t))
    dve.drain()
    for t, (_, n) in enumerate(TILES):
        last = dve.bn_aggr(mean_var[0:n, t], stats[0:n, t])
    last.then_inc(aggregated, 1)
    dve.wait_ge(aggregated, m + 1)
    dve.tensor_scalar(var_eps[:], mean_var[:, :, 1], EPS, None, ALU.add).then_inc(var_ready, 1)


class AttentionInputs:

    MATS = ("Wq", "Wk", "Wv", "Wo")

    def __init__(self, p, wts):
        self.nc, self.wts = p.nc, wts
        self.raw = p.sb("at_raw", [D, len(self.MATS), 2 * D])
        self.bv, self.bo = p.sb("at_bv", [P, D]), p.sb("at_bo", [D + 1, D])
        self.cols = p.sb("at_cols", [P, 8])
        self.loaded = p.sem("at_loaded")
        self.N = 2 * len(self.MATS) + 2 + 2 * A_HEADS * 3

    def load(self, q):
        wts = self.wts
        for k, m in enumerate(self.MATS):
            for half in range(2):
                q.dma_start(self.raw[:, k, half * D:(half + 1) * D], wts[m]).then_inc(self.loaded, 16)
        q.dma_start(self.bv[:], on_all_rows(wts["bv"])).then_inc(self.loaded, 16)
        q.dma_start(self.bo[D:D + 1], row(wts["bo"])).then_inc(self.loaded, 16)
        with self.nc.allow_non_contiguous_dma(reason="biases as columns, beside the heads' rows"):
            for at, m in ((0, "bq"), (4, "bk")):
                for h in range(A_HEADS):
                    t, j = h // A_HPT, h % A_HPT
                    src = wts[m][h * A_DH:(h + 1) * A_DH].rearrange("(n a) -> n a", a=1)
                    for copy in range(3):
                        r = A_GROUP * j + A_DH * copy
                        q.dma_start(self.cols[r:r + A_DH, at + t:at + t + 1], src).then_inc(self.loaded, 16)


def fusion_attention(p, inputs, ident, rows_of):
    nc = p.nc
    SCALE = 1.0 / float(np.sqrt(A_DH))

    with ExitStack() as ctx:
        def sb(name, shape, dtype=F32):
            return ctx.enter_context(nc.sbuf_tensor("at_" + name, shape, dtype))

        def sem(name):
            return p.sem("at_" + name)

        wq, wk = sb("wq", [P, 2, A_HALF], F32R), sb("wk", [P, 2, A_HALF], F32R)
        wv, wo = sb("wv", [P, 2, D], F32R), sb("wo", [D + 1, 2, D], F32R)
        bv, cols = inputs.bv, inputs.cols
        lo_rows, head_rows = sb("lo_rows", [P, 2]), sb("head_rows", [P, A_HPT])
        power = sb("power", [P, 2])

        stats, mean_var = sb("stats", [P, 2, 6]), sb("mean_var", [P, 2, 2])
        var_eps, rstd = sb("var_eps", [P, 2]), sb("rstd", [P, 2])
        z, zc = sb("z", [P, 2, D]), sb("zc", [P, 2, D])
        xs = sb("xs", [P, 2, 2 * D], F32R)
        xT = sb("xT", [P, SEQP], F32R)
        qk_lo = sb("qk_lo", [P, 2, SEQP], F32R)
        KF = sb("KF", [P, A_TENSORS, SEQP], F32R)
        QF = sb("QF", [P, 2, A_TENSORS, SEQP], F32R)
        KB = sb("KB", [P, 2, A_TENSORS, A_HPT, SEQP], F32R)
        QP = sb("QP", [P, 2, A_TENSORS, SEQP], F32R)
        mpad = sb("mpad", [P, 2, A_TENSORS, P], F32R)
        PT = sb("PT", [P, 2, A_TENSORS, A_HPT * SEQP])
        V = sb("V", [P, 2, 2, A_HEADS, A_DH + 1])
        oU = sb("oU", [P, SEQP])
        rsum = sb("rsum", [P, 2, A_HEADS])
        o_rows = sb("o_rows", [P, 2, 2, P], BF16)
        oT = sb("oT", [D + 1, SEQP], F32R)
        ident_bf = sb("ident_bf", [P, P], BF16)

        scores = p.psum(ctx, "at_scores", [P, 2, 512])
        scores_t = p.psum(ctx, "at_scores_t", [P, 2, 512])
        maxT = p.psum(ctx, "at_maxT", [P, A_TENSORS, SEQP])
        outT = p.psum(ctx, "at_outT", [P, SEQP + 2 * P])
        outs = outT[:, SEQP:].rearrange("p (a h r) -> p a h r", a=2, h=A_HEADS)
        work = [p.psum(ctx, f"at_work{k}", [P, 512]) for k in range(2)]

        with ExitStack() as setup:
            def tmp(name, shape, dtype=F32):
                return setup.enter_context(nc.sbuf_tensor("at_" + name, shape, dtype))

            MATS, raw, bo = inputs.MATS, inputs.raw, inputs.bo
            hi, lo = tmp("hi", [P, len(MATS), D], F32R), tmp("lo", [P, len(MATS), D], F32R)
            row_index = tmp("row_index", [P, 1], I32)
            row_in_group = tmp("row_in_group", [P, 1])
            steps = tmp("steps", [P, 5])
            cleared, indexed, masks, ones_set = sem("cleared"), sem("indexed"), sem("masks"), sem("ones_set")
            turned, w_hi, w_lo, placed = sem("w_turned"), sem("w_hi"), sem("w_lo"), sem("w_placed")
            turn = work[0][:, 0:len(MATS) * D].rearrange("p (m o) -> p m o", m=len(MATS))

            with nc.Block() as block:
                @block.scalar
                def _(act):
                    act.wait_ge(turned, 1)
                    act.activation(hi[:], turn, ACT.Copy).then_inc(w_hi, 1)

                @block.gpsimd
                def _(pool):
                    pool.memset(V[:], 1.0).then_inc(cleared, 1)
                    pool.memset(power[:], -0.5).then_inc(cleared, 1)
                    for t in (xT, QP, mpad):
                        pool.memset(t[:].bitcast(F32), 0.0).then_inc(cleared, 1)
                    pool.memset(oT[:].bitcast(F32), 1.0).then_inc(cleared, 1)
                    for t in (z, mean_var, head_rows, o_rows):
                        pool.memset(t[:], 0.0).then_inc(cleared, 1)
                    pool.tensor_copy(ident_bf[:], ident[:]).then_inc(cleared, 1)
                    pool.wait_ge(cleared, 11)
                    for j in range(A_HPT):
                        rows = slice(A_GROUP * j, A_GROUP * (j + 1))
                        pool.memset(head_rows[rows, j:j + 1], 1.0).then_inc(indexed, 1)
                        pool.wait_ge(indexed, 2 * j + 1)
                        pool.iota(row_index[rows], pattern=[[0, 1]], base=0, channel_multiplier=1).then_inc(indexed, 1)
                        pool.wait_ge(indexed, 2 * j + 2)

                @block.tensor
                def _(pe):
                    pe.wait_ge(inputs.loaded, inputs.N * 16)
                    for k in range(len(MATS)):
                        last = pe.transpose(turn[:, k], raw[:, k], ident[0:D, 0:D])
                    last.then_inc(turned, 1)

                @block.vector
                def _(dve):
                    dve.memset(wq[:].bitcast(F32), 0.0).then_inc(masks, 1)
                    dve.memset(wk[:].bitcast(F32), 0.0).then_inc(masks, 1)
                    dve.memset(outT[:], 1.0).then_inc(masks, 1)
                    dve.wait_ge(indexed, 2 * A_HPT)
                    dve.tensor_copy(row_in_group[:], row_index[:]).then_inc(masks, 1)
                    dve.wait_ge(masks, 4)
                    for k, edge in enumerate((A_DH, 2 * A_DH, 3 * A_DH, 3 * A_DH + 1)):
                        dve.tensor_scalar(steps[:, k:k + 1], row_in_group[:], float(edge), None, ALU.is_ge)\
                            .then_inc(masks, 1)
                    dve.wait_ge(masks, 8)
                    dve.tensor_tensor(lo_rows[:, 0:1], steps[:, 1:2], steps[:, 2:3], ALU.subtract).then_inc(masks, 1)
                    dve.tensor_tensor(lo_rows[:, 1:2], steps[:, 0:1], steps[:, 1:2], ALU.subtract).then_inc(masks, 1)
                    dve.tensor_tensor(steps[:, 4:5], steps[:, 2:3], steps[:, 3:4], ALU.subtract).then_inc(masks, 1)
                    dve.wait_ge(masks, 11)
                    dve.wait_ge(inputs.loaded, inputs.N * 16)
                    dve.tensor_tensor(cols[:, 4:6], cols[:, 4:6], steps[:, 4:5].broadcast_to([P, 2]), ALU.add)\
                        .then_inc(ones_set, 1)
                    dve.wait_ge(w_hi, 1)
                    dve.tensor_tensor(lo[:], turn, hi[:].bitcast(F32), ALU.subtract).then_inc(w_lo, 1)
                    dve.tensor_copy(wo[D:D + 1, 0], bo[D:D + 1]).then_inc(w_lo, 1)
                    dve.wait_ge(w_lo, 2)
                    for part, src in ((0, hi), (1, lo)):
                        for k, dst in ((0, wq), (1, wk)):
                            place_heads(dve, dst[:, part:part + 1], src[:, k:k + 1].bitcast(F32), A_DH, A_GROUP, placed)
                        dve.tensor_copy(wv[:, part], src[:, 2].bitcast(F32))
                        dve.tensor_copy(wo[0:D, part], src[0:D, 3].bitcast(F32))
                    dve.tensor_tensor(wo[D:D + 1, 1], bo[D:D + 1], wo[D:D + 1, 0].bitcast(F32), ALU.subtract)
                    dve.wait_ge(ones_set, 1)
                    for at, who in ((0, 0), (4, 1)):
                        dve.tensor_scalar(cols[:, at + 2:at + 4], cols[:, at:at + 2], lo_rows[:, who:who + 1],
                                          None, ALU.mult)

        aggregated, var_ready, rstd_ready, normed, z_ready, x_hi, x_cut, x_turned, xT_set = (
            sem("aggregated"), sem("var_ready"), sem("rstd_ready"), sem("normed"), sem("z_ready"), sem("x_hi"),
            sem("x_cut"), sem("x_turned"), sem("xT_set"))
        projected, lo_part, qk_cut, k_split, v_made, v_set = (
            sem("projected"), sem("lo_part"), sem("qk_cut"), sem("k_split"), sem("v_made"), sem("v_set"))
        scored, max_set, max_turned, q_set = sem("scored"), sem("max_set"), sem("max_turned"), sem("q_set")
        out_copied, outs_turned = sem("out_copied"), sem("outs_turned")
        scored_t, exped, weighed, sums_inv, o_set, o_turned, oT_set, y_made, y_added = (
            sem("scored_t"), sem("exped"), sem("weighed"), sem("sums_inv"), sem("o_set"), sem("o_turned"),
            sem("oT_set"), sem("y_made"), sem("y_added"))

        def each_step(eng, step):
            for n in range(-3, 2):
                step(n, n % 2)
            with eng.Fori(1, B // 2 - 2) as i:
                step(i * 2, 0)
                step(i * 2 + 1, 1)
            for n in range(B - 4, B + 1):
                step(n, n % 2)

        with nc.Block() as block:
            @block.vector
            def _(dve):
                def find_max(m, tile):
                    n = TILES[tile][1]
                    dve.wait_ge(scored, m * 2 + (tile + 1))
                    if tile == 0 and due(m):
                        dve.wait_ge(max_turned, m)
                    dve.tensor_reduce(mpad[0:n, tile].rearrange("p t (j r) -> p t j r", r=A_GROUP)[:, :, :, 3 * A_DH],
                                      scores[0:n, :, 0:A_HPT * SEQP].rearrange("p t (j s) -> p t j s", j=A_HPT)[:, :, :, 0:SEQ],
                                      AX.X, ALU.max, negate=True).then_inc(max_set, 1)

                def join_max(m, par):
                    dve.wait_ge(max_turned, m + 1)
                    if due(m * 2 - 2):
                        dve.wait_ge(scored_t, m * 2 - 2)
                    dve.tensor_tensor(QP[:, par, :, 0:SEQ], maxT[:, :, 0:SEQ], QF[:, par, :, 0:SEQ].bitcast(F32),
                                      ALU.add).then_inc(q_set, 1)

                def cut_qk(m, i, par):
                    t, is_q = i % 2, i // 2
                    dst = QF[:, par, t] if is_q else KF[:, t]
                    dve.wait_ge(lo_part, m * 4 + (i + 1))
                    if i == 0 and due(m * 2):
                        dve.wait_ge(k_split, m * 2)
                    dve.scalar_tensor_tensor(out=dst, in0=work[(i + 1) % 2][:, 0:SEQP],
                                             scalar=cols[:, (0 if is_q else 4) + t:(1 if is_q else 5) + t],
                                             in1=qk_lo[:, i % 2].bitcast(F32), op0=ALU.add, op1=ALU.subtract)\
                        .then_inc(qk_cut, 1)

                def set_v(m, par):
                    dve.wait_ge(v_made, m + 1)
                    if due(m - 1):
                        dve.wait_ge(weighed, m - 1)
                    for tile, (_, n) in enumerate(TILES):
                        last = dve.tensor_tensor(
                            V[0:n, par, tile, :, 0:A_DH],
                            work[1][0:n, tile * D:(tile + 1) * D].rearrange("p (h c) -> p h c", h=A_HEADS),
                            bv[0:n].rearrange("p (h c) -> p h c", h=A_HEADS), ALU.add)
                    last.then_inc(v_set, 1)

                def norm_z(m):
                    dve.wait_ge(rstd_ready, m + 1)
                    for tile, (_, n) in enumerate(TILES):
                        last = dve.tensor_scalar(z[0:n, tile], rows_of(m, tile), mean_var[0:n, tile, 0:1],
                                                 rstd[0:n, tile:tile + 1], ALU.subtract, ALU.mult)
                    last.then_inc(normed, 1)
                    dve.wait_ge(normed, m + 1)
                    if due(m):
                        dve.wait_ge(x_cut, m)
                    dve.tensor_scalar(zc[:], z[:], -CLIP, CLIP, ALU.max, ALU.min).then_inc(z_ready, 1)

                def normalise_o(m, par):
                    dve.wait_ge(outs_turned, m + 1)
                    if due(m - 1):
                        dve.wait_ge(o_turned, m - 1)
                    dve.reciprocal(rsum[:], outs[:, :, :, A_DH]).then_inc(sums_inv, 1)
                    dve.wait_ge(sums_inv, m + 1)
                    dve.tensor_tensor(o_rows[:, par, :, 0:D].rearrange("p a (h c) -> p a h c", h=A_HEADS), outs[:, :, :, 0:A_DH],
                                      rsum[:].unsqueeze(3).broadcast_to([P, 2, A_HEADS, A_DH]), ALU.mult)\
                        .then_inc(o_set, 1)

                def add_y(m):
                    dve.wait_ge(y_made, m + 1)
                    for tile, (_, n) in enumerate(TILES):
                        last = dve.tensor_tensor(rows_of(m, tile), rows_of(m, tile),
                                                 work[1][0:n, tile * D:(tile + 1) * D], ALU.add)
                    last.then_inc(y_added, 1)

                def step(n, par):
                    if live(n + 3):
                        set_stats(dve, rows_of, mean_var, stats, var_eps, aggregated, var_ready, n + 3)
                    if live(n + 1):
                        find_max(n + 1, 0)
                    if live(n - 1):
                        add_y(n - 1)
                    if live(n + 1):
                        find_max(n + 1, 1)
                    if live(n + 2):
                        cut_qk(n + 2, 0, par)
                        cut_qk(n + 2, 1, par)
                    if live(n + 3):
                        norm_z(n + 3)
                    if live(n + 1):
                        join_max(n + 1, 1 - par)
                    if live(n + 2):
                        cut_qk(n + 2, 2, par)
                        cut_qk(n + 2, 3, par)
                        set_v(n + 2, par)
                    if live(n):
                        normalise_o(n, par)

                each_step(dve, step)

            @block.gpsimd
            def _(pool):
                def step(n, par):
                    if live(n + 3):
                        pool.wait_ge(var_ready, n + 4)
                        pool.tensor_tensor(rstd[:], var_eps[:], power[:], ALU.pow).then_inc(rstd_ready, 1)
                    if live(n + 2):
                        m = n + 2
                        if due(m * 2 - 2):
                            pool.wait_ge(scored_t, m * 2 - 2)
                        for t in range(A_TENSORS):
                            pool.wait_ge(qk_cut, m * 4 + (t + 1))
                            pool.tensor_tensor(KB[:, par, t],
                                               KF[:, t].bitcast(F32).unsqueeze(1).broadcast_to([P, A_HPT, SEQP]),
                                               head_rows[:].unsqueeze(2).broadcast_to([P, A_HPT, SEQP]), ALU.mult)\
                                .then_inc(k_split, 1)
                    if live(n + 3):
                        pool.wait_ge(x_hi, n + 4)
                        pool.tensor_tensor(xs[:, :, D:], zc[:], xs[:, :, 0:D].bitcast(F32), ALU.subtract)\
                            .then_inc(x_cut, 1)

                each_step(pool, step)

            @block.scalar
            def _(act):
                def exp(m, tile):
                    n = TILES[tile][1]
                    act.wait_ge(scored_t, m * 2 + (tile + 1))
                    if tile == 0 and due(m):
                        act.wait_ge(weighed, m)
                    act.activation(PT[0:n, tile], scores_t[0:n, :, 0:A_HPT * SEQP], ACT.Exp, scale=SCALE)\
                        .then_inc(exped, 1)

                def part_lo(m, i):
                    t, is_q = i % 2, i // 2
                    at = (2 if is_q else 6) + t
                    act.wait_ge(projected, m * 4 + (i + 1))
                    if due(m * 4 + (i - 1)):
                        act.wait_ge(qk_cut, m * 4 + (i - 1))
                    act.activation(qk_lo[:, i % 2], work[(i + 1) % 2][:, 0:SEQP], ACT.Identity,
                                   bias=cols[:, at:at + 1], scale=lo_rows[:, 1 - is_q:2 - is_q]).then_inc(lo_part, 1)

                def step(n, par):
                    if live(n):
                        exp(n, 0)
                    if live(n - 1):
                        act.wait_ge(o_turned, n)
                        if due(n - 1):
                            act.wait_ge(y_made, n - 1)
                        act.activation(oT[0:D, 0:SEQ], work[0][:].bitcast(BF16)[0:D, 0:SEQ], ACT.Copy).then_inc(oT_set, 1)
                    if live(n):
                        exp(n, 1)
                    if live(n + 2):
                        act.wait_ge(x_turned, n + 3)
                        if due(n + 2):
                            act.wait_ge(v_made, n + 2)
                        act.activation(xT[:, 0:SEQ], work[0][:, 0:SEQ], ACT.Copy).then_inc(xT_set, 1)
                        part_lo(n + 2, 0)
                        part_lo(n + 2, 1)
                    if live(n):
                        act.wait_ge(weighed, n + 1)
                        if due(n):
                            act.wait_ge(outs_turned, n)
                        act.activation(oU[:], outT[:, 0:SEQP], ACT.Copy).then_inc(out_copied, 1)
                    if live(n + 2):
                        part_lo(n + 2, 2)
                        part_lo(n + 2, 3)
                    if live(n + 3):
                        act.wait_ge(z_ready, n + 4)
                        if due(n + 3):
                            act.wait_ge(x_turned, n + 3)
                        act.activation(xs[:, :, 0:D], zc[:], ACT.Copy).then_inc(x_hi, 1)

                each_step(act, step)

            @block.tensor
            def _(pe):
                def score(m, par, tile):
                    at, n = TILES[tile]
                    if tile == 0:
                        pe.wait_ge(k_split, m * 2 + 2)
                        pe.wait_ge(qk_cut, m * 4 + 4)
                    if due(m * 2 + tile):
                        pe.wait_ge(max_set, m * 2 + tile)
                    for t in range(A_TENSORS):
                        last = pe.matmul(scores[0:n, t, 0:A_HPT * SEQP], QF[:, par, t, at:at + n],
                                         KB[:, par, t].rearrange("p j s -> p (j s)"), start=True, stop=True)
                    last.then_inc(scored, 1)

                def score_t(m, par, tile):
                    at, n = TILES[tile]
                    if tile == 0:
                        pe.wait_ge(q_set, m + 1)
                    if due(m * 2 + tile):
                        pe.wait_ge(exped, m * 2 + tile)
                    for t in range(A_TENSORS):
                        for j in range(A_HPT):
                            last = pe.matmul(scores_t[0:n, t, j * SEQP:(j + 1) * SEQP], KB[:, par, t, j, at:at + n],
                                             QP[:, par, t], start=True, stop=True)
                    last.then_inc(scored_t, 1)

                def turn_x(m):
                    pe.wait_ge(x_cut, m + 1)
                    if due(m):
                        pe.wait_ge(qk_cut, m * 4)
                    if due(m - 2):
                        pe.wait_ge(oT_set, m - 2)
                    for tile, (at, n) in enumerate(TILES):
                        last = pe.transpose(work[0][:, at:at + n], xs[0:n, tile].bitcast(F32), ident[0:n, 0:n])
                    last.then_inc(x_turned, 1)

                def project(m, i):
                    t, wgt = i % 2, wq if i // 2 else wk
                    if i == 0:
                        pe.wait_ge(xT_set, m + 1)
                        if due(m):
                            pe.wait_ge(v_set, m)
                        if due(m - 2):
                            pe.wait_ge(y_added, m - 2)
                    if i >= 2:
                        pe.wait_ge(qk_cut, m * 4 + (i - 1))
                    for part in range(2):
                        last = pe.matmul(work[(i + 1) % 2][:, 0:SEQP], wgt[:, part, t * P:(t + 1) * P], xT[:],
                                         start=part == 0, stop=part == 1)
                    last.then_inc(projected, 1)

                def project_v(m):
                    pe.wait_ge(qk_cut, m * 4 + 3)
                    for tile, (at, n) in enumerate(TILES):
                        for part in range(2):
                            last = pe.matmul(work[1][0:n, tile * D:(tile + 1) * D], xT[:, at:at + n], wv[:, part],
                                             start=part == 0, stop=part == 1)
                    last.then_inc(v_made, 1)

                def weigh(m, par):
                    pe.wait_ge(exped, m * 2 + 2)
                    pe.wait_ge(v_set, m + 1)
                    if due(m):
                        pe.wait_ge(o_set, m)
                    for keys, (_, kn) in enumerate(TILES):
                        for h in range(A_HEADS):
                            t, j = h // A_HPT, h % A_HPT
                            last = pe.matmul(outT[32 * h:32 * h + A_DH + 1, 0:SEQP], V[0:kn, par, keys, h],
                                             PT[0:kn, keys, t, j * SEQP:(j + 1) * SEQP],
                                             start=keys == 0, stop=keys == 1)
                    last.then_inc(weighed, 1)

                def turn_outs(m):
                    pe.wait_ge(out_copied, m + 1)
                    for tile, (at, n) in enumerate(TILES):
                        last = pe.transpose(outT[0:n, SEQP + tile * P:SEQP + (tile + 1) * P], oU[:, at:at + n], ident[:])
                    last.then_inc(outs_turned, 1)

                def turn_max(m):
                    pe.wait_ge(max_set, m * 2 + 2)
                    for tile, (at, n) in enumerate(TILES):
                        for t in range(A_TENSORS):
                            last = pe.transpose(maxT[:, t, at:at + n], mpad[0:n, tile, t].bitcast(F32), ident[0:n, 0:n])
                    last.then_inc(max_turned, 1)

                def turn_o(m, par):
                    pe.wait_ge(o_set, m + 1)
                    if live(m + 2):
                        pe.wait_ge(qk_cut, m * 4 + 12)
                    elif due(m):
                        pe.wait_ge(oT_set, m)
                    for tile, (at, n) in enumerate(TILES):
                        last = pe.transpose(work[0][:].bitcast(BF16)[:, at:at + n], o_rows[0:n, par, tile],
                                            ident_bf[0:n, 0:n])
                    last.then_inc(o_turned, 1)

                def project_o(m):
                    pe.wait_ge(oT_set, m + 1)
                    if live(m + 2):
                        pe.wait_ge(v_set, m + 3)
                    else:
                        pe.wait_ge(y_added, m)
                    for tile, (at, n) in enumerate(TILES):
                        for part in range(2):
                            last = pe.matmul(work[1][0:n, tile * D:(tile + 1) * D], oT[:, at:at + n], wo[:, part],
                                             start=part == 0, stop=part == 1)
                    last.then_inc(y_made, 1)

                def step(n, par):
                    if live(n):
                        score_t(n, par, 0)
                    if live(n + 1):
                        score(n + 1, 1 - par, 0)
                    if live(n - 1):
                        turn_o(n - 1, 1 - par)
                    if live(n):
                        score_t(n, par, 1)
                    if live(n - 1):
                        project_o(n - 1)
                    if live(n + 2):
                        turn_x(n + 2)
                    if live(n + 1):
                        score(n + 1, 1 - par, 1)
                    if live(n + 2):
                        project(n + 2, 0)
                        project(n + 2, 1)
                    if live(n):
                        weigh(n, par)
                    if live(n + 1):
                        turn_max(n + 1)
                    if live(n + 2):
                        project(n + 2, 2)
                        project(n + 2, 3)
                    if live(n):
                        turn_outs(n)
                    if live(n + 2):
                        project_v(n + 2)

                each_step(pe, step)


class ExpertInputs:

    def __init__(self, p, wts):
        self.nc, self.wts = p.nc, wts
        halves = FF // P
        self.w1_raw = p.sb("ex_w1_raw", [P, FF])
        self.wd_raw = p.sb("ex_wd_raw", [P, halves, EXPERTS * D + EXPERTS])
        self.b_raw = p.sb("ex_b_raw", [33, EXPERTS * D])
        self.b1, self.bg = p.sb("ex_b1", [P, halves]), p.sb("ex_bg", [EXPERTS, 1])
        self.loaded = p.sem("ex_loaded")
        self.N = 2 + 3 * halves + 2 + 1

    def load(self, q):
        wts, wide = self.wts, EXPERTS * D
        for half in range(2):
            q.dma_start(self.w1_raw[half * D:(half + 1) * D], wts["W1"]).then_inc(self.loaded, 16)
        for half in range(FF // P):
            rows = slice(half * P, (half + 1) * P)
            q.dma_start(self.wd_raw[:, half, 0:wide].rearrange("p (e d) -> p e d", e=EXPERTS),
                        wts["Wd"][:, rows].rearrange("e i d -> i e d")).then_inc(self.loaded, 16)
            q.dma_start(self.wd_raw[:, half, wide:], wts["Wg"][rows]).then_inc(self.loaded, 16)
            with self.nc.allow_non_contiguous_dma(reason="bias as columns"):
                q.dma_start(self.b1[:, half:half + 1], wts["b1"][rows].rearrange("(n a) -> n a", a=1))\
                    .then_inc(self.loaded, 16)
        for r in (0, 32):
            q.dma_start(self.b_raw[r:r + 1], row(wts["bd"].rearrange("e d -> (e d)"))).then_inc(self.loaded, 16)
        with self.nc.allow_non_contiguous_dma(reason="bias as a column"):
            q.dma_start(self.bg[:], wts["bg"].rearrange("(n a) -> n a", a=1)).then_inc(self.loaded, 16)


def experts(p, inputs, ident, rows_of, out):
    nc = p.nc
    HALVES = FF // P
    WIDE = EXPERTS * D
    G = 4

    with ExitStack() as ctx:
        def sb(name, shape, dtype=F32):
            return ctx.enter_context(nc.sbuf_tensor("ex_" + name, shape, dtype))

        def sem(name):
            return p.sem("ex_" + name)

        w1 = sb("w1", [P, 2, FF], F32R)
        wd = sb("wd", [P, 2, HALVES, WIDE + EXPERTS], F32R)
        b1, bg = inputs.b1, inputs.bg
        biases, ones = sb("biases", [33, WIDE], F32R), sb("ones", [33, P], F32R)
        rank, power = sb("rank", [P, EXPERTS]), sb("power", [P, 2])

        stats, mean_var = sb("stats", [P, 2, 6]), sb("mean_var", [P, 2, 2])
        var_eps, rstd = sb("var_eps", [P, 2]), sb("rstd", [P, 2])
        z = sb("z", [P, 2, D])
        xs = sb("xs", [P, 2, 2 * D], F32R)
        xT = sb("xT", [P, 2, SEQP], F32R)
        H = sb("H", [P, 2, HALVES, SEQP])
        H_hi = sb("H_hi", [P, 2 * G, HALVES, SEQP], F32R)
        H_lo = sb("H_lo", [P, 2 * G, HALVES, SEQP], F32R)
        logit_rows = sb("logit_rows", [EXPERTS, SEQP])
        top, less = sb("top", [P, 2 * G]), sb("less", [P, 2 * G, EXPERTS])
        e_less, e_sum = sb("e_less", [P, 2 * G, EXPERTS]), sb("e_sum", [P, 2 * G])
        prob = sb("prob", [P, 2 * G])
        first, chosen = sb("first", [P, 2 * G]), sb("chosen", [P, 2 * G, EXPERTS])
        gate = sb("gate", [P, 2 * G, EXPERTS])
        weighted = sb("weighted", [P, 2, EXPERTS, D])
        summed = sb("summed", [P, 2, D])

        turned_x = p.psum(ctx, "ex_turned_x", [P, 512])
        up_rows = p.psum(ctx, "ex_up", [P, HALVES, SEQP])
        logits = p.psum(ctx, "ex_logits", [P, 2 * G, EXPERTS])
        y = [p.psum(ctx, f"ex_y{k}", [P, EXPERTS, D]) for k in range(4)]

        with ExitStack() as setup:
            def tmp(name, shape, dtype=F32):
                return setup.enter_context(nc.sbuf_tensor("ex_" + name, shape, dtype))

            w1_raw, wd_raw, b_raw = inputs.w1_raw, inputs.wd_raw, inputs.b_raw
            b_hi = tmp("b_hi", [33, WIDE], F32R)
            cleared, w_hi = sem("cleared"), sem("w_hi")

            with nc.Block() as block:
                @block.gpsimd
                def _(pool):
                    pool.memset(biases[:].bitcast(F32), 0.0).then_inc(cleared, 1)
                    pool.memset(ones[:].bitcast(F32), 1.0)
                    pool.memset(power[:], -0.5)
                    pool.memset(xT[:].bitcast(F32), 0.0)
                    pool.memset(z[:], 0.0)
                    pool.memset(mean_var[:], 0.0)
                    for e in range(EXPERTS):
                        pool.memset(rank[:, e:e + 1], float(EXPERTS - e))

                @block.vector
                def _(dve):
                    dve.memset(logits[:], 0.0)
                    dve.wait_ge(inputs.loaded, inputs.N * 16)
                    dve.tensor_copy(w1[:, 0], w1_raw[:]).then_inc(w_hi, 1)
                    dve.tensor_copy(wd[:, 0], wd_raw[:]).then_inc(w_hi, 1)
                    dve.tensor_copy(b_hi[:], b_raw[:]).then_inc(w_hi, 1)
                    dve.wait_ge(w_hi, 3)
                    dve.tensor_tensor(w1[:, 1], w1_raw[:], w1[:, 0].bitcast(F32), ALU.subtract)
                    dve.tensor_tensor(wd[:, 1], wd_raw[:], wd[:, 0].bitcast(F32), ALU.subtract)
                    dve.wait_ge(cleared, 1)
                    dve.tensor_copy(biases[0:1], b_hi[0:1].bitcast(F32))
                    dve.tensor_tensor(biases[32:33], b_raw[32:33], b_hi[32:33].bitcast(F32), ALU.subtract)

        aggregated, var_ready, rstd_ready, z_ready, x_hi, x_cut, x_turned, xT_set = (
            sem("aggregated"), sem("var_ready"), sem("rstd_ready"), sem("z_ready"), sem("x_hi"),
            sem("x_cut"), sem("x_turned"), sem("xT_set"))
        up_done, gelu_done, h_hi, h_cut = sem("up_done"), sem("gelu_done"), sem("h_hi"), sem("h_cut")
        logits_made, logits_copied = sem("logits_made"), sem("logits_copied")
        gated, gate_step, gate_exp, gate_sum, gate_set = (
            sem("gated"), sem("gate_step"), sem("gate_exp"), sem("gate_sum"), sem("gate_set"))
        y_made, y_weighted, y_summed, added, stored = (
            sem("y_made"), sem("y_weighted"), sem("y_summed"), sem("added"), sem("stored"))
        GATE_STEPS = 6

        def each_step(eng, step):
            for n in range(-7, 8):
                step(n, n % 8)
            with eng.Fori(1, B // 8 - 1) as i:
                for k in range(8):
                    step(i * 8 + k, k)
            for n in range(B - 8, B):
                step(n, n % 8)

        with nc.Block() as block:
            @block.sync
            def _(sp):
                def step(n, k):
                    if k % 2 == 1 and live(n):
                        sp.wait_ge(added, n * 2 + 2)
                        for tile, (at, rows) in enumerate(TILES):
                            sp.dma_start(out[bass.ds(n - 1, 2), at:at + rows].rearrange("b s d -> s b d"),
                                         rows_of(n - 1, tile, 2)).then_inc(stored, 16)

                each_step(sp, step)
                sp.wait_ge(stored, B * 16)

            @block.vector
            def _(dve):
                def choose(q):
                    wide = [P, 2 * G, EXPERTS]
                    base = q * GATE_STEPS
                    dve.wait_ge(gated, q * G + G)
                    dve.tensor_reduce(top[:], logits[:], AX.X, ALU.max).then_inc(gate_step, 1)
                    dve.wait_ge(gate_step, base + 1)
                    dve.tensor_tensor(less[:], logits[:], top[:].unsqueeze(2).broadcast_to(wide), ALU.subtract)\
                        .then_inc(gate_sum, 1)
                    dve.wait_ge(gate_sum, q + 1)
                    dve.scalar_tensor_tensor(out=chosen[:], in0=less[:], scalar=0.0,
                                             in1=rank[:].unsqueeze(1).broadcast_to(wide), op0=ALU.is_ge, op1=ALU.mult)\
                        .then_inc(gate_step, 1)
                    dve.wait_ge(gate_step, base + 2)
                    dve.tensor_reduce(first[:], chosen[:], AX.X, ALU.max).then_inc(gate_step, 1)
                    dve.wait_ge(gate_exp, q + 1)
                    dve.tensor_reduce(e_sum[:], e_less[:], AX.X, ALU.add).then_inc(gate_step, 1)
                    dve.wait_ge(gate_step, base + 4)
                    dve.reciprocal(prob[:], e_sum[:]).then_inc(gate_step, 1)
                    dve.tensor_tensor(chosen[:], chosen[:], first[:].unsqueeze(2).broadcast_to(wide), ALU.is_equal)\
                        .then_inc(gate_step, 1)
                    dve.wait_ge(gate_step, base + 6)
                    dve.tensor_tensor(gate[:], chosen[:], prob[:].unsqueeze(2).broadcast_to(wide), ALU.mult)\
                        .then_inc(gate_set, 1)
                    dve.wait_ge(gate_set, q + 1)

                def combine(m, b, par, tile):
                    n = TILES[tile][1]
                    dve.wait_ge(y_made, m * 2 + (tile + 1))
                    dve.tensor_tensor(weighted[0:n, tile], y[2 * par + tile][0:n],
                                      gate[0:n, 2 * b + tile].unsqueeze(2).broadcast_to([n, EXPERTS, D]), ALU.mult)\
                        .then_inc(y_weighted, 1)
                    dve.wait_ge(y_weighted, m * 2 + (tile + 1))
                    dve.tensor_reduce(summed[0:n, tile], weighted[0:n, tile].rearrange("p e d -> p d e"), AX.X, ALU.add)\
                        .then_inc(y_summed, 1)
                    dve.wait_ge(y_summed, m * 2 + (tile + 1))
                    dve.tensor_tensor(rows_of(m, tile), rows_of(m, tile), summed[0:n, tile], ALU.add).then_inc(added, 1)

                def step(n, k):
                    b, par = k % G, k % 2
                    if live(n + 7):
                        set_stats(dve, rows_of, mean_var, stats, var_eps, aggregated, var_ready, n + 7)
                    if live(n):
                        combine(n, b, par, 0)
                    if live(n + 7):
                        m = n + 7
                        dve.wait_ge(rstd_ready, m + 1)
                        if due(m):
                            dve.wait_ge(x_cut, m)
                        for tile, (_, rows) in enumerate(TILES):
                            last = dve.tensor_scalar(z[0:rows, tile], rows_of(m, tile), mean_var[0:rows, tile, 0:1],
                                                     rstd[0:rows, tile:tile + 1], ALU.subtract, ALU.mult)
                        last.then_inc(z_ready, 1)
                    if live(n):
                        combine(n, b, par, 1)
                    if b == G - 1 and live(n + 4):
                        choose((n + 4 - b) // G if isinstance(n, int) else q_of(n, k))

                def q_of(n, k):
                    return QREG[0] * 2 + (k // G + 1)

                QREG = [None]
                for n in range(-7, 8):
                    step(n, n % 8)
                with dve.Fori(1, B // 8 - 1) as i:
                    QREG[0] = i
                    for k in range(8):
                        step(i * 8 + k, k)
                for n in range(B - 8, B):
                    step(n, n % 8)

            @block.gpsimd
            def _(pool):
                def step(n, k):
                    if live(n + 7):
                        pool.wait_ge(var_ready, n + 8)
                        pool.tensor_tensor(rstd[:], var_eps[:], power[:], ALU.pow).then_inc(rstd_ready, 1)
                    if live(n + 5):
                        m, slot = n + 5, (k + 5) % 8
                        pool.wait_ge(h_hi, m + 1)
                        pool.tensor_tensor(H_lo[:, slot], H[:, slot % 2], H_hi[:, slot].bitcast(F32), ALU.subtract)\
                            .then_inc(h_cut, 1)
                    if live(n + 7):
                        pool.wait_ge(x_hi, n + 8)
                        pool.tensor_tensor(xs[:, :, D:], z[:], xs[:, :, 0:D].bitcast(F32), ALU.subtract)\
                            .then_inc(x_cut, 1)

                each_step(pool, step)

            @block.scalar
            def _(act):
                def step(n, k, q):
                    if live(n + 4):
                        m = n + 4
                        act.wait_ge(logits_made, m + 1)
                        if due(m):
                            act.wait_ge(gated, m)
                        act.activation(logit_rows[:], turned_x[0:EXPERTS, P * 2:P * 2 + SEQP], ACT.Identity, bias=bg[:])\
                            .then_inc(logits_copied, 1)
                    if live(n + 5):
                        m, slot = n + 5, (k + 5) % 8
                        act.wait_ge(up_done, m + 1)
                        if due(m - 1):
                            act.wait_ge(h_cut, m - 1)
                        for half in range(HALVES):
                            last = act.activation(H[:, slot % 2, half], up_rows[:, half], ACT.Gelu,
                                                  bias=b1[:, half:half + 1])
                        last.then_inc(gelu_done, 1)
                        act.wait_ge(gelu_done, m + 1)
                        if due(m * 2 - 14):
                            act.wait_ge(y_made, m * 2 - 14)
                        act.activation(H_hi[:, slot], H[:, slot % 2], ACT.Copy).then_inc(h_hi, 1)
                    if live(n + 6):
                        m = n + 6
                        act.wait_ge(x_turned, m + 1)
                        if due(m - 1):
                            act.wait_ge(up_done, m - 1)
                        act.activation(xT[:, (k + 6) % 2, 0:SEQ], turned_x[:, 0:SEQ], ACT.Copy).then_inc(xT_set, 1)
                    if live(n + 7):
                        m = n + 7
                        act.wait_ge(z_ready, m + 1)
                        if due(m):
                            act.wait_ge(x_turned, m)
                        act.activation(xs[:, :, 0:D], z[:], ACT.Copy).then_inc(x_hi, 1)
                    if k % G == G - 1 and live(n + 4):
                        act.wait_ge(gate_sum, q + 1)
                        act.activation(e_less[:], less[:], ACT.Exp).then_inc(gate_exp, 1)

                for n in range(-7, 8):
                    step(n, n % 8, (n + 4) // G)
                with act.Fori(1, B // 8 - 1) as i:
                    for k in range(8):
                        step(i * 8 + k, k, i * 2 + (k // G + 1))
                for n in range(B - 8, B):
                    step(n, n % 8, (n + 4) // G)

            @block.tensor
            def _(pe):
                def run_experts(m, slot, par, tile):
                    at, n = TILES[tile]
                    if due(m * 2 - 3 + tile):
                        pe.wait_ge(y_weighted, m * 2 - 3 + tile)
                    acc = y[2 * par + tile][0:n].rearrange("p e d -> p (e d)")
                    pe.matmul(acc, ones[:, 0:n], biases[:], start=True, stop=False)
                    for half in range(HALVES):
                        for h, part in ((H_hi, 0), (H_hi, 1), (H_lo, 0)):
                            last = pe.matmul(acc, h[:, slot, half, at:at + n], wd[:, part, half, 0:WIDE],
                                             start=False, stop=half == HALVES - 1 and h is H_lo)
                    last.then_inc(y_made, 1)

                def step(n, k, q):
                    if live(n + 5):
                        m = n + 5
                        pe.wait_ge(xT_set, m + 1)
                        if due(m):
                            pe.wait_ge(gelu_done, m)
                        for half in range(HALVES):
                            for part in range(2):
                                last = pe.matmul(up_rows[:, half], w1[:, part, half * P:(half + 1) * P],
                                                 xT[:, (k + 5) % 2], start=part == 0, stop=part == 1)
                        last.then_inc(up_done, 1)
                    if live(n):
                        run_experts(n, k, k % 2, 0)
                    if live(n + 4):
                        m, b = n + 4, k % G
                        pe.wait_ge(logits_copied, m + 1)
                        if b == 0 and due(q):
                            pe.wait_ge(gate_sum, q)
                    if live(n + 6):
                        m = n + 6
                        pe.wait_ge(x_cut, m + 1)
                        if due(m):
                            pe.wait_ge(xT_set, m)
                        if due(m - 1):
                            pe.wait_ge(logits_copied, m - 1)
                        for tile, (at, rows) in enumerate(TILES):
                            last = pe.transpose(turned_x[:, at:at + rows], xs[0:rows, tile].bitcast(F32),
                                                ident[0:rows, 0:rows])
                        last.then_inc(x_turned, 1)
                    if live(n + 4):
                        for tile, (at, rows) in enumerate(TILES):
                            last = pe.transpose(logits[0:rows, 2 * b + tile], logit_rows[:, at:at + rows],
                                                ident[0:EXPERTS, 0:EXPERTS])
                        last.then_inc(gated, 1)
                    if live(n):
                        run_experts(n, k, k % 2, 1)
                    if live(n + 5):
                        m, slot = n + 5, (k + 5) % 8
                        pe.wait_ge(h_cut, m + 1)
                        if live(m + 1):
                            pe.wait_ge(xT_set, m + 2)
                        acc = turned_x[0:EXPERTS, P * 2:P * 2 + SEQP]
                        for half in range(HALVES):
                            for h, part in ((H_hi, 0), (H_hi, 1), (H_lo, 0)):
                                last = pe.matmul(acc, wd[:, part, half, WIDE:], h[:, slot, half],
                                                 start=half == 0 and part == 0 and h is H_hi,
                                                 stop=half == HALVES - 1 and h is H_lo)
                        last.then_inc(logits_made, 1)

                for n in range(-7, 8):
                    step(n, n % 8, (n + 4) // G)
                with pe.Fori(1, B // 8 - 1) as i:
                    for k in range(8):
                        step(i * 8 + k, k, i * 2 + (k // G + 1))
                for n in range(B - 8, B):
                    step(n, n % 8, (n + 4) // G)



IMAGE_WEIGHTS = ("ln0_g", "ln0_b", "ln1_g", "ln1_b", "conv1_w", "conv1_b", "conv2_w", "conv2_b", "conv3_w",
                 "conv3_b", "out_w", "out_b")
TEXT_WEIGHTS = ("emb", "Wq", "bq", "Wv", "bv", "Wo", "bo", "W1", "b1", "W2", "b2", "ln1_g", "ln1_b", "ln2_g",
                "ln2_b", "fin_g", "fin_b")
ATTENTION_WEIGHTS = ("Wq", "bq", "Wk", "bk", "Wv", "bv", "Wo", "bo")
EXPERT_WEIGHTS = ("W1", "b1", "Wg", "bg", "Wd", "bd")


def early_fusion_embed(nc, x, x_txt, pos, weights, out):
    def of(prefix, names):
        return {name: weights[prefix + name] for name in names}

    with ExitStack() as ctx:
        p = Program(nc, ctx, B)
        ident = p.sb("ident", [P, P])
        h_img, h_txt = p.sb("h_img", [T, B, LAT]), p.sb("h_txt", [S_TXT, B, D])

        def rows_of(n, tile, count=None):
            h = h_txt if tile else h_img
            v = h[:, bass.ds(n, count or 1)]
            return v if count else v.rearrange("p a d -> p (a d)")

        text = TextInputs(p, x_txt, pos, of("L0_txt_", TEXT_WEIGHTS))
        attention = AttentionInputs(p, of("L0_attn_", ATTENTION_WEIGHTS))
        expert = ExpertInputs(p, of("L0_ffn_", EXPERT_WEIGHTS))
        constants(p, ident, [text.cols_all, attention.cols, expert.b_raw])
        image_branch(p, x, of("L0_tok_", IMAGE_WEIGHTS), ident, h_img, [text, attention, expert])
        text_branch(p, text, ident, h_txt)
        fusion_attention(p, attention, ident, rows_of)
        experts(p, expert, ident, rows_of, out)


def positional_table():
    at = np.arange(S_TXT, dtype=np.float32)[:, None]
    freq = np.exp(np.arange(0, D, 2, dtype=np.float32) * np.float32(-np.log(10000.0) / D))
    table = np.zeros((S_TXT, D), np.float32)
    table[:, 0::2], table[:, 1::2] = np.sin(at * freq), np.cos(at * freq)
    return table


def kernel(**inputs):
    import concourse.bacc as _bacc
    from concourse import mybir as _mybir
    from concourse.bass_utils import run_bass_kernel_spmd as _run

    nc = _bacc.Bacc("TRN2", target_bir_lowering=False, num_devices=1)
    arrays = {name: np.ascontiguousarray(a) for name, a in inputs.items()}
    arrays["pos"] = positional_table()
    dram = {name: nc.dram_tensor(name, a.shape, _mybir.dt.from_np(a.dtype), kind="ExternalInput").ap()
            for name, a in arrays.items()}
    out = nc.dram_tensor("out", (B, T + S_TXT, D), F32, kind="ExternalOutput").ap()
    weights = {name: ap for name, ap in dram.items() if name.startswith("L0_")}
    early_fusion_embed(nc, dram["x"], dram["x_txt"], dram["pos"], weights, out)
    r = _run(nc, [arrays], core_ids=[0])
    return r.results[0]["out"]
```

```python
from contextlib import ExitStack

import numpy as np

import concourse.bass as bass
from concourse import mybir

F32 = mybir.dt.float32
F32R = mybir.dt.float32r
BF16 = mybir.dt.bfloat16
I32 = mybir.dt.int32
ALU = mybir.AluOpType
ACT = mybir.ActivationFunctionType
AX = mybir.AxisListType

P = 128
EPS = 1e-5
B = 64
T, J, LAT = 128, 64, 64
QUAD = 4
JP = J + 4


class Count:

    def __init__(self, base):
        self.base, self.k = base, 0

    def up(self, by=1):
        self.k += by
        return self.base + self.k


class Program:

    def __init__(self, nc, ctx, samples):
        self.nc, self.ctx, self.samples = nc, ctx, samples
        self.quads = samples // QUAD

    def sb(self, name, shape, dtype=F32):
        return self.ctx.enter_context(self.nc.sbuf_tensor(name, shape, dtype))

    def psum(self, ctx, name, shape, dtype=F32):
        return ctx.enter_context(self.nc.psum_tensor(name, shape, dtype))

    def sem(self, name):
        return self.ctx.enter_context(self.nc.semaphore(name))


def row(ap):
    return ap.rearrange("(a n) -> a n", a=1)


def on_all_rows(ap, rows=P):
    return row(ap).broadcast_to([rows, ap.shape[0]])



def image_branch(p, x, wts, ident, h_img, later_loads):
    nc = p.nc
    TAPS = (15, 10, 10)
    KD = (3, 2, 2)
    COLS = (3, 3, 2, 1)
    OUT_HALVES = (1, 1, 2)

    with ExitStack() as ctx:
        def sb(name, shape, dtype=F32):
            return ctx.enter_context(nc.sbuf_tensor(name, shape, dtype))

        def sem(name):
            return p.sem("im_" + name)

        w = [sb(f"im_w{c}", [P, TAPS[c] * OUT_HALVES[c], 2, P], F32R) for c in range(3)]
        bias = [sb(f"im_bias{c}", [P, OUT_HALVES[c]]) for c in range(3)]
        g0_jd, b0_jd = sb("im_g0_jd", [P, 3 * J]), sb("im_b0_jd", [P, 3 * J])
        g0, b0 = sb("im_g0", [P, 3 * J]), sb("im_b0", [P, 3 * J])
        g1_jd, b1_jd = sb("im_g1_jd", [P, 2 * J]), sb("im_b1_jd", [P, 2 * J])
        g1, b1 = sb("im_g1", [P, 2 * J]), sb("im_b1", [P, 2 * J])
        g1_col, b1_col = sb("im_g1_col", [P, 1]), sb("im_b1_col", [P, 1])
        w_out, bias_out = sb("im_w_out", [P, LAT]), sb("im_bias_out", [P, LAT])

        loaded = [sem(f"w_loaded{c}") for c in range(3)]
        small_loaded, zeroed = sem("small_loaded"), sem("zeroed")
        turned, hi_cut, lo_cut = sem("w_turned"), sem("w_hi_cut"), sem("w_lo_cut")

        a_hi = [sb(f"im_a_hi{c}", [P, (2 if c == 0 else 1), QUAD, COLS[c], JP], F32R) for c in range(3)]
        a_lo = [sb(f"im_a_lo{c}", [P, (2 if c == 0 else 1), QUAD, COLS[c], JP], F32R) for c in range(3)]

        with ExitStack() as setup:
            raw = [setup.enter_context(nc.sbuf_tensor(f"im_raw{c}", [P, OUT_HALVES[c], P * TAPS[c]], F32))
                   for c in range(3)]
            turn = [p.psum(setup, f"im_turn{k}", [P, 4, P]) for k in range(4)]
            jobs = [(c, t, h) for c in range(3) for h in range(OUT_HALVES[c]) for t in range(TAPS[c])]
            packs = [[q for q in jobs if q[0] == c] for c in range(3)]
            packs = [q[k:k + 4] for q in packs for k in range(0, len(q), 4)]

            with nc.Block() as block:
                @block.sync
                def _(sp):
                    for c in range(3):
                        sp.dma_start(raw[c][:], wts[f"conv{c + 1}_w"].rearrange("(h o) i a b -> o h (i a b)", o=P))\
                            .then_inc(loaded[c], 16)
                    with nc.allow_non_contiguous_dma(reason="biases and gains as columns"):
                        for c in range(3):
                            sp.dma_start(bias[c][:], wts[f"conv{c + 1}_b"].rearrange("(h o) -> o h", o=P))\
                                .then_inc(small_loaded, 16)
                        sp.dma_start(g1_col[:], wts["ln1_g"].rearrange("(n a) -> n a", a=1)).then_inc(small_loaded, 16)
                        sp.dma_start(b1_col[:], wts["ln1_b"].rearrange("(n a) -> n a", a=1)).then_inc(small_loaded, 16)
                    sp.dma_start(g0_jd[:], on_all_rows(wts["ln0_g"])).then_inc(small_loaded, 16)
                    sp.dma_start(b0_jd[:], on_all_rows(wts["ln0_b"])).then_inc(small_loaded, 16)
                    sp.dma_start(g1_jd[:], on_all_rows(wts["ln1_g"])).then_inc(small_loaded, 16)
                    sp.dma_start(b1_jd[:], on_all_rows(wts["ln1_b"])).then_inc(small_loaded, 16)
                    sp.dma_start(w_out[:], wts["out_w"]).then_inc(small_loaded, 16)
                    sp.dma_start(bias_out[:], on_all_rows(wts["out_b"])).then_inc(small_loaded, 16)

                @block.gpsimd
                def _(pool):
                    for c in range(3):
                        pool.memset(a_hi[c][:].bitcast(F32), 0.0).then_inc(zeroed, 1)
                        pool.memset(a_lo[c][:].bitcast(F32), 0.0).then_inc(zeroed, 1)

                @block.tensor
                def _(pe):
                    for n, pack in enumerate(packs):
                        c = pack[0][0]
                        pe.wait_ge(loaded[c], 16)
                        if n >= 4:
                            pe.wait_ge(lo_cut, n - 3)
                        for k, (c, t, h) in enumerate(pack):
                            src = raw[c][:, h].rearrange("o (i t) -> o t i", t=TAPS[c])[:, t]
                            last = pe.transpose(turn[n % 4][:, k], src, ident[:])
                        last.then_inc(turned, 1)

                def slots(n):
                    c, t, h = packs[n][0]
                    k = h * TAPS[c] + t
                    return w[c], k, len(packs[n])

                @block.scalar
                def _(act):
                    for n in range(len(packs)):
                        dst, k, m = slots(n)
                        act.wait_ge(turned, n + 1)
                        act.activation(dst[:, k:k + m, 0], turn[n % 4][:, 0:m], ACT.Copy).then_inc(hi_cut, 1)

                @block.vector
                def _(dve):
                    for n in range(len(packs)):
                        dst, k, m = slots(n)
                        dve.wait_ge(hi_cut, n + 1)
                        dve.tensor_tensor(dst[:, k:k + m, 1], turn[n % 4][:, 0:m], dst[:, k:k + m, 0].bitcast(F32),
                                          ALU.subtract).then_inc(lo_cut, 1)
                    dve.wait_ge(small_loaded, 11 * 16)
                    for dst, src in ((g0, g0_jd), (b0, b0_jd)):
                        dve.tensor_copy(dst[:].rearrange("p (d j) -> p d j", d=3),
                                        src[:].rearrange("p (j d) -> p d j", d=3))
                    for dst, src in ((g1, g1_jd), (b1, b1_jd)):
                        dve.tensor_copy(dst[:].rearrange("p (d j) -> p d j", d=2),
                                        src[:].rearrange("p (j d) -> p d j", d=2))

        xin = sb("im_x", [P, 2, QUAD, 3 * J])
        act_out = [sb("im_h1", [P, QUAD, 3 * J]), sb("im_h2", [P, QUAD, 2 * J]), sb("im_h3", [P, QUAD, 2 * J])]
        scaled, normed = sb("im_scaled", [P, QUAD, 3 * J]), sb("im_normed", [P, QUAD, 3 * J])
        stats, mean_var = sb("im_stats", [P, QUAD, 6]), sb("im_mean_var", [P, QUAD, 2])
        var_eps, rstd = sb("im_var_eps", [P, QUAD]), sb("im_rstd", [P, QUAD])
        power = sb("im_power", [P, QUAD])
        res = sb("im_res", [P, QUAD, P])
        res_t = sb("im_res_t", [P, QUAD, P])
        c1 = [p.psum(ctx, f"im_c1{k}", [P, 2, 3, J]) for k in range(2)]
        c2 = p.psum(ctx, "im_c2", [P, QUAD, 2, J])
        c3 = p.psum(ctx, "im_c3", [P, 2, QUAD, J])
        turned_res = p.psum(ctx, "im_turned_res", [P, QUAD, P])
        out_rows = p.psum(ctx, "im_out_rows", [P, QUAD, LAT])

        x_loaded = [sem("x_loaded0"), sem("x_loaded1")]
        power_set = sem("power_set")
        dve_step = sem("dve_step")
        var_ready, rstd_ready = sem("var_ready"), sem("rstd_ready")
        normed_ready, hi_ready, lo_ready = sem("normed_ready"), sem("hi_ready"), sem("lo_ready")
        conv_done = [sem(f"conv{c}_done") for c in range(3)]
        relu_done = [sem(f"relu{c}_done") for c in range(3)]
        res_ready, res_turned, res_scaled, out_done, rows_stored = (
            sem("res_ready"), sem("res_turned"), sem("res_scaled"), sem("out_done"), sem("rows_stored"))

        U = p.quads
        assert U % 2 == 0 and U >= 4

        def each_quad(eng, before, step):
            before()
            step(0, 0, True, False)
            step(1, 1, False, False)
            if U > 4:
                with eng.Fori(1, U // 2 - 1) as i:
                    step(i * 2, 0, False, False)
                    step(i * 2 + 1, 1, False, False)
            step(U - 2, 0, False, False)
            step(U - 1, 1, False, True)

        STATS = QUAD
        FULL = STATS + QUAD
        TURN = 3 * FULL + STATS

        def cuts_before(n):
            return n * 3 + 1

        def norms_before(n, first):
            return 1 if first else n * 4

        def steps_before(n, first):
            return FULL if first else n * TURN + (FULL - STATS)

        with nc.Block() as block:
            @block.sync
            def _(sp):
                def load(n, par):
                    sp.dma_start(xin[:, par], x[bass.ds(n * QUAD, QUAD)].rearrange("b t j d -> t b (j d)"))\
                        .then_inc(x_loaded[par], 16)

                def step(n, par, first, last):
                    if not last:
                        if not first:
                            sp.wait_ge(normed_ready, (n * 3 - 2) * QUAD)
                        load(n + 1, 1 - par)
                    if first:
                        for inputs in later_loads:
                            inputs.load(sp)

                each_quad(sp, lambda: load(0, 0), step)

            @block.vector
            def _(dve):
                def statistics(src, c, half_ready=None):
                    for b in range(QUAD):
                        if half_ready and b % 2 == 0:
                            dve.wait_ge(half_ready[0], half_ready[1] + b // 2)
                        dve.bn_stats(stats[:, b], src[:, b])
                    dve.drain()
                    for b in range(QUAD):
                        dve.bn_aggr(mean_var[:, b], stats[:, b]).then_inc(dve_step, 1)
                    dve.wait_ge(dve_step, c.up(QUAD))
                    dve.tensor_scalar(var_eps[:], mean_var[:, :, 1], EPS, None, ALU.add).then_inc(var_ready, 1)

                def normalise(src, size, gain, shift, c, norms, cuts, first=False, by_column=False,
                              half_ready=None):
                    statistics(src, c, half_ready)
                    for b in range(QUAD):
                        img, to, by = src[:, b], scaled[:, b, 0:size], gain[:]
                        if by_column:
                            img = img.rearrange("p (j d) -> p d j", d=3)
                            to, by = (v.rearrange("p (d j) -> p d j", d=3) for v in (to, by))
                        dve.scalar_tensor_tensor(out=to, in0=img, scalar=mean_var[:, b, 0:1], in1=by,
                                                 op0=ALU.subtract, op1=ALU.mult).then_inc(dve_step, 1)
                    dve.wait_ge(dve_step, c.up(QUAD))
                    dve.wait_ge(rstd_ready, norms.up())
                    if not first:
                        dve.wait_ge(lo_ready, cuts.up() - 1)
                    for b in range(QUAD):
                        dve.scalar_tensor_tensor(out=normed[:, b, 0:size], in0=scaled[:, b, 0:size],
                                                 scalar=rstd[:, b:b + 1], in1=shift[:],
                                                 op0=ALU.mult, op1=ALU.add).then_inc(normed_ready, 1)

                def last_norm(c, norms):
                    statistics(act_out[2], c)
                    dve.wait_ge(rstd_ready, norms.up())
                    for b in range(QUAD):
                        last = dve.tensor_scalar(res[:, b], act_out[2][:, b], mean_var[:, b, 0:1], rstd[:, b:b + 1],
                                                 ALU.subtract, ALU.mult)
                    last.then_inc(res_ready, 1)

                def store_rows(n):
                    dve.wait_ge(out_done, n + 1)
                    dve.tensor_tensor(h_img[:, bass.ds(n * QUAD, QUAD)], out_rows[:],
                                      bias_out[:].unsqueeze(1).broadcast_to([P, QUAD, LAT]), ALU.add)\
                        .then_inc(rows_stored, 1)

                def first_norm(n, par, c, norms, cuts, first=False):
                    dve.wait_ge(x_loaded[par], (n - par) * 8 + 16)
                    normalise(xin[:, par], 3 * J, g0, b0, c, norms, cuts, first, by_column=True)

                def before():
                    dve.memset(power[:], -0.5).then_inc(power_set, 1)
                    c = Count(0)
                    first_norm(0, 0, c, Count(0), Count(0), True)
                    assert c.k == FULL

                def step(n, par, first, last):
                    c, norms, cuts = Count(steps_before(n, first)), Count(norms_before(n, first)), Count(cuts_before(n))
                    if not last:
                        first_norm(n + 1, 1 - par, c, norms, cuts)
                    if not isinstance(n, int) or n > 1:
                        store_rows(n - 2)
                    normalise(act_out[0], 3 * J, g0, b0, c, norms, cuts, half_ready=(relu_done[0], n * 2 + 1))
                    if not first:
                        dve.wait_ge(relu_done[2], n)
                        last_norm(c, norms)
                    dve.wait_ge(relu_done[1], n + 1)
                    normalise(act_out[1], 2 * J, g1, b1, c, norms, cuts)
                    if last:
                        store_rows(n - 1)
                        dve.wait_ge(relu_done[2], n + 1)
                        last_norm(c, norms)
                        store_rows(n)
                    else:
                        assert c.k == (TURN - STATS if first else TURN)

                each_quad(dve, before, step)

            @block.gpsimd
            def _(pool):
                def rstd_of(norms):
                    pool.wait_ge(var_ready, norms.up())
                    pool.tensor_tensor(rstd[:], var_eps[:], power[:], ALU.pow).then_inc(rstd_ready, 1)

                def lo_of(c, par, cuts):
                    cols = COLS[c]
                    sample = (cuts.up() - 1) * QUAD
                    for b in range(QUAD):
                        pool.wait_ge(hi_ready, sample + (b + 1))
                        last = pool.tensor_tensor(
                            a_lo[c][:, par, b, :, 2:2 + J],
                            normed[:, b, 0:cols * J].rearrange("p (d j) -> p d j", d=cols),
                            a_hi[c][:, par, b, :, 2:2 + J].bitcast(F32), ALU.subtract)
                    last.then_inc(lo_ready, 1)

                def before():
                    pool.wait_ge(power_set, 1)
                    rstd_of(Count(0))
                    lo_of(0, 0, Count(0))

                def step(n, par, first, last):
                    norms, cuts = Count(norms_before(n, first)), Count(cuts_before(n))
                    if not last:
                        rstd_of(norms)
                        lo_of(0, 1 - par, cuts)
                    rstd_of(norms)
                    lo_of(1, 0, cuts)
                    if not first:
                        rstd_of(norms)
                    rstd_of(norms)
                    lo_of(2, 0, cuts)
                    if last:
                        rstd_of(norms)

                each_quad(pool, before, step)

            @block.scalar
            def _(act):
                def hi_of(c, par, cuts):
                    cols = COLS[c]
                    sample = (cuts.up() - 1) * QUAD
                    for b in range(QUAD):
                        act.wait_ge(normed_ready, sample + (b + 1))
                        act.activation(a_hi[c][:, par, b, :, 2:2 + J],
                                       normed[:, b, 0:cols * J].rearrange("p (d j) -> p d j", d=cols), ACT.Copy)\
                            .then_inc(hi_ready, 1)

                def relu(c, n):
                    if c == 0:
                        for k in range(2):
                            act.wait_ge(conv_done[0], n * 2 + k + 1)
                            act.activation(act_out[0][:, 2 * k:2 * k + 2], c1[k][:].rearrange("p b d j -> p b (d j)"),
                                           ACT.Relu, bias=bias[0][:, 0:1]).then_inc(relu_done[0], 1)
                    elif c == 1:
                        act.wait_ge(conv_done[1], n + 1)
                        act.activation(act_out[1][:], c2[:].rearrange("p b d j -> p b (d j)"), ACT.Relu,
                                       bias=bias[1][:, 0:1]).then_inc(relu_done[1], 1)
                    else:
                        act.wait_ge(conv_done[2], n + 1)
                        for half in range(2):
                            last = act.activation(act_out[2][:, :, half * J:half * J + J], c3[:, half], ACT.Relu,
                                                  bias=bias[2][:, half:half + 1])
                        last.then_inc(relu_done[2], 1)

                def scale_res(n):
                    act.wait_ge(res_turned, n + 1)
                    if not isinstance(n, int) or n > 0:
                        act.wait_ge(out_done, n)
                    act.activation(res_t[:], turned_res[:], ACT.Identity, bias=b1_col[:], scale=g1_col[:])\
                        .then_inc(res_scaled, 1)

                def step(n, par, first, last):
                    cuts = Count(cuts_before(n))
                    if not last:
                        hi_of(0, 1 - par, cuts)
                    relu(0, n)
                    hi_of(1, 0, cuts)
                    if not first:
                        relu(2, n - 1)
                    relu(1, n)
                    if not first:
                        scale_res(n - 1)
                    hi_of(2, 0, cuts)
                    if last:
                        relu(2, n)
                        scale_res(n)

                each_quad(act, lambda: hi_of(0, 0, Count(0)), step)

            @block.tensor
            def _(pe):
                def conv(c, par, cuts, n, between=None):
                    pe.wait_ge(lo_ready, cuts)
                    hi, lo = a_hi[c][:, par], a_lo[c][:, par]
                    halves = ((0, 2), (2, 4)) if c == 0 else ((0, 4),)
                    for k, (b0_, b1_) in enumerate(halves):
                        if k and between:
                            between()
                        for half in range(OUT_HALVES[c]):
                            acc = c1[k][:] if c == 0 else c2[:] if c == 1 else c3[:, half].unsqueeze(2)
                            taps = [(kj, kd) for kd in ((1, 0, 2) if c == 0 else range(2)) for kj in range(5)]
                            for kj, kd in taps:
                                shift = kd - 1 if c == 0 else kd
                                d0 = max(0, -shift) if c == 0 else 0
                                d1 = min(3, 3 - shift) if c == 0 else COLS[c + 1]
                                slot = half * TAPS[c] + kj * KD[c] + kd
                                for part, img in ((0, hi), (1, hi), (0, lo)):
                                    opens = (kj, kd) == taps[0] and part == 0 and img is hi
                                    closes = (kj, kd) == taps[-1] and img is lo
                                    last = pe.matmul(acc[:, :, d0:d1], w[c][:, slot, part],
                                                     img[:, b0_:b1_, d0 + shift:d1 + shift, kj:kj + J],
                                                     start=opens, stop=closes)
                        if c == 0:
                            last.then_inc(conv_done[0], 1)
                    if c:
                        last.then_inc(conv_done[c], 1)

                def turn_res(n):
                    pe.wait_ge(res_ready, n + 1)
                    for b in range(QUAD):
                        last = pe.transpose(turned_res[:, b], res[:, b], ident[:])
                    last.then_inc(res_turned, 1)

                def project(n):
                    pe.wait_ge(res_scaled, n + 1)
                    for b in range(QUAD):
                        last = pe.matmul(out_rows[:, b], res_t[:, b], w_out[:], start=True, stop=True)
                    last.then_inc(out_done, 1)

                def step(n, par, first, last):
                    cuts = cuts_before(n)
                    two_before = not isinstance(n, int) or n > 1
                    conv(0, par, 1 if first else n * 3 - 1, n, (lambda: project(n - 2)) if two_before else None)
                    if not first:
                        conv(2, 0, cuts, n - 1)
                    conv(1, 0, cuts + (1 if last else 2), n)
                    if not first:
                        turn_res(n - 1)
                    if last:
                        project(n - 1)
                        conv(2, 0, cuts + 2, n)
                        turn_res(n)
                        project(n)

                each_quad(pe, lambda: None, step)


def constants(p, ident, clear):
    nc = p.nc
    cleared, made = p.sem("ident_cleared"), p.sem("ident_made")
    with nc.Block() as block:
        @block.gpsimd
        def _(pool):
            for t in clear:
                pool.memset(t[:], 0.0)
            pool.memset(ident[:], 0.0).then_inc(cleared, 1)
            pool.wait_ge(cleared, 1)
            pool.affine_select(out=ident[:], in_=ident[:], compare_op=ALU.not_equal, fill=1.0, base=0,
                               pattern=[[-1, P]], channel_multiplier=1).then_inc(made, 1)
            pool.wait_ge(made, 1)



S_TXT = 77
SP_TXT = S_TXT + 1
D = 64
LAYERS, HEADS, FF, VOCAB = 4, 8, 256, 100
DH = D // HEADS

SEC = {}
_at = 0
for _name, _width in (("q", 2 * 2 * P), ("k", 2 * 2 * P), ("v", 2 * D), ("o", 2 * D), ("ff1", 2 * FF)):
    SEC[_name] = (_at, _at + _width)
    _at += _width
W_COLS = _at
W_ATT = SEC["ff1"][0]
ROWS_OF = ("bv", "bo", "ln1_g", "ln1_b", "b2", "ln2_g", "ln2_b")
GROUP = 32
HPT = P // GROUP
TENSORS = HEADS // HPT


def place_heads(dve, dst, src, head_dim, group, done):
    for copy in range(3):
        dve.tensor_copy(
            dst.rearrange("p l (j r) -> p l j r", r=group)[:, :, :, copy * head_dim:(copy + 1) * head_dim],
            src.rearrange("p l (j c) -> p l j c", c=head_dim)).then_inc(done, 1)


class TextInputs:

    def __init__(self, p, tokens, pos, wts):
        self.nc, self.wts, self.dram_tokens, self.dram_pos = p.nc, wts, tokens, pos

        def sb(name, shape, dtype=F32):
            return p.sb("tx_" + name, shape, dtype)

        self.raw = {m: sb("raw_" + m, [P, LAYERS, FF if m == "W1" else D]) for m in ("Wq", "Wv", "Wo", "W1")}
        self.w2_all = sb("w2_all", [P, LAYERS + 1, 2, D])
        self.rows_all = sb("rows_all", [S_TXT, LAYERS + 1, len(ROWS_OF), D])
        self.cols_all = sb("cols_all", [P, LAYERS + 1, 10])
        self.fin_g, self.fin_b = sb("fin_g", [S_TXT, D]), sb("fin_b", [S_TXT, D])
        self.toks = sb("toks", [VOCAB, p.samples * S_TXT], I32)
        self.emb, self.pos = sb("emb", [VOCAB, D]), sb("pos", [S_TXT, D])
        self.w_loaded, self.small_loaded, self.tok_loaded = p.sem("tx_w_loaded"), p.sem("tx_small_loaded"), p.sem("tx_tok_loaded")
        self.N_W = 2 * len(self.raw) + 1
        self.N_SMALL = len(ROWS_OF) + 2 + 2 + 2 * HEADS * 3
        self.N_TOK = 3

    def load(self, q):
        nc, wts = self.nc, self.wts
        q.dma_start(self.toks[:], self.dram_tokens.rearrange("(a b) t -> a (b t)", a=1)
                    .broadcast_to([VOCAB, self.toks.shape[1]])).then_inc(self.tok_loaded, 16)
        q.dma_start(self.emb[:], wts["emb"]).then_inc(self.tok_loaded, 16)
        q.dma_start(self.pos[:], self.dram_pos).then_inc(self.tok_loaded, 16)
        for m in self.raw:
            for half in range(2):
                q.dma_start(self.raw[m][half * D:(half + 1) * D], wts[m].rearrange("l i o -> i l o"))\
                    .then_inc(self.w_loaded, 16)
        q.dma_start(self.w2_all[:, 0:LAYERS], wts["W2"].rearrange("l (k i) o -> i l k o", i=P)).then_inc(self.w_loaded, 16)
        for k, m in enumerate(ROWS_OF):
            src = wts[m].rearrange("(a l) d -> a l d", a=1).broadcast_to([S_TXT, LAYERS, D])
            q.dma_start(self.rows_all[:, 0:LAYERS, k], src).then_inc(self.small_loaded, 16)
        q.dma_start(self.fin_g[:], on_all_rows(wts["fin_g"], S_TXT)).then_inc(self.small_loaded, 16)
        q.dma_start(self.fin_b[:], on_all_rows(wts["fin_b"], S_TXT)).then_inc(self.small_loaded, 16)
        with nc.allow_non_contiguous_dma(reason="biases as columns, beside the heads' rows"):
            for k in range(2):
                q.dma_start(self.cols_all[:, 0:LAYERS, 8 + k], wts["b1"][:, k * P:(k + 1) * P].rearrange("l i -> i l"))\
                    .then_inc(self.small_loaded, 16)
            for at, m in ((0, "bq"), (4, "bv")):
                for h in range(HEADS):
                    t, j = h // HPT, h % HPT
                    src = wts[m][:, h * DH:(h + 1) * DH].rearrange("l c -> c l")
                    for copy in range(3):
                        r = GROUP * j + DH * copy
                        q.dma_start(self.cols_all[r:r + DH, 0:LAYERS, at + t], src).then_inc(self.small_loaded, 16)


def text_branch(p, inputs, ident, h_txt):
    nc, S = p.nc, p.samples
    U = p.quads
    R = S_TXT
    QW = QUAD * SP_TXT
    SCALE = 1.0 / float(np.sqrt(DH))

    with ExitStack() as ctx:
        def sb(name, shape, dtype=F32):
            return ctx.enter_context(nc.sbuf_tensor("tx_" + name, shape, dtype))

        def sem(name):
            return p.sem("tx_" + name)

        w_all = sb("w_all", [P, LAYERS + 1, W_COLS], F32R)
        w2_all, rows_all, cols_all, fin_g, fin_b = (
            inputs.w2_all, inputs.rows_all, inputs.cols_all, inputs.fin_g, inputs.fin_b)
        row_in_group, lo_rows = sb("row_in_group", [P, 1]), sb("lo_rows", [P, 2])
        head_rows = sb("head_rows", [P, HPT])
        V = sb("V", [P, 2, QUAD, HEADS, DH + 1])
        xT = sb("xT", [P, QUAD, SP_TXT], F32R)
        xTf = sb("xTf", [P, 2, QUAD, SP_TXT], F32R)
        oT = sb("oT", [P, QUAD, SP_TXT], F32R)
        QP = sb("QP", [P, 2, TENSORS, SP_TXT], F32R)
        mpad = sb("mpad", [R, TENSORS, P], F32R)
        power = sb("power", [P, QUAD])

        with ExitStack() as setup:
            def tmp(name, shape, dtype=F32):
                return setup.enter_context(nc.sbuf_tensor("tx_" + name, shape, dtype))

            raw, toks, emb, pos_sb = inputs.raw, inputs.toks, inputs.emb, inputs.pos
            q_hi, q_lo = tmp("q_hi", [P, LAYERS, D], F32R), tmp("q_lo", [P, LAYERS, D], F32R)
            row_index = tmp("row_index", [P, 1], I32)
            steps = tmp("steps", [P, 5])
            word = tmp("word", [VOCAB, 1], I32)
            word_f = tmp("word_f", [VOCAB, 1])
            hot = tmp("hot", [VOCAB, 2, QUAD, R])
            emb_rows = [p.psum(setup, f"tx_emb_rows{k}", [P, QUAD, D]) for k in range(2)]

            cleared, indexed, masks, cut, placed = (
                sem("cleared"), sem("indexed"), sem("masks"), sem("w_cut"), sem("w_placed"))
            ones_set, hot_made, embedded, summed = (
                sem("ones_set"), sem("hot_made"), sem("embedded"), sem("pos_added"))

            with nc.Block() as block:
                @block.gpsimd
                def _(pool):
                    pool.memset(V[:], 1.0).then_inc(cleared, 1)
                    pool.memset(power[:], -0.5).then_inc(cleared, 1)
                    for t in (xT, xTf, oT, QP, mpad):
                        pool.memset(t[:].bitcast(F32), 0.0).then_inc(cleared, 1)
                    pool.memset(head_rows[:], 0.0).then_inc(cleared, 1)
                    for t in (w_all[:].bitcast(F32), w2_all[:], rows_all[:]):
                        pool.memset(t[:, LAYERS:], 0.0).then_inc(cleared, 1)
                    pool.wait_ge(cleared, 11)
                    for j in range(HPT):
                        rows = slice(GROUP * j, GROUP * (j + 1))
                        pool.memset(head_rows[rows, j:j + 1], 1.0).then_inc(indexed, 1)
                        pool.wait_ge(indexed, 2 * j + 1)
                        pool.iota(row_index[rows], pattern=[[0, 1]], base=0, channel_multiplier=1).then_inc(indexed, 1)
                        pool.wait_ge(indexed, 2 * j + 2)
                    pool.iota(word[:], pattern=[[0, 1]], base=0, channel_multiplier=1).then_inc(indexed, 1)

                @block.vector
                def _(dve):
                    sec = {m: w_all[:, 0:LAYERS, a:b] for m, (a, b) in SEC.items()}
                    dve.memset(sec["q"].bitcast(F32), 0.0).then_inc(masks, 1)
                    dve.memset(sec["k"].bitcast(F32), 0.0).then_inc(masks, 1)
                    dve.wait_ge(indexed, 2 * HPT + 1)
                    dve.tensor_copy(row_in_group[:], row_index[:]).then_inc(masks, 1)
                    dve.tensor_copy(word_f[:], word[:]).then_inc(masks, 1)
                    dve.wait_ge(masks, 4)
                    for k, edge in enumerate((DH, 2 * DH, 3 * DH, 3 * DH + 1)):
                        dve.tensor_scalar(steps[:, k:k + 1], row_in_group[:], float(edge), None, ALU.is_ge)\
                            .then_inc(masks, 1)
                    dve.wait_ge(masks, 8)
                    dve.tensor_tensor(lo_rows[:, 0:1], steps[:, 1:2], steps[:, 2:3], ALU.subtract).then_inc(masks, 1)
                    dve.tensor_tensor(lo_rows[:, 1:2], steps[:, 0:1], steps[:, 1:2], ALU.subtract).then_inc(masks, 1)
                    dve.tensor_tensor(steps[:, 4:5], steps[:, 2:3], steps[:, 3:4], ALU.subtract).then_inc(masks, 1)
                    dve.wait_ge(masks, 11)
                    dve.wait_ge(inputs.small_loaded, inputs.N_SMALL * 16)
                    dve.tensor_tensor(cols_all[:, :, 4:6], cols_all[:, :, 4:6],
                                      steps[:, 4:5].unsqueeze(1).broadcast_to([P, LAYERS + 1, 2]), ALU.add)\
                        .then_inc(ones_set, 1)
                    dve.wait_ge(inputs.w_loaded, inputs.N_W * 16)
                    pairs = [(raw["Wq"][:], q_hi[:], q_lo[:]),
                             (raw["Wv"][:], sec["v"][:, :, 0:D], sec["v"][:, :, D:]),
                             (raw["Wo"][:], sec["o"][:, :, 0:D], sec["o"][:, :, D:]),
                             (raw["W1"][:], sec["ff1"][:, :, 0:FF], sec["ff1"][:, :, FF:])]
                    for src, hi, lo in pairs:
                        dve.tensor_copy(hi, src).then_inc(cut, 1)
                    dve.wait_ge(cut, 4)
                    for src, hi, lo in pairs:
                        dve.tensor_tensor(lo, src, hi.bitcast(F32), ALU.subtract).then_inc(cut, 1)
                    dve.wait_ge(cut, 8)
                    for part in range(2):
                        a, b = part * 2 * P, (part + 1) * 2 * P
                        place_heads(dve, sec["q"][:, :, a:b], (q_lo if part else q_hi)[:].bitcast(F32), DH, GROUP, placed)
                        place_heads(dve, sec["k"][:, :, a:b],
                                    sec["v"][:, :, part * D:(part + 1) * D].bitcast(F32), DH, GROUP, placed)
                    dve.wait_ge(ones_set, 1)
                    for at, who in ((0, 0), (4, 1)):
                        dve.tensor_scalar(cols_all[:, :, at + 2:at + 4], cols_all[:, :, at:at + 2],
                                          lo_rows[:, who:who + 1], None, ALU.mult)
                    dve.wait_ge(inputs.tok_loaded, inputs.N_TOK * 16)

                    def make_hot(n, par):
                        dve.tensor_scalar(hot[:, par].rearrange("v b t -> v (b t)"),
                                          toks[:, bass.ds(n * (QUAD * R), QUAD * R)], word_f[:, 0:1], None,
                                          ALU.is_equal).then_inc(hot_made, 1)

                    def add_pos(n, par):
                        dve.wait_ge(embedded, n + 1)
                        dve.tensor_tensor(h_txt[:, bass.ds(n * QUAD, QUAD)], emb_rows[par][0:R],
                                          pos_sb[:].unsqueeze(1).broadcast_to([R, QUAD, D]), ALU.add)\
                            .then_inc(summed, 1)

                    make_hot(0, 0)
                    make_hot(1, 1)
                    with dve.Fori(0, U // 2 - 1) as i:
                        add_pos(i * 2, 0)
                        make_hot(i * 2 + 2, 0)
                        add_pos(i * 2 + 1, 1)
                        make_hot(i * 2 + 3, 1)
                    add_pos(U - 2, 0)
                    add_pos(U - 1, 1)

                @block.tensor
                def _(pe):
                    def quad(n, par, first):
                        if not first:
                            pe.wait_ge(summed, n - 1)
                        pe.wait_ge(hot_made, n + 1)
                        for b in range(QUAD):
                            last = pe.matmul(emb_rows[par][0:R, b], hot[:, par, b], emb[:], start=True, stop=True)
                        last.then_inc(embedded, 1)

                    quad(0, 0, True)
                    quad(1, 1, True)
                    with pe.Fori(1, U // 2) as i:
                        quad(i * 2, 0, False)
                        quad(i * 2 + 1, 1, False)

        w = sb("w", [P, W_COLS], F32R)
        w2 = sb("w2", [P, 2, D])
        rows = sb("rows", [R, len(ROWS_OF), D])
        cols = sb("cols", [P, 10])
        xs = sb("xs", [P, QUAD, 2 * D], F32R)
        qk_lo = sb("qk_lo", [P, 2, QW], F32R)
        KF = sb("KF", [P, TENSORS, QW], F32R)
        QF = sb("QF", [P, 2, TENSORS, QUAD, SP_TXT], F32R)
        KB = sb("KB", [P, 2, TENSORS, HPT, QW], F32R)
        PT = sb("PT", [P, 2, TENSORS, HPT * SP_TXT])
        oU = sb("oU", [P, TENSORS, SP_TXT])
        rsum = sb("rsum", [R, HEADS])
        o_rows = sb("o_rows", [R, 2, QUAD, D])
        os_ = sb("os", [P, QUAD, 2 * D], F32R)
        y, yn, x_shift = sb("y", [R, 2, QUAD, D]), sb("yn", [R, 2, QUAD, D]), sb("x_shift", [R, 2, QUAD, D])
        var_eps, neg_mean, rstd, neg_mean_rstd = (
            sb("var_eps", [R, 2, QUAD]), sb("neg_mean", [R, 2, QUAD]), sb("rstd", [R, 2, QUAD]),
            sb("neg_mean_rstd", [R, 2, QUAD]))
        stats, mean_var = sb("stats", [R, QUAD, 6]), sb("mean_var", [R, QUAD, 2])
        HT = sb("HT", [P, 2, 2, QW])

        w_set = sem("w_set")
        x_hi, x_cut, x_turned, xT_set = sem("x_hi"), sem("x_cut"), sem("x_turned"), sem("xT_set")
        projected, lo_part, qk_cut, k_split = sem("projected"), sem("lo_part"), sem("qk_cut"), sem("k_split")
        v_made, v_set = sem("v_made"), sem("v_set")
        scored, max_set, max_turned, q_set = sem("scored"), sem("max_set"), sem("max_turned"), sem("q_set")
        scored_t, exped, weighed = sem("scored_t"), sem("exped"), sem("weighed")
        out_copied, outs_turned, outs_cleared = sem("out_copied"), sem("outs_turned"), sem("outs_cleared")
        sums_inv, o_set, o_hi, o_cut, o_turned, oT_set = (
            sem("sums_inv"), sem("o_set"), sem("o_hi"), sem("o_cut"), sem("o_turned"), sem("oT_set"))
        y_made, y_set, y_aggr, y_var, y_rstd, y_scale, y_normed, y_gain, shifted, x_new = (
            sem("y_made"), sem("y_set"), sem("y_aggr"), sem("y_var"), sem("y_rstd"), sem("y_scale"),
            sem("y_normed"), sem("y_gain"), sem("x_shifted"), sem("x_new"))
        f_hi, f_cut, f_turned, fT_set, f_up, f_gelu = (
            sem("f_hi"), sem("f_cut"), sem("f_turned"), sem("fT_set"), sem("f_up"), sem("f_gelu"))

        scores = p.psum(ctx, "tx_scores", [P, 2, 512])
        scores_t = p.psum(ctx, "tx_scores_t", [P, 2, 512])
        maxT = p.psum(ctx, "tx_maxT", [P, TENSORS, SP_TXT])
        out_bank = p.psum(ctx, "tx_out_bank", [P, 512])
        outT = out_bank[:, 0:TENSORS * SP_TXT].rearrange("p (t s) -> p t s", t=TENSORS)
        outs = out_bank[0:R, 256:256 + TENSORS * P].rearrange("p (t j r) -> p t j r", t=TENSORS, j=HPT)
        work = [p.psum(ctx, f"tx_work{k}", [P, 512]) for k in range(2)]

        def sec(m, part, a=0, b=None):
            lo, hi = SEC[m]
            half = (hi - lo) // 2
            return w[:, lo + part * half + a:lo + part * half + (half if b is None else b)]

        def of(m):
            return rows[:, ROWS_OF.index(m)].unsqueeze(1).broadcast_to([R, QUAD, D])

        def quads(n):
            return h_txt[:, bass.ds(n * QUAD, QUAD)]

        def turns(eng, body):
            body(0, 0, True, False, False)
            body(1, 1, False, False, False)
            if U > 4:
                with eng.Fori(1, U // 2 - 1) as i:
                    body(i * 2, 0, False, False, False)
                    body(i * 2 + 1, 1, False, False, False)
            body(U - 2, 0, False, True, False)
            body(U - 1, 1, False, True, True)

        def norm_at(l, g, ff):
            return l * (2 * U) + (U if ff else 0) + g

        def ln_stats(dve, n, par, y_psum, bias, between=None):
            dve.wait_ge(y_made, n + 1)
            dve.tensor_tensor(y[:, par], y_psum, of(bias), ALU.add).then_inc(y_set, 1)
            dve.wait_ge(y_set, n + 1)
            for b in range(QUAD):
                dve.bn_stats(stats[:, b], y[:, par, b])
            if between:
                between()
            dve.drain()
            for b in range(QUAD):
                last = dve.bn_aggr(mean_var[:, b], stats[:, b])
            last.then_inc(y_aggr, 1)
            dve.wait_ge(y_aggr, n + 1)
            dve.tensor_scalar(neg_mean[:, par], mean_var[:, :, 0], -1.0, None, ALU.mult)
            dve.tensor_scalar(var_eps[:, par], mean_var[:, :, 1], EPS, None, ALU.add).then_inc(y_var, 1)

        def ln_scale(pool, n, par):
            pool.wait_ge(y_var, n + 1)
            pool.tensor_tensor(rstd[:, par], var_eps[:, par], power[0:R], ALU.pow).then_inc(y_rstd, 1)
            pool.wait_ge(y_rstd, n + 1)
            pool.tensor_tensor(neg_mean_rstd[:, par], neg_mean[:, par], rstd[:, par], ALU.mult).then_inc(y_scale, 1)

        def ln_norm(act, n, par, samples=range(QUAD)):
            act.wait_ge(y_scale, n + 1)
            for b in samples:
                last = act.activation(yn[:, par, b], y[:, par, b], ACT.Identity,
                                      bias=neg_mean_rstd[:, par, b:b + 1], scale=rstd[:, par, b:b + 1])
            if QUAD - 1 in samples:
                last.then_inc(y_normed, 1)

        def ln_shift(pool, n, par, g, shift):
            pool.tensor_tensor(x_shift[:, par], quads(g), of(shift), ALU.add).then_inc(shifted, 1)

        def ln_sum(dve, n, par, g, gain):
            dve.wait_ge(y_normed, n + 1)
            dve.tensor_tensor(yn[:, par], yn[:, par], of(gain), ALU.mult).then_inc(y_gain, 1)
            dve.wait_ge(y_gain, n + 1)
            dve.wait_ge(shifted, n + 1)
            dve.tensor_tensor(quads(g), yn[:, par], x_shift[:, par], ALU.add).then_inc(x_new, 1)

        def at_most(g, k):
            return isinstance(g, int) and g <= k

        with nc.Block() as block:
            @block.vector
            def _(dve):
                def set_attention_weights(l):
                    dve.tensor_copy(w[:, 0:W_ATT], w_all[:, bass.ds(l, 1), 0:W_ATT].rearrange("p a n -> p (a n)").bitcast(F32))\
                        .then_inc(w_set, 1)

                def set_cols(l):
                    dve.tensor_copy(cols[:], cols_all[:, bass.ds(l, 1)].rearrange("p a n -> p (a n)")).then_inc(w_set, 1)

                def set_feed_forward_weights(l):
                    dve.tensor_copy(w[:, W_ATT:], w_all[:, bass.ds(l, 1), W_ATT:].rearrange("p a n -> p (a n)").bitcast(F32))\
                        .then_inc(w_set, 1)
                    dve.tensor_copy(w2[:], w2_all[:, bass.ds(l, 1)].rearrange("p a k n -> p (a k) n")).then_inc(w_set, 1)

                def set_rows(l):
                    dve.tensor_copy(rows[:], rows_all[:, bass.ds(l, 1)].rearrange("p a k n -> p (a k) n")).then_inc(w_set, 1)

                def cut_qk(n, i, par):
                    t, is_q = i % 2, i // 2
                    dst = QF[:, par, t].rearrange("p b s -> p (b s)") if is_q else KF[:, t]
                    dve.wait_ge(lo_part, n * 4 + i + 1)
                    dve.scalar_tensor_tensor(out=dst, in0=work[(i + 1) % 2][:, 0:QW],
                                             scalar=cols[:, (0 if is_q else 4) + t:(1 if is_q else 5) + t],
                                             in1=qk_lo[:, i % 2].bitcast(F32), op0=ALU.add, op1=ALU.subtract)\
                        .then_inc(qk_cut, 1)

                def set_v(n, par):
                    dve.wait_ge(v_made, n + 1)
                    bias = of("bv").rearrange("p b (h c) -> p b h c", h=HEADS)
                    src = work[1][0:R, 0:QUAD * D].rearrange("p (b h c) -> p b h c", b=QUAD, h=HEADS)
                    dve.tensor_tensor(V[0:R, par, :, :, 0:DH], src, bias, ALU.add).then_inc(v_set, 1)

                def find_max(nb):
                    dve.wait_ge(scored, nb + 1)
                    dve.tensor_reduce(mpad[0:R].rearrange("p t (j r) -> p t j r", r=GROUP)[:, :, :, 3 * DH],
                                      scores[0:R, :, 0:HPT * SP_TXT].rearrange("p t (j s) -> p t j s", j=HPT)[:, :, :, 0:R],
                                      AX.X, ALU.max, negate=True).then_inc(max_set, 1)

                def join_max(nb, par, b):
                    dve.wait_ge(max_turned, nb + 1)
                    dve.tensor_tensor(QP[:, b % 2, :, 0:R], maxT[:, :, 0:R], QF[:, par, :, b, 0:R].bitcast(F32),
                                      ALU.add).then_inc(q_set, 1)

                def normalise_o(nb, par, b):
                    dve.wait_ge(outs_turned, nb + 1)
                    dve.reciprocal(rsum[:].rearrange("p (t j) -> p t j", t=TENSORS), outs[:, :, :, DH]).then_inc(sums_inv, 1)
                    dve.wait_ge(sums_inv, nb + 1)
                    dve.tensor_tensor(o_rows[:, par, b].rearrange("p (t j c) -> p t j c", t=TENSORS, j=HPT),
                                      outs[:, :, :, 0:DH],
                                      rsum[:].rearrange("p (t j) -> p t j", t=TENSORS).unsqueeze(3)
                                      .broadcast_to([R, TENSORS, HPT, DH]), ALU.mult).then_inc(o_set, 1)

                y_rows = work[1][0:R, 0:QUAD * D].rearrange("p (b d) -> p b d", b=QUAD)

                dve.memset(out_bank[:], 0.0).then_inc(outs_cleared, 1)
                dve.memset(PT[:], 0.0).then_inc(outs_cleared, 1)
                for rows_split in (xs, os_):
                    dve.memset(rows_split[:].bitcast(F32), 0.0).then_inc(outs_cleared, 1)
                set_attention_weights(0)
                set_cols(0)
                set_feed_forward_weights(0)
                set_rows(0)
                dve.wait_ge(w_set, 2)
                for i in range(2):
                    cut_qk(0, i, 0)
                with dve.Fori(0, LAYERS) as l:
                    for i in range(2, 4):
                        cut_qk(l * U, i, 0)
                    dve.wait_ge(w_set, l * 5 + 5)
                    set_v(l * U, 0)
                    find_max(l * U * QUAD)
                    join_max(l * U * QUAD, 0, 0)
                    find_max(l * U * QUAD + 1)
                    join_max(l * U * QUAD + 1, 0, 1)

                    def attention(g, par, first, last2, last):
                        n = l * U + g
                        ln = norm_at(l, g - 1, False)

                        def join_second():
                            if not last:
                                join_max(n * QUAD + (QUAD + 1), 1 - par, 1)

                        for b in range(QUAD):
                            if b == 3 and not last:
                                find_max(n * QUAD + QUAD)
                            if b in (1, 2):
                                join_max(n * QUAD + (b + 1), par, b + 1)
                            if b:
                                normalise_o(n * QUAD + (b - 1), par, b - 1)
                            elif not first:
                                normalise_o(n * QUAD - 1, 1 - par, QUAD - 1)
                            if b == 2 and not last:
                                set_v(n + 1, 1 - par)
                            if b == 3 and not last:
                                join_max(n * QUAD + QUAD, 1 - par, 0)
                            if b < QUAD - 2 or b == QUAD - 1 and not last:
                                find_max(n * QUAD + (b + 2))
                            if b == 0 and not last:
                                cut_qk(n + 1, 0, 1 - par)
                                cut_qk(n + 1, 1, 1 - par)
                            if b == 1 and not last:
                                cut_qk(n + 1, 2, 1 - par)
                                cut_qk(n + 1, 3, 1 - par)
                            if b == 2 and not at_most(g, 1):
                                ln_sum(dve, ln - 1, par, g - 2, "ln1_g")
                            if b == 3 and first:
                                join_second()
                            if b == 3 and not first:
                                ln_stats(dve, ln, 1 - par, y_rows, "bo", between=join_second)
                        if last:
                            normalise_o(n * QUAD + (QUAD - 1), par, QUAD - 1)
                            ln_sum(dve, ln, 1 - par, g - 1, "ln1_g")
                            ln_stats(dve, ln + 1, par, y_rows, "bo")

                    turns(dve, attention)

                    def feed_forward(g, par, first, last2, last):
                        ln = norm_at(l, g, True)
                        if last:
                            dve.wait_ge(y_made, ln + 1)
                            set_cols(l + 1)
                        ln_stats(dve, ln, par, y_rows, "b2")
                        if last:
                            dve.wait_ge(w_set, l * 5 + 7)
                            for i in range(2):
                                cut_qk(l * U + U, i, 0)
                            set_feed_forward_weights(l + 1)
                        if first:
                            ln_sum(dve, ln - 1, 1 - par, U - 1, "ln1_g")
                            set_attention_weights(l + 1)
                        else:
                            ln_sum(dve, ln - 1, 1 - par, g - 1, "ln2_g")
                        if last:
                            ln_sum(dve, ln, par, g, "ln2_g")
                            set_rows(l + 1)

                    turns(dve, feed_forward)

            @block.gpsimd
            def _(pool):
                def cut(rows_f32, split, hi_ready, done, n):
                    pool.wait_ge(hi_ready, n + 1)
                    pool.tensor_tensor(split[0:R, :, D:], rows_f32, split[0:R, :, 0:D].bitcast(F32), ALU.subtract)\
                        .then_inc(done, 1)

                def split_k(n, par):
                    for t in range(TENSORS):
                        pool.wait_ge(qk_cut, n * 4 + t + 1)
                        pool.tensor_tensor(KB[:, par, t], KF[:, t].bitcast(F32).unsqueeze(1).broadcast_to([P, HPT, QW]),
                                           head_rows[:].unsqueeze(2).broadcast_to([P, HPT, QW]), ALU.mult)\
                            .then_inc(k_split, 1)

                cut(quads(0), xs, x_hi, x_cut, 0)
                cut(quads(1), xs, x_hi, x_cut, 1)
                with pool.Fori(0, LAYERS) as l:
                    split_k(l * U, 0)
                    pool.wait_ge(w_set, l * 5 + 5)

                    def attention(g, par, first, last2, last):
                        n = l * U + g
                        ln = norm_at(l, g - 1, False)
                        if not first:
                            cut(o_rows[:, 1 - par], os_, o_hi, o_cut, n - 1)
                        if last:
                            cut(quads(0), xs, f_hi, f_cut, l * U)
                        if not last:
                            split_k(n + 1, 1 - par)
                        if not first:
                            ln_shift(pool, ln, 1 - par, g - 1, "ln1_b")
                        if not last2:
                            cut(quads(g + 2), xs, x_hi, x_cut, n + 2)
                        if last:
                            cut(quads(1), xs, f_hi, f_cut, l * U + 1)
                        if not first:
                            ln_scale(pool, ln, 1 - par)
                        if last:
                            cut(o_rows[:, par], os_, o_hi, o_cut, n)
                            ln_shift(pool, ln + 1, par, g, "ln1_b")
                            ln_scale(pool, ln + 1, par)

                    turns(pool, attention)

                    def feed_forward(g, par, first, last2, last):
                        n, ln = l * U + g, norm_at(l, g, True)
                        if not last2:
                            cut(quads(g + 2), xs, f_hi, f_cut, n + 2)
                        else:
                            cut(quads(g + 2 - U), xs, x_hi, x_cut, n + 2)
                        pool.wait_ge(x_new, ln - 1)
                        ln_shift(pool, ln, par, g, "ln2_b")
                        ln_scale(pool, ln, par)

                    turns(pool, feed_forward)

            @block.scalar
            def _(act):
                def hi(rows_f32, split, done):
                    act.activation(split[0:R, :, 0:D], rows_f32, ACT.Copy).then_inc(done, 1)

                def set_turned(dst, turned, done, n):
                    act.wait_ge(turned, n + 1)
                    act.activation(dst[:, :, 0:R], work[0][:].rearrange("p (b s) -> p b s", b=QUAD)[:, :, 0:R], ACT.Copy)\
                        .then_inc(done, 1)

                def part_lo(n, i):
                    t, is_q = i % 2, i // 2
                    at = (2 if is_q else 6) + t
                    act.wait_ge(projected, n * 4 + i + 1)
                    act.activation(qk_lo[:, i % 2], work[(i + 1) % 2][:, 0:QW], ACT.Identity,
                                   bias=cols[:, at:at + 1], scale=lo_rows[:, 1 - is_q:2 - is_q]).then_inc(lo_part, 1)

                def exp(nb, b, fresh):
                    act.wait_ge(scored_t, nb + 1)
                    if not fresh:
                        act.wait_ge(weighed, nb - 1)
                    act.activation(PT[0:R, b % 2], scores_t[0:R, :, 0:HPT * SP_TXT], ACT.Exp, scale=SCALE)\
                        .then_inc(exped, 1)

                def copy_outs(nb):
                    act.wait_ge(weighed, nb + 1)
                    act.activation(oU[:], outT, ACT.Copy).then_inc(out_copied, 1)

                def gelu(n, par):
                    act.wait_ge(f_up, n + 1)
                    for half in range(2):
                        src = (scores_t if par else scores)[:, half, 0:QW]
                        last = act.activation(HT[:, par, half], src, ACT.Gelu, bias=cols[:, 8 + half:9 + half])
                    last.then_inc(f_gelu, 1)

                act.wait_ge(outs_cleared, 4)
                hi(quads(0), xs, x_hi)
                set_turned(xT, x_turned, xT_set, 0)
                hi(quads(1), xs, x_hi)
                act.wait_ge(w_set, 2)
                for i in range(2):
                    part_lo(0, i)
                with act.Fori(0, LAYERS) as l:
                    for i in range(2, 4):
                        part_lo(l * U, i)

                    def attention(g, par, first, last2, last):
                        n = l * U + g
                        ln = norm_at(l, g - 1, False)
                        for b in range(QUAD):
                            exp(n * QUAD + b, b, first and b < 2)
                            if b or not first:
                                copy_outs(n * QUAD + (b - 1))
                            if b == 0 and not last:
                                set_turned(xT, x_turned, xT_set, n + 1)
                            if b == 0 and not last:
                                part_lo(n + 1, 0)
                                part_lo(n + 1, 1)
                            if b == 1 and not last:
                                part_lo(n + 1, 2)
                                part_lo(n + 1, 3)
                            if b == 0 and not first:
                                act.wait_ge(o_set, n * QUAD)
                                hi(o_rows[:, 1 - par], os_, o_hi)
                            if b < 2 and not at_most(g, 1):
                                ln_norm(act, ln - 1, par, (2 * b, 2 * b + 1))
                            if b == 2 and not last2:
                                hi(quads(g + 2), xs, x_hi)
                            if b == 2 and not first:
                                set_turned(oT, o_turned, oT_set, n - 1)
                            if last:
                                if b < 2:
                                    act.wait_ge(x_new, norm_at(l, b, False) + 1)
                                    hi(quads(b), xs, f_hi)
                                if b == 0:
                                    set_turned(xTf[:, 0], f_turned, fT_set, l * U)
                                if b == 3:
                                    set_turned(xTf[:, 1], f_turned, fT_set, l * U + 1)
                        if last:
                            copy_outs(n * QUAD + (QUAD - 1))
                            act.wait_ge(o_set, n * QUAD + QUAD)
                            hi(o_rows[:, par], os_, o_hi)
                            ln_norm(act, ln, 1 - par)
                            set_turned(oT, o_turned, oT_set, n)
                            gelu(l * U, 0)

                    turns(act, attention)

                    def feed_forward(g, par, first, last2, last):
                        n = l * U + g
                        if not last2:
                            act.wait_ge(x_new, norm_at(l, g + 2, False) + 1)
                            hi(quads(g + 2), xs, f_hi)
                        if not last:
                            gelu(n + 1, 1 - par)
                        if last2 and not last:
                            act.wait_ge(x_new, norm_at(l, 0, True) + 1)
                            hi(quads(0), xs, x_hi)
                        if last:
                            set_turned(xT, x_turned, xT_set, n + 1)
                            act.wait_ge(x_new, norm_at(l, 1, True) + 1)
                            hi(quads(1), xs, x_hi)
                        ln_norm(act, norm_at(l, g, True) - 1, 1 - par)
                        if not last2:
                            set_turned(xTf[:, par], f_turned, fT_set, n + 2)
                        if last:
                            act.wait_ge(w_set, l * 5 + 7)
                            for i in range(2):
                                part_lo(n + 1, i)
                            ln_norm(act, norm_at(l, g, True), par)

                    turns(act, feed_forward)

            @block.tensor
            def _(pe):
                def turn(src, ready, done, n):
                    pe.wait_ge(ready, n + 1)
                    for b in range(QUAD):
                        last = pe.transpose(work[0][:, b * P:(b + 1) * P], src[:, b].bitcast(F32), ident[:])
                    last.then_inc(done, 1)

                def project(n, i):
                    t, m = i % 2, "q" if i // 2 else "k"
                    if i >= 2:
                        pe.wait_ge(qk_cut, n * 4 + i - 1)
                    for part in range(2):
                        last = pe.matmul(work[(i + 1) % 2][:, 0:QW], sec(m, part, t * P, (t + 1) * P),
                                         xT[:].rearrange("p b s -> p (b s)"), start=part == 0, stop=part == 1)
                    last.then_inc(projected, 1)

                def project_v(n):
                    pe.wait_ge(qk_cut, n * 4 + 3)
                    for b in range(QUAD):
                        for part in range(2):
                            last = pe.matmul(work[1][0:R, b * D:(b + 1) * D], xT[:, b, 0:R], sec("v", part),
                                             start=part == 0, stop=part == 1)
                    last.then_inc(v_made, 1)

                def score(n, par, b):
                    if b == 0:
                        pe.wait_ge(k_split, n * 2 + 2)
                        pe.wait_ge(qk_cut, n * 4 + 4)
                    for t in range(TENSORS):
                        k = KB[:, par, t].rearrange("p j (b s) -> p j b s", b=QUAD)[:, :, b]
                        last = pe.matmul(scores[0:R, t, 0:HPT * SP_TXT], QF[:, par, t, b, 0:R], k, start=True, stop=True)
                    last.then_inc(scored, 1)

                def turn_max(nb):
                    pe.wait_ge(max_set, nb + 1)
                    for t in range(TENSORS):
                        last = pe.transpose(maxT[:, t, 0:R], mpad[0:R, t].bitcast(F32), ident[0:R, 0:R])
                    last.then_inc(max_turned, 1)

                def score_t(n, par, b, fresh):
                    nb = n * QUAD + b
                    pe.wait_ge(q_set, nb + 1)
                    if not fresh:
                        pe.wait_ge(exped, nb)
                    for t in range(TENSORS):
                        for j in range(HPT):
                            k = KB[:, par, t, j].rearrange("p (b s) -> p b s", b=QUAD)[:, b, 0:R]
                            last = pe.matmul(scores_t[0:R, t, j * SP_TXT:(j + 1) * SP_TXT], k, QP[:, b % 2, t],
                                             start=True, stop=True)
                    last.then_inc(scored_t, 1)

                def weigh(nb, n, par, b, fresh):
                    pe.wait_ge(exped, nb + 1)
                    if b == 0:
                        pe.wait_ge(v_set, n + 1)
                    if not fresh:
                        pe.wait_ge(o_set, nb)
                    for t in range(TENSORS):
                        for j in range(HPT):
                            last = pe.matmul(outT[32 * j:32 * j + DH + 1, t], V[:, par, b, t * HPT + j],
                                             PT[:, b % 2, t, j * SP_TXT:(j + 1) * SP_TXT], start=True, stop=True)
                    last.then_inc(weighed, 1)

                def turn_outs(nb):
                    pe.wait_ge(out_copied, nb + 1)
                    for t in range(TENSORS):
                        last = pe.transpose(out_bank[0:R, 256 + t * P:256 + (t + 1) * P], oU[:, t, 0:R], ident[:])
                    last.then_inc(outs_turned, 1)

                def project_o(n, ln, bank_ready):
                    pe.wait_ge(oT_set, n + 1)
                    pe.wait_ge(*bank_ready)
                    for b in range(QUAD):
                        for part in range(2):
                            last = pe.matmul(work[1][0:R, b * D:(b + 1) * D], oT[:, b, 0:R], sec("o", part),
                                             start=part == 0, stop=part == 1)
                    last.then_inc(y_made, 1)

                def up(n, par):
                    pe.wait_ge(fT_set, n + 1)
                    for half in range(2):
                        for part in range(2):
                            last = pe.matmul((scores_t if par else scores)[:, half, 0:QW],
                                             sec("ff1", part, half * P, (half + 1) * P),
                                             xTf[:, par].rearrange("p b s -> p (b s)"), start=part == 0, stop=part == 1)
                    last.then_inc(f_up, 1)

                def down(n, ln, par):
                    pe.wait_ge(f_gelu, n + 1)
                    pe.wait_ge(y_set, ln)
                    for b in range(QUAD):
                        for half in range(2):
                            last = pe.matmul(work[1][0:R, b * D:(b + 1) * D],
                                             HT[:, par, half].rearrange("p (b s) -> p b s", b=QUAD)[:, b, 0:R],
                                             w2[:, half], start=half == 0, stop=half == 1)
                    last.then_inc(y_made, 1)

                pe.wait_ge(outs_cleared, 4)
                turn(xs, x_cut, x_turned, 0)
                pe.wait_ge(xT_set, 1)
                pe.wait_ge(w_set, 1)
                for i in range(2):
                    project(0, i)
                with pe.Fori(0, LAYERS) as l:
                    for i in range(2, 4):
                        project(l * U, i)
                    pe.wait_ge(w_set, l * 5 + 4)
                    project_v(l * U)
                    score(l * U, 0, 0)
                    turn_max(l * U * QUAD)
                    score(l * U, 0, 1)

                    def attention(g, par, first, last2, last):
                        n = l * U + g
                        ln = norm_at(l, g - 1, False)
                        for b in range(QUAD):
                            score_t(n, par, b, first and b == 0)
                            if b == 0 and not last:
                                turn(xs, x_cut, x_turned, n + 1)
                            if b == QUAD - 1 and not last:
                                score(n + 1, 1 - par, 0)
                            if b > 0:
                                weigh(n * QUAD + (b - 1), n, par, b - 1, first and b == 1)
                            elif not first:
                                weigh(n * QUAD - 1, n - 1, 1 - par, QUAD - 1, False)
                            if b < QUAD - 1:
                                turn_max(n * QUAD + (b + 1))
                            if b < QUAD - 2:
                                score(n, par, b + 2)
                            if b == 1 and not last:
                                project(n + 1, 2)
                                project(n + 1, 3)
                            if b == 2 and not last:
                                project_v(n + 1)
                            if b == 3 and not first:
                                project_o(n - 1, ln, (y_set, ln) if last else (v_set, n + 2))
                            if b or not first:
                                turn_outs(n * QUAD + (b - 1))
                            if b == QUAD - 1 and not last:
                                turn_max(n * QUAD + QUAD)
                                score(n + 1, 1 - par, 1)
                            if b == 0 and not last:
                                pe.wait_ge(xT_set, n + 2)
                                if first or isinstance(g, int) and g == 1:
                                    pe.wait_ge(v_set, n + 1)
                                else:
                                    pe.wait_ge(y_set, ln)
                                project(n + 1, 0)
                                project(n + 1, 1)
                            if b == 2 and not first:
                                if not last:
                                    pe.wait_ge(qk_cut, n * 4 + 8)
                                else:
                                    pe.wait_ge(fT_set, l * U + 1)
                                turn(os_, o_cut, o_turned, n - 1)
                            if b == 0 and last:
                                turn(xs, f_cut, f_turned, l * U)
                            if b == 3 and last:
                                turn(xs, f_cut, f_turned, l * U + 1)
                                up(l * U, 0)
                        if last:
                            weigh(n * QUAD + (QUAD - 1), n, par, QUAD - 1, False)
                            turn_outs(n * QUAD + (QUAD - 1))
                            pe.wait_ge(fT_set, l * U + 2)
                            turn(os_, o_cut, o_turned, n)
                            project_o(n, norm_at(l, g, False), (y_set, ln + 1))

                    turns(pe, attention)

                    def feed_forward(g, par, first, last2, last):
                        n = l * U + g
                        down(n, norm_at(l, g, True), par)
                        if not last:
                            up(n + 1, 1 - par)
                        if not last2:
                            turn(xs, f_cut, f_turned, n + 2)
                        elif not last:
                            turn(xs, x_cut, x_turned, n + 2)
                        else:
                            pe.wait_ge(w_set, l * 5 + 6)
                            pe.wait_ge(xT_set, n + 2)
                            pe.wait_ge(y_set, norm_at(l, g, True) + 1)
                            for i in range(2):
                                project(n + 1, i)

                    turns(pe, feed_forward)

        def end_at(n):
            return LAYERS * 2 * U + n

        def over_quads(eng, body):
            body(0, 0, True)
            body(1, 1, False)
            with eng.Fori(1, U // 2) as i:
                body(i * 2, 0, False)
                body(i * 2 + 1, 1, False)

        with nc.Block() as block:
            @block.vector
            def _(dve):
                def gain(q, par):
                    n = end_at(q)
                    dve.wait_ge(y_normed, n + 1)
                    dve.tensor_tensor(yn[:, par], yn[:, par], fin_g[:].unsqueeze(1).broadcast_to([R, QUAD, D]), ALU.mult)\
                        .then_inc(y_gain, 1)

                def quad(q, par, first):
                    n = end_at(q)
                    for b in range(QUAD):
                        dve.bn_stats(stats[:, b], quads(q)[:, b])
                    dve.drain()
                    for b in range(QUAD):
                        last = dve.bn_aggr(mean_var[:, b], stats[:, b])
                    last.then_inc(y_aggr, 1)
                    dve.wait_ge(y_aggr, n + 1)
                    dve.tensor_scalar(neg_mean[:, par], mean_var[:, :, 0], -1.0, None, ALU.mult)
                    dve.tensor_scalar(var_eps[:, par], mean_var[:, :, 1], EPS, None, ALU.add).then_inc(y_var, 1)
                    if not first:
                        gain(q - 1, 1 - par)

                over_quads(dve, quad)
                gain(U - 1, 1)

            @block.gpsimd
            def _(pool):
                def add(q, par):
                    pool.wait_ge(y_gain, end_at(q) + 1)
                    pool.tensor_tensor(quads(q), yn[:, par], fin_b[:].unsqueeze(1).broadcast_to([R, QUAD, D]), ALU.add)\
                        .then_inc(x_new, 1)

                def quad(q, par, first):
                    n = end_at(q)
                    pool.wait_ge(y_var, n + 1)
                    pool.tensor_tensor(rstd[:, par], var_eps[:, par], power[0:R], ALU.pow).then_inc(y_rstd, 1)
                    pool.wait_ge(y_rstd, n + 1)
                    pool.tensor_tensor(neg_mean_rstd[:, par], neg_mean[:, par], rstd[:, par], ALU.mult)\
                        .then_inc(y_scale, 1)
                    if not first:
                        add(q - 1, 1 - par)

                over_quads(pool, quad)
                add(U - 1, 1)

            @block.scalar
            def _(act):
                def quad(q, par, first):
                    n = end_at(q)
                    act.wait_ge(y_scale, n + 1)
                    for b in range(QUAD):
                        last = act.activation(yn[:, par, b], quads(q)[:, b], ACT.Identity,
                                              bias=neg_mean_rstd[:, par, b:b + 1], scale=rstd[:, par, b:b + 1])
                    last.then_inc(y_normed, 1)

                over_quads(act, quad)



SEQ = T + S_TXT
SEQP = SEQ + 1
TILES = ((0, T), (T, S_TXT))
A_HEADS = 4
A_DH = D // A_HEADS
A_GROUP = 64
A_HPT = P // A_GROUP
A_TENSORS = A_HEADS // A_HPT
A_HALF = A_TENSORS * P
CLIP = 10000.0
EXPERTS = 8


def live(n):
    return not isinstance(n, int) or 0 <= n < B


def due(value):
    return not isinstance(value, int) or value > 0


def set_stats(dve, rows_of, mean_var, stats, neg_mean, var_eps, aggregated, var_ready, m, between=None):
    for t, (_, n) in enumerate(TILES):
        dve.bn_stats(stats[0:n, t], rows_of(m, t))
    if between:
        between()
    dve.drain()
    for t, (_, n) in enumerate(TILES):
        last = dve.bn_aggr(mean_var[0:n, t], stats[0:n, t])
    last.then_inc(aggregated, 1)
    dve.wait_ge(aggregated, m + 1)
    dve.tensor_scalar(neg_mean[:], mean_var[:, :, 0], -1.0, None, ALU.mult)
    dve.tensor_scalar(var_eps[:], mean_var[:, :, 1], EPS, None, ALU.add).then_inc(var_ready, 1)


class AttentionInputs:

    MATS = ("Wq", "Wk", "Wv", "Wo")

    def __init__(self, p, wts):
        self.nc, self.wts = p.nc, wts
        self.raw = p.sb("at_raw", [D, len(self.MATS), 2 * D])
        self.bv, self.bo = p.sb("at_bv", [P, D]), p.sb("at_bo", [D + 1, D])
        self.cols = p.sb("at_cols", [P, 8])
        self.loaded = p.sem("at_loaded")
        self.N = 2 * len(self.MATS) + 2 + 2 * A_HEADS * 3

    def load(self, q):
        wts = self.wts
        for k, m in enumerate(self.MATS):
            for half in range(2):
                q.dma_start(self.raw[:, k, half * D:(half + 1) * D], wts[m]).then_inc(self.loaded, 16)
        q.dma_start(self.bv[:], on_all_rows(wts["bv"])).then_inc(self.loaded, 16)
        q.dma_start(self.bo[D:D + 1], row(wts["bo"])).then_inc(self.loaded, 16)
        with self.nc.allow_non_contiguous_dma(reason="biases as columns, beside the heads' rows"):
            for at, m in ((0, "bq"), (4, "bk")):
                for h in range(A_HEADS):
                    t, j = h // A_HPT, h % A_HPT
                    src = wts[m][h * A_DH:(h + 1) * A_DH].rearrange("(n a) -> n a", a=1)
                    for copy in range(3):
                        r = A_GROUP * j + A_DH * copy
                        q.dma_start(self.cols[r:r + A_DH, at + t:at + t + 1], src).then_inc(self.loaded, 16)


def set_scale(pool, neg_mean, var_eps, power, rstd, neg_mean_rstd, var_ready, rstd_ready, scale_ready, m):
    pool.wait_ge(var_ready, m + 1)
    pool.tensor_tensor(rstd[:], var_eps[:], power[:], ALU.pow).then_inc(rstd_ready, 1)
    pool.wait_ge(rstd_ready, m + 1)
    pool.tensor_tensor(neg_mean_rstd[:], neg_mean[:], rstd[:], ALU.mult).then_inc(scale_ready, 1)


def norm_rows(act, rows_of, z, rstd, neg_mean_rstd, scale_ready, normed, m):
    act.wait_ge(scale_ready, m + 1)
    for t, (_, n) in enumerate(TILES):
        last = act.activation(z[0:n, t], rows_of(m, t), ACT.Identity, bias=neg_mean_rstd[0:n, t:t + 1],
                              scale=rstd[0:n, t:t + 1])
    last.then_inc(normed, 1)


def fusion_attention(p, inputs, ident, rows_of):
    nc = p.nc
    SCALE = 1.0 / float(np.sqrt(A_DH))

    with ExitStack() as ctx:
        def sb(name, shape, dtype=F32):
            return ctx.enter_context(nc.sbuf_tensor("at_" + name, shape, dtype))

        def sem(name):
            return p.sem("at_" + name)

        wq, wk = sb("wq", [P, 2, A_HALF], F32R), sb("wk", [P, 2, A_HALF], F32R)
        wv, wo = sb("wv", [P, 2, D], F32R), sb("wo", [D + 1, 2, D], F32R)
        bv, cols = inputs.bv, inputs.cols
        lo_rows, head_rows = sb("lo_rows", [P, 2]), sb("head_rows", [P, A_HPT])
        power = sb("power", [P, 2])

        stats, mean_var = sb("stats", [P, 2, 6]), sb("mean_var", [P, 2, 2])
        var_eps, rstd = sb("var_eps", [P, 2]), sb("rstd", [P, 2])
        neg_mean, neg_mean_rstd = sb("neg_mean", [P, 2]), sb("neg_mean_rstd", [P, 2])
        z, zc = sb("z", [P, 2, D]), sb("zc", [P, 2, D])
        xs = sb("xs", [P, 2, 2 * D], F32R)
        xT = sb("xT", [P, SEQP], F32R)
        qk_lo = sb("qk_lo", [P, 2, SEQP], F32R)
        KF = sb("KF", [P, A_TENSORS, SEQP], F32R)
        QF = sb("QF", [P, 2, A_TENSORS, SEQP], F32R)
        KB = sb("KB", [P, 2, A_TENSORS, A_HPT, SEQP], F32R)
        QP = sb("QP", [P, 2, A_TENSORS, SEQP], F32R)
        mpad = sb("mpad", [P, 2, A_TENSORS, P], F32R)
        PT = sb("PT", [P, 2, A_TENSORS, A_HPT * SEQP])
        V = sb("V", [P, 2, 2, A_HEADS, A_DH + 1])
        oU = sb("oU", [P, SEQP])
        rsum = sb("rsum", [P, 2, A_HEADS])
        o_rows = sb("o_rows", [P, 2, 2, P], BF16)
        oT = sb("oT", [D + 1, SEQP], F32R)
        ident_bf = sb("ident_bf", [P, P], BF16)

        scores = p.psum(ctx, "at_scores", [P, 2, 512])
        scores_t = p.psum(ctx, "at_scores_t", [P, 2, 512])
        maxT = p.psum(ctx, "at_maxT", [P, A_TENSORS, SEQP])
        outT = p.psum(ctx, "at_outT", [P, SEQP + 2 * P])
        outs = outT[:, SEQP:].rearrange("p (a h r) -> p a h r", a=2, h=A_HEADS)
        work = [p.psum(ctx, f"at_work{k}", [P, 512]) for k in range(2)]

        with ExitStack() as setup:
            def tmp(name, shape, dtype=F32):
                return setup.enter_context(nc.sbuf_tensor("at_" + name, shape, dtype))

            MATS, raw, bo = inputs.MATS, inputs.raw, inputs.bo
            hi, lo = tmp("hi", [P, len(MATS), D], F32R), tmp("lo", [P, len(MATS), D], F32R)
            row_index = tmp("row_index", [P, 1], I32)
            row_in_group = tmp("row_in_group", [P, 1])
            steps = tmp("steps", [P, 5])
            cleared, indexed, masks, ones_set = sem("cleared"), sem("indexed"), sem("masks"), sem("ones_set")
            turned, w_hi, w_lo, placed = sem("w_turned"), sem("w_hi"), sem("w_lo"), sem("w_placed")
            turn = work[0][:, 0:len(MATS) * D].rearrange("p (m o) -> p m o", m=len(MATS))

            with nc.Block() as block:
                @block.scalar
                def _(act):
                    act.wait_ge(turned, 1)
                    act.activation(hi[:], turn, ACT.Copy).then_inc(w_hi, 1)

                @block.gpsimd
                def _(pool):
                    pool.memset(V[:], 1.0).then_inc(cleared, 1)
                    pool.memset(power[:], -0.5).then_inc(cleared, 1)
                    for t in (xT, QP, mpad):
                        pool.memset(t[:].bitcast(F32), 0.0).then_inc(cleared, 1)
                    pool.memset(oT[:].bitcast(F32), 1.0).then_inc(cleared, 1)
                    for t in (z, mean_var, head_rows, o_rows):
                        pool.memset(t[:], 0.0).then_inc(cleared, 1)
                    pool.tensor_copy(ident_bf[:], ident[:]).then_inc(cleared, 1)
                    pool.wait_ge(cleared, 11)
                    for j in range(A_HPT):
                        rows = slice(A_GROUP * j, A_GROUP * (j + 1))
                        pool.memset(head_rows[rows, j:j + 1], 1.0).then_inc(indexed, 1)
                        pool.wait_ge(indexed, 2 * j + 1)
                        pool.iota(row_index[rows], pattern=[[0, 1]], base=0, channel_multiplier=1).then_inc(indexed, 1)
                        pool.wait_ge(indexed, 2 * j + 2)

                @block.tensor
                def _(pe):
                    pe.wait_ge(inputs.loaded, inputs.N * 16)
                    for k in range(len(MATS)):
                        last = pe.transpose(turn[:, k], raw[:, k], ident[0:D, 0:D])
                    last.then_inc(turned, 1)

                @block.vector
                def _(dve):
                    dve.memset(wq[:].bitcast(F32), 0.0).then_inc(masks, 1)
                    dve.memset(wk[:].bitcast(F32), 0.0).then_inc(masks, 1)
                    dve.memset(outT[:], 1.0).then_inc(masks, 1)
                    dve.wait_ge(indexed, 2 * A_HPT)
                    dve.tensor_copy(row_in_group[:], row_index[:]).then_inc(masks, 1)
                    dve.wait_ge(masks, 4)
                    for k, edge in enumerate((A_DH, 2 * A_DH, 3 * A_DH, 3 * A_DH + 1)):
                        dve.tensor_scalar(steps[:, k:k + 1], row_in_group[:], float(edge), None, ALU.is_ge)\
                            .then_inc(masks, 1)
                    dve.wait_ge(masks, 8)
                    dve.tensor_tensor(lo_rows[:, 0:1], steps[:, 1:2], steps[:, 2:3], ALU.subtract).then_inc(masks, 1)
                    dve.tensor_tensor(lo_rows[:, 1:2], steps[:, 0:1], steps[:, 1:2], ALU.subtract).then_inc(masks, 1)
                    dve.tensor_tensor(steps[:, 4:5], steps[:, 2:3], steps[:, 3:4], ALU.subtract).then_inc(masks, 1)
                    dve.wait_ge(masks, 11)
                    dve.wait_ge(inputs.loaded, inputs.N * 16)
                    dve.tensor_tensor(cols[:, 4:6], cols[:, 4:6], steps[:, 4:5].broadcast_to([P, 2]), ALU.add)\
                        .then_inc(ones_set, 1)
                    dve.wait_ge(w_hi, 1)
                    dve.tensor_tensor(lo[:], turn, hi[:].bitcast(F32), ALU.subtract).then_inc(w_lo, 1)
                    dve.tensor_copy(wo[D:D + 1, 0], bo[D:D + 1]).then_inc(w_lo, 1)
                    dve.wait_ge(w_lo, 2)
                    for part, src in ((0, hi), (1, lo)):
                        for k, dst in ((0, wq), (1, wk)):
                            place_heads(dve, dst[:, part:part + 1], src[:, k:k + 1].bitcast(F32), A_DH, A_GROUP, placed)
                        dve.tensor_copy(wv[:, part], src[:, 2].bitcast(F32))
                        dve.tensor_copy(wo[0:D, part], src[0:D, 3].bitcast(F32))
                    dve.tensor_tensor(wo[D:D + 1, 1], bo[D:D + 1], wo[D:D + 1, 0].bitcast(F32), ALU.subtract)
                    dve.wait_ge(ones_set, 1)
                    for at, who in ((0, 0), (4, 1)):
                        dve.tensor_scalar(cols[:, at + 2:at + 4], cols[:, at:at + 2], lo_rows[:, who:who + 1],
                                          None, ALU.mult)

        aggregated, var_ready, rstd_ready, scale_ready, normed, z_ready, x_hi, x_cut, x_turned, xT_set = (
            sem("aggregated"), sem("var_ready"), sem("rstd_ready"), sem("scale_ready"), sem("normed"), sem("z_ready"), sem("x_hi"),
            sem("x_cut"), sem("x_turned"), sem("xT_set"))
        projected, lo_part, qk_cut, k_split, v_made, v_set = (
            sem("projected"), sem("lo_part"), sem("qk_cut"), sem("k_split"), sem("v_made"), sem("v_set"))
        scored, max_set, max_turned, q_set = sem("scored"), sem("max_set"), sem("max_turned"), sem("q_set")
        out_copied, outs_turned = sem("out_copied"), sem("outs_turned")
        scored_t, exped, weighed, sums_inv, o_set, o_turned, oT_set, y_made, y_added = (
            sem("scored_t"), sem("exped"), sem("weighed"), sem("sums_inv"), sem("o_set"), sem("o_turned"),
            sem("oT_set"), sem("y_made"), sem("y_added"))

        def each_step(eng, step):
            for n in range(-3, 2):
                step(n, n % 2)
            with eng.Fori(1, B // 2 - 2) as i:
                step(i * 2, 0)
                step(i * 2 + 1, 1)
            for n in range(B - 4, B + 1):
                step(n, n % 2)

        with nc.Block() as block:
            @block.vector
            def _(dve):
                def find_max(m, tile):
                    n = TILES[tile][1]
                    dve.wait_ge(scored, m * 2 + (tile + 1))
                    if tile == 0 and due(m):
                        dve.wait_ge(max_turned, m)
                    dve.tensor_reduce(mpad[0:n, tile].rearrange("p t (j r) -> p t j r", r=A_GROUP)[:, :, :, 3 * A_DH],
                                      scores[0:n, :, 0:A_HPT * SEQP].rearrange("p t (j s) -> p t j s", j=A_HPT)[:, :, :, 0:SEQ],
                                      AX.X, ALU.max, negate=True).then_inc(max_set, 1)

                def join_max(m, par):
                    dve.wait_ge(max_turned, m + 1)
                    if due(m * 2 - 2):
                        dve.wait_ge(scored_t, m * 2 - 2)
                    dve.tensor_tensor(QP[:, par, :, 0:SEQ], maxT[:, :, 0:SEQ], QF[:, par, :, 0:SEQ].bitcast(F32),
                                      ALU.add).then_inc(q_set, 1)

                def cut_qk(m, i, par):
                    t, is_q = i % 2, i // 2
                    dst = QF[:, par, t] if is_q else KF[:, t]
                    dve.wait_ge(lo_part, m * 4 + (i + 1))
                    if i == 0 and due(m * 2):
                        dve.wait_ge(k_split, m * 2)
                    dve.scalar_tensor_tensor(out=dst, in0=work[(i + 1) % 2][:, 0:SEQP],
                                             scalar=cols[:, (0 if is_q else 4) + t:(1 if is_q else 5) + t],
                                             in1=qk_lo[:, i % 2].bitcast(F32), op0=ALU.add, op1=ALU.subtract)\
                        .then_inc(qk_cut, 1)

                def set_v(m, par):
                    dve.wait_ge(v_made, m + 1)
                    if due(m - 1):
                        dve.wait_ge(weighed, m - 1)
                    for tile, (_, n) in enumerate(TILES):
                        last = dve.tensor_tensor(
                            V[0:n, par, tile, :, 0:A_DH],
                            work[1][0:n, tile * D:(tile + 1) * D].rearrange("p (h c) -> p h c", h=A_HEADS),
                            bv[0:n].rearrange("p (h c) -> p h c", h=A_HEADS), ALU.add)
                    last.then_inc(v_set, 1)

                def clip_z(m):
                    dve.wait_ge(normed, m + 1)
                    if due(m):
                        dve.wait_ge(x_cut, m)
                    dve.tensor_scalar(zc[:], z[:], -CLIP, CLIP, ALU.max, ALU.min).then_inc(z_ready, 1)

                def normalise_o(m, par):
                    dve.wait_ge(outs_turned, m + 1)
                    if due(m - 1):
                        dve.wait_ge(o_turned, m - 1)
                    dve.reciprocal(rsum[:], outs[:, :, :, A_DH]).then_inc(sums_inv, 1)
                    dve.wait_ge(sums_inv, m + 1)
                    dve.tensor_tensor(o_rows[:, par, :, 0:D].rearrange("p a (h c) -> p a h c", h=A_HEADS), outs[:, :, :, 0:A_DH],
                                      rsum[:].unsqueeze(3).broadcast_to([P, 2, A_HEADS, A_DH]), ALU.mult)\
                        .then_inc(o_set, 1)

                def add_y(m):
                    dve.wait_ge(y_made, m + 1)
                    for tile, (_, n) in enumerate(TILES):
                        last = dve.tensor_tensor(rows_of(m, tile), rows_of(m, tile),
                                                 work[1][0:n, tile * D:(tile + 1) * D], ALU.add)
                    last.then_inc(y_added, 1)

                def step(n, par):
                    if live(n + 3):
                        set_stats(dve, rows_of, mean_var, stats, neg_mean, var_eps, aggregated, var_ready, n + 3,
                                  between=(lambda: find_max(n + 1, 0)) if live(n + 1) else None)
                    elif live(n + 1):
                        find_max(n + 1, 0)
                    if live(n - 1):
                        add_y(n - 1)
                    if live(n + 1):
                        find_max(n + 1, 1)
                    if live(n + 2):
                        cut_qk(n + 2, 0, par)
                        cut_qk(n + 2, 1, par)
                    if live(n + 3):
                        clip_z(n + 3)
                    if live(n + 1):
                        join_max(n + 1, 1 - par)
                    if live(n + 2):
                        cut_qk(n + 2, 2, par)
                        cut_qk(n + 2, 3, par)
                    if live(n):
                        normalise_o(n, par)
                    if live(n + 2):
                        set_v(n + 2, par)

                each_step(dve, step)

            @block.gpsimd
            def _(pool):
                def step(n, par):
                    if live(n + 3):
                        set_scale(pool, neg_mean, var_eps, power, rstd, neg_mean_rstd, var_ready, rstd_ready,
                                  scale_ready, n + 3)
                    if live(n + 2):
                        m = n + 2
                        if due(m * 2 - 2):
                            pool.wait_ge(scored_t, m * 2 - 2)
                        for t in range(A_TENSORS):
                            pool.wait_ge(qk_cut, m * 4 + (t + 1))
                            pool.tensor_tensor(KB[:, par, t],
                                               KF[:, t].bitcast(F32).unsqueeze(1).broadcast_to([P, A_HPT, SEQP]),
                                               head_rows[:].unsqueeze(2).broadcast_to([P, A_HPT, SEQP]), ALU.mult)\
                                .then_inc(k_split, 1)
                    if live(n + 3):
                        pool.wait_ge(x_hi, n + 4)
                        pool.tensor_tensor(xs[:, :, D:], zc[:], xs[:, :, 0:D].bitcast(F32), ALU.subtract)\
                            .then_inc(x_cut, 1)

                each_step(pool, step)

            @block.scalar
            def _(act):
                def exp(m, tile):
                    n = TILES[tile][1]
                    act.wait_ge(scored_t, m * 2 + (tile + 1))
                    if tile == 0 and due(m):
                        act.wait_ge(weighed, m)
                    act.activation(PT[0:n, tile], scores_t[0:n, :, 0:A_HPT * SEQP], ACT.Exp, scale=SCALE)\
                        .then_inc(exped, 1)

                def part_lo(m, i):
                    t, is_q = i % 2, i // 2
                    at = (2 if is_q else 6) + t
                    act.wait_ge(projected, m * 4 + (i + 1))
                    if due(m * 4 + (i - 1)):
                        act.wait_ge(qk_cut, m * 4 + (i - 1))
                    act.activation(qk_lo[:, i % 2], work[(i + 1) % 2][:, 0:SEQP], ACT.Identity,
                                   bias=cols[:, at:at + 1], scale=lo_rows[:, 1 - is_q:2 - is_q]).then_inc(lo_part, 1)

                def step(n, par):
                    if live(n):
                        exp(n, 0)
                    if live(n - 1):
                        act.wait_ge(o_turned, n)
                        if due(n - 1):
                            act.wait_ge(y_made, n - 1)
                        act.activation(oT[0:D, 0:SEQ], work[0][:].bitcast(BF16)[0:D, 0:SEQ], ACT.Copy).then_inc(oT_set, 1)
                    if live(n):
                        exp(n, 1)
                    if live(n + 2):
                        act.wait_ge(x_turned, n + 3)
                        if due(n + 2):
                            act.wait_ge(v_made, n + 2)
                        act.activation(xT[:, 0:SEQ], work[0][:, 0:SEQ], ACT.Copy).then_inc(xT_set, 1)
                        part_lo(n + 2, 0)
                        part_lo(n + 2, 1)
                    if live(n + 3):
                        norm_rows(act, rows_of, z, rstd, neg_mean_rstd, scale_ready, normed, n + 3)
                    if live(n):
                        act.wait_ge(weighed, n + 1)
                        if due(n):
                            act.wait_ge(outs_turned, n)
                        act.activation(oU[:], outT[:, 0:SEQP], ACT.Copy).then_inc(out_copied, 1)
                    if live(n + 2):
                        part_lo(n + 2, 2)
                        part_lo(n + 2, 3)
                    if live(n + 3):
                        act.wait_ge(z_ready, n + 4)
                        if due(n + 3):
                            act.wait_ge(x_turned, n + 3)
                        act.activation(xs[:, :, 0:D], zc[:], ACT.Copy).then_inc(x_hi, 1)

                each_step(act, step)

            @block.tensor
            def _(pe):
                def score(m, par, tile):
                    at, n = TILES[tile]
                    if tile == 0:
                        pe.wait_ge(k_split, m * 2 + 2)
                        pe.wait_ge(qk_cut, m * 4 + 4)
                    if due(m * 2 + tile):
                        pe.wait_ge(max_set, m * 2 + tile)
                    for t in range(A_TENSORS):
                        last = pe.matmul(scores[0:n, t, 0:A_HPT * SEQP], QF[:, par, t, at:at + n],
                                         KB[:, par, t].rearrange("p j s -> p (j s)"), start=True, stop=True)
                    last.then_inc(scored, 1)

                def score_t(m, par, tile):
                    at, n = TILES[tile]
                    if tile == 0:
                        pe.wait_ge(q_set, m + 1)
                    if due(m * 2 + tile):
                        pe.wait_ge(exped, m * 2 + tile)
                    for t in range(A_TENSORS):
                        for j in range(A_HPT):
                            last = pe.matmul(scores_t[0:n, t, j * SEQP:(j + 1) * SEQP], KB[:, par, t, j, at:at + n],
                                             QP[:, par, t], start=True, stop=True)
                    last.then_inc(scored_t, 1)

                def turn_x(m):
                    pe.wait_ge(x_cut, m + 1)
                    if due(m):
                        pe.wait_ge(qk_cut, m * 4)
                    if due(m - 2):
                        pe.wait_ge(oT_set, m - 2)
                    for tile, (at, n) in enumerate(TILES):
                        last = pe.transpose(work[0][:, at:at + n], xs[0:n, tile].bitcast(F32), ident[0:n, 0:n])
                    last.then_inc(x_turned, 1)

                def project(m, i):
                    t, wgt = i % 2, wq if i // 2 else wk
                    if i == 0:
                        pe.wait_ge(xT_set, m + 1)
                        if due(m):
                            pe.wait_ge(v_set, m)
                        if due(m - 2):
                            pe.wait_ge(y_added, m - 2)
                    if i >= 2:
                        pe.wait_ge(qk_cut, m * 4 + (i - 1))
                    for part in range(2):
                        last = pe.matmul(work[(i + 1) % 2][:, 0:SEQP], wgt[:, part, t * P:(t + 1) * P], xT[:],
                                         start=part == 0, stop=part == 1)
                    last.then_inc(projected, 1)

                def project_v(m):
                    pe.wait_ge(qk_cut, m * 4 + 3)
                    for tile, (at, n) in enumerate(TILES):
                        for part in range(2):
                            last = pe.matmul(work[1][0:n, tile * D:(tile + 1) * D], xT[:, at:at + n], wv[:, part],
                                             start=part == 0, stop=part == 1)
                    last.then_inc(v_made, 1)

                def weigh(m, par):
                    pe.wait_ge(exped, m * 2 + 2)
                    pe.wait_ge(v_set, m + 1)
                    if due(m):
                        pe.wait_ge(o_set, m)
                    for keys, (_, kn) in enumerate(TILES):
                        for h in range(A_HEADS):
                            t, j = h // A_HPT, h % A_HPT
                            last = pe.matmul(outT[32 * h:32 * h + A_DH + 1, 0:SEQP], V[0:kn, par, keys, h],
                                             PT[0:kn, keys, t, j * SEQP:(j + 1) * SEQP],
                                             start=keys == 0, stop=keys == 1)
                    last.then_inc(weighed, 1)

                def turn_outs(m):
                    pe.wait_ge(out_copied, m + 1)
                    for tile, (at, n) in enumerate(TILES):
                        last = pe.transpose(outT[0:n, SEQP + tile * P:SEQP + (tile + 1) * P], oU[:, at:at + n], ident[:])
                    last.then_inc(outs_turned, 1)

                def turn_max(m):
                    pe.wait_ge(max_set, m * 2 + 2)
                    for tile, (at, n) in enumerate(TILES):
                        for t in range(A_TENSORS):
                            last = pe.transpose(maxT[:, t, at:at + n], mpad[0:n, tile, t].bitcast(F32), ident[0:n, 0:n])
                    last.then_inc(max_turned, 1)

                def turn_o(m, par):
                    pe.wait_ge(o_set, m + 1)
                    if live(m + 2):
                        pe.wait_ge(qk_cut, m * 4 + 12)
                    elif due(m):
                        pe.wait_ge(oT_set, m)
                    for tile, (at, n) in enumerate(TILES):
                        last = pe.transpose(work[0][:].bitcast(BF16)[:, at:at + n], o_rows[0:n, par, tile],
                                            ident_bf[0:n, 0:n])
                    last.then_inc(o_turned, 1)

                def project_o(m):
                    pe.wait_ge(oT_set, m + 1)
                    if live(m + 2):
                        pe.wait_ge(v_set, m + 3)
                    else:
                        pe.wait_ge(y_added, m)
                    for tile, (at, n) in enumerate(TILES):
                        for part in range(2):
                            last = pe.matmul(work[1][0:n, tile * D:(tile + 1) * D], oT[:, at:at + n], wo[:, part],
                                             start=part == 0, stop=part == 1)
                    last.then_inc(y_made, 1)

                def step(n, par):
                    if live(n):
                        score_t(n, par, 0)
                    if live(n + 1):
                        score(n + 1, 1 - par, 0)
                    if live(n - 1):
                        turn_o(n - 1, 1 - par)
                    if live(n):
                        score_t(n, par, 1)
                    if live(n - 1):
                        project_o(n - 1)
                    if live(n + 2):
                        turn_x(n + 2)
                    if live(n + 1):
                        score(n + 1, 1 - par, 1)
                    if live(n + 2):
                        project(n + 2, 0)
                        project(n + 2, 1)
                    if live(n):
                        weigh(n, par)
                    if live(n + 1):
                        turn_max(n + 1)
                    if live(n + 2):
                        project(n + 2, 2)
                        project(n + 2, 3)
                    if live(n):
                        turn_outs(n)
                    if live(n + 2):
                        project_v(n + 2)

                each_step(pe, step)


class ExpertInputs:

    def __init__(self, p, wts):
        self.nc, self.wts = p.nc, wts
        halves = FF // P
        self.w1_raw = p.sb("ex_w1_raw", [P, FF])
        self.wd_raw = p.sb("ex_wd_raw", [P, halves, EXPERTS * D + EXPERTS])
        self.b_raw = p.sb("ex_b_raw", [33, EXPERTS * D])
        self.b1, self.bg = p.sb("ex_b1", [P, halves]), p.sb("ex_bg", [EXPERTS, 1])
        self.loaded = p.sem("ex_loaded")
        self.N = 2 + 3 * halves + 2 + 1

    def load(self, q):
        wts, wide = self.wts, EXPERTS * D
        for half in range(2):
            q.dma_start(self.w1_raw[half * D:(half + 1) * D], wts["W1"]).then_inc(self.loaded, 16)
        for half in range(FF // P):
            rows = slice(half * P, (half + 1) * P)
            q.dma_start(self.wd_raw[:, half, 0:wide].rearrange("p (e d) -> p e d", e=EXPERTS),
                        wts["Wd"][:, rows].rearrange("e i d -> i e d")).then_inc(self.loaded, 16)
            q.dma_start(self.wd_raw[:, half, wide:], wts["Wg"][rows]).then_inc(self.loaded, 16)
            with self.nc.allow_non_contiguous_dma(reason="bias as columns"):
                q.dma_start(self.b1[:, half:half + 1], wts["b1"][rows].rearrange("(n a) -> n a", a=1))\
                    .then_inc(self.loaded, 16)
        for r in (0, 32):
            q.dma_start(self.b_raw[r:r + 1], row(wts["bd"].rearrange("e d -> (e d)"))).then_inc(self.loaded, 16)
        with self.nc.allow_non_contiguous_dma(reason="bias as a column"):
            q.dma_start(self.bg[:], wts["bg"].rearrange("(n a) -> n a", a=1)).then_inc(self.loaded, 16)


def experts(p, inputs, ident, rows_of, out):
    nc = p.nc
    HALVES = FF // P
    WIDE = EXPERTS * D
    G = 4

    with ExitStack() as ctx:
        def sb(name, shape, dtype=F32):
            return ctx.enter_context(nc.sbuf_tensor("ex_" + name, shape, dtype))

        def sem(name):
            return p.sem("ex_" + name)

        w1 = sb("w1", [P, 2, FF], F32R)
        wd = sb("wd", [P, 2, HALVES, WIDE + EXPERTS], F32R)
        b1, bg = inputs.b1, inputs.bg
        biases, ones = sb("biases", [33, WIDE], F32R), sb("ones", [33, P], F32R)
        rank, power = sb("rank", [P, EXPERTS]), sb("power", [P, 2])

        stats, mean_var = sb("stats", [P, 2, 6]), sb("mean_var", [P, 2, 2])
        var_eps, rstd = sb("var_eps", [P, 2]), sb("rstd", [P, 2])
        neg_mean, neg_mean_rstd = sb("neg_mean", [P, 2]), sb("neg_mean_rstd", [P, 2])
        z = sb("z", [P, 2, D])
        xs = sb("xs", [P, 2, 2 * D], F32R)
        xT = sb("xT", [P, 2, SEQP], F32R)
        H = sb("H", [P, 2, HALVES, SEQP])
        H_hi = sb("H_hi", [P, 2 * G, HALVES, SEQP], F32R)
        H_lo = sb("H_lo", [P, 2 * G, HALVES, SEQP], F32R)
        logit_rows = sb("logit_rows", [EXPERTS, SEQP])
        top, less = sb("top", [P, 2 * G]), sb("less", [P, 2 * G, EXPERTS])
        e_less, e_sum = sb("e_less", [P, 2 * G, EXPERTS]), sb("e_sum", [P, 2 * G])
        prob = sb("prob", [P, 2 * G])
        first, chosen = sb("first", [P, 2 * G]), sb("chosen", [P, 2 * G, EXPERTS])
        gate = sb("gate", [P, 2 * G, EXPERTS])
        weighted = sb("weighted", [P, 2, EXPERTS, D])
        summed = sb("summed", [P, 2, D])

        turned_x = p.psum(ctx, "ex_turned_x", [P, 512])
        up_rows = p.psum(ctx, "ex_up", [P, HALVES, SEQP])
        logits = p.psum(ctx, "ex_logits", [P, 2 * G, EXPERTS])
        y = [p.psum(ctx, f"ex_y{k}", [P, EXPERTS, D]) for k in range(4)]

        with ExitStack() as setup:
            def tmp(name, shape, dtype=F32):
                return setup.enter_context(nc.sbuf_tensor("ex_" + name, shape, dtype))

            w1_raw, wd_raw, b_raw = inputs.w1_raw, inputs.wd_raw, inputs.b_raw
            b_hi = tmp("b_hi", [33, WIDE], F32R)
            cleared, w_hi = sem("cleared"), sem("w_hi")

            with nc.Block() as block:
                @block.gpsimd
                def _(pool):
                    pool.memset(biases[:].bitcast(F32), 0.0).then_inc(cleared, 1)
                    pool.memset(ones[:].bitcast(F32), 1.0)
                    pool.memset(power[:], -0.5)
                    pool.memset(xT[:].bitcast(F32), 0.0)
                    pool.memset(z[:], 0.0)
                    pool.memset(mean_var[:], 0.0)
                    for e in range(EXPERTS):
                        pool.memset(rank[:, e:e + 1], float(EXPERTS - e))

                @block.vector
                def _(dve):
                    dve.memset(logits[:], 0.0)
                    dve.wait_ge(inputs.loaded, inputs.N * 16)
                    dve.tensor_copy(w1[:, 0], w1_raw[:]).then_inc(w_hi, 1)
                    dve.tensor_copy(wd[:, 0], wd_raw[:]).then_inc(w_hi, 1)
                    dve.tensor_copy(b_hi[:], b_raw[:]).then_inc(w_hi, 1)
                    dve.wait_ge(w_hi, 3)
                    dve.tensor_tensor(w1[:, 1], w1_raw[:], w1[:, 0].bitcast(F32), ALU.subtract)
                    dve.tensor_tensor(wd[:, 1], wd_raw[:], wd[:, 0].bitcast(F32), ALU.subtract)
                    dve.wait_ge(cleared, 1)
                    dve.tensor_copy(biases[0:1], b_hi[0:1].bitcast(F32))
                    dve.tensor_tensor(biases[32:33], b_raw[32:33], b_hi[32:33].bitcast(F32), ALU.subtract)

        aggregated, var_ready, rstd_ready, scale_ready, z_ready, x_hi, x_cut, x_turned, xT_set = (
            sem("aggregated"), sem("var_ready"), sem("rstd_ready"), sem("scale_ready"), sem("z_ready"),
            sem("x_hi"), sem("x_cut"), sem("x_turned"), sem("xT_set"))
        up_done, gelu_done, h_hi, h_cut = sem("up_done"), sem("gelu_done"), sem("h_hi"), sem("h_cut")
        logits_made, logits_copied = sem("logits_made"), sem("logits_copied")
        gated, gate_step, gate_exp, gate_sum, gate_set = (
            sem("gated"), sem("gate_step"), sem("gate_exp"), sem("gate_sum"), sem("gate_set"))
        y_made, y_weighted, y_summed, added, stored = (
            sem("y_made"), sem("y_weighted"), sem("y_summed"), sem("added"), sem("stored"))
        GATE_STEPS = 6

        def each_step(eng, step):
            for n in range(-7, 8):
                step(n, n % 8)
            with eng.Fori(1, B // 8 - 1) as i:
                for k in range(8):
                    step(i * 8 + k, k)
            for n in range(B - 8, B):
                step(n, n % 8)

        with nc.Block() as block:
            @block.sync
            def _(sp):
                def step(n, k):
                    if k % 2 == 1 and live(n):
                        sp.wait_ge(added, n * 2 + 2)
                        for tile, (at, rows) in enumerate(TILES):
                            sp.dma_start(out[bass.ds(n - 1, 2), at:at + rows].rearrange("b s d -> s b d"),
                                         rows_of(n - 1, tile, 2)).then_inc(stored, 16)

                each_step(sp, step)
                sp.wait_ge(stored, B * 16)

            @block.vector
            def _(dve):
                def choose(q):
                    wide = [P, 2 * G, EXPERTS]
                    base = q * GATE_STEPS
                    dve.wait_ge(gated, q * G + G)
                    dve.tensor_reduce(top[:], logits[:], AX.X, ALU.max).then_inc(gate_step, 1)
                    dve.wait_ge(gate_step, base + 1)
                    dve.tensor_tensor(less[:], logits[:], top[:].unsqueeze(2).broadcast_to(wide), ALU.subtract)\
                        .then_inc(gate_sum, 1)
                    dve.wait_ge(gate_sum, q + 1)
                    dve.scalar_tensor_tensor(out=chosen[:], in0=less[:], scalar=0.0,
                                             in1=rank[:].unsqueeze(1).broadcast_to(wide), op0=ALU.is_ge, op1=ALU.mult)\
                        .then_inc(gate_step, 1)
                    dve.wait_ge(gate_step, base + 2)
                    dve.tensor_reduce(first[:], chosen[:], AX.X, ALU.max).then_inc(gate_step, 1)
                    dve.wait_ge(gate_exp, q + 1)
                    dve.tensor_reduce(e_sum[:], e_less[:], AX.X, ALU.add).then_inc(gate_step, 1)
                    dve.wait_ge(gate_step, base + 4)
                    dve.reciprocal(prob[:], e_sum[:]).then_inc(gate_step, 1)
                    dve.tensor_tensor(chosen[:], chosen[:], first[:].unsqueeze(2).broadcast_to(wide), ALU.is_equal)\
                        .then_inc(gate_step, 1)
                    dve.wait_ge(gate_step, base + 6)
                    dve.tensor_tensor(gate[:], chosen[:], prob[:].unsqueeze(2).broadcast_to(wide), ALU.mult)\
                        .then_inc(gate_set, 1)
                    dve.wait_ge(gate_set, q + 1)

                def combine(m, b, par, tile):
                    n = TILES[tile][1]
                    dve.wait_ge(y_made, m * 2 + (tile + 1))
                    dve.tensor_tensor(weighted[0:n, tile], y[2 * par + tile][0:n],
                                      gate[0:n, 2 * b + tile].unsqueeze(2).broadcast_to([n, EXPERTS, D]), ALU.mult)\
                        .then_inc(y_weighted, 1)
                    dve.wait_ge(y_weighted, m * 2 + (tile + 1))
                    dve.tensor_reduce(summed[0:n, tile], weighted[0:n, tile].rearrange("p e d -> p d e"), AX.X, ALU.add)\
                        .then_inc(y_summed, 1)
                    dve.wait_ge(y_summed, m * 2 + (tile + 1))
                    dve.tensor_tensor(rows_of(m, tile), rows_of(m, tile), summed[0:n, tile], ALU.add).then_inc(added, 1)

                def step(n, k):
                    b, par = k % G, k % 2
                    if live(n + 7):
                        if due(n + 7):
                            dve.wait_ge(scale_ready, n + 7)
                        set_stats(dve, rows_of, mean_var, stats, neg_mean, var_eps, aggregated, var_ready, n + 7)
                    if live(n):
                        combine(n, b, par, 0)
                    if live(n):
                        combine(n, b, par, 1)
                    if b == G - 1 and live(n + 4):
                        choose((n + 4 - b) // G if isinstance(n, int) else q_of(n, k))

                def q_of(n, k):
                    return QREG[0] * 2 + (k // G + 1)

                QREG = [None]
                for n in range(-7, 8):
                    step(n, n % 8)
                with dve.Fori(1, B // 8 - 1) as i:
                    QREG[0] = i
                    for k in range(8):
                        step(i * 8 + k, k)
                for n in range(B - 8, B):
                    step(n, n % 8)

            @block.gpsimd
            def _(pool):
                def step(n, k):
                    if live(n + 7):
                        set_scale(pool, neg_mean, var_eps, power, rstd, neg_mean_rstd, var_ready, rstd_ready,
                                  scale_ready, n + 7)
                    if live(n + 5):
                        m, slot = n + 5, (k + 5) % 8
                        pool.wait_ge(h_hi, m + 1)
                        pool.tensor_tensor(H_lo[:, slot], H[:, slot % 2], H_hi[:, slot].bitcast(F32), ALU.subtract)\
                            .then_inc(h_cut, 1)
                    if live(n + 7):
                        pool.wait_ge(x_hi, n + 8)
                        pool.tensor_tensor(xs[:, :, D:], z[:], xs[:, :, 0:D].bitcast(F32), ALU.subtract)\
                            .then_inc(x_cut, 1)

                each_step(pool, step)

            @block.scalar
            def _(act):
                def step(n, k, q):
                    if live(n + 4):
                        m = n + 4
                        act.wait_ge(logits_made, m + 1)
                        if due(m):
                            act.wait_ge(gated, m)
                        act.activation(logit_rows[:], turned_x[0:EXPERTS, P * 2:P * 2 + SEQP], ACT.Identity, bias=bg[:])\
                            .then_inc(logits_copied, 1)
                    if live(n + 5):
                        m, slot = n + 5, (k + 5) % 8
                        act.wait_ge(up_done, m + 1)
                        if due(m - 1):
                            act.wait_ge(h_cut, m - 1)
                        for half in range(HALVES):
                            last = act.activation(H[:, slot % 2, half], up_rows[:, half], ACT.Gelu,
                                                  bias=b1[:, half:half + 1])
                        last.then_inc(gelu_done, 1)
                        act.wait_ge(gelu_done, m + 1)
                        if due(m * 2 - 14):
                            act.wait_ge(y_made, m * 2 - 14)
                        act.activation(H_hi[:, slot], H[:, slot % 2], ACT.Copy).then_inc(h_hi, 1)
                    if live(n + 6):
                        m = n + 6
                        act.wait_ge(x_turned, m + 1)
                        if due(m - 1):
                            act.wait_ge(up_done, m - 1)
                        act.activation(xT[:, (k + 6) % 2, 0:SEQ], turned_x[:, 0:SEQ], ACT.Copy).then_inc(xT_set, 1)
                    if live(n + 7):
                        m = n + 7
                        if due(m):
                            act.wait_ge(x_cut, m)
                        norm_rows(act, rows_of, z, rstd, neg_mean_rstd, scale_ready, z_ready, m)
                        act.wait_ge(z_ready, m + 1)
                        if due(m):
                            act.wait_ge(x_turned, m)
                        act.activation(xs[:, :, 0:D], z[:], ACT.Copy).then_inc(x_hi, 1)
                    if k % G == G - 1 and live(n + 4):
                        act.wait_ge(gate_sum, q + 1)
                        act.activation(e_less[:], less[:], ACT.Exp).then_inc(gate_exp, 1)

                for n in range(-7, 8):
                    step(n, n % 8, (n + 4) // G)
                with act.Fori(1, B // 8 - 1) as i:
                    for k in range(8):
                        step(i * 8 + k, k, i * 2 + (k // G + 1))
                for n in range(B - 8, B):
                    step(n, n % 8, (n + 4) // G)

            @block.tensor
            def _(pe):
                def run_experts(m, slot, par, tile):
                    at, n = TILES[tile]
                    if due(m * 2 - 3 + tile):
                        pe.wait_ge(y_weighted, m * 2 - 3 + tile)
                    acc = y[2 * par + tile][0:n].rearrange("p e d -> p (e d)")
                    pe.matmul(acc, ones[:, 0:n], biases[:], start=True, stop=False)
                    for half in range(HALVES):
                        for h, part in ((H_hi, 0), (H_hi, 1), (H_lo, 0)):
                            last = pe.matmul(acc, h[:, slot, half, at:at + n], wd[:, part, half, 0:WIDE],
                                             start=False, stop=half == HALVES - 1 and h is H_lo)
                    last.then_inc(y_made, 1)

                def step(n, k, q):
                    if live(n + 5):
                        m = n + 5
                        pe.wait_ge(xT_set, m + 1)
                        if due(m):
                            pe.wait_ge(gelu_done, m)
                        for half in range(HALVES):
                            for part in range(2):
                                last = pe.matmul(up_rows[:, half], w1[:, part, half * P:(half + 1) * P],
                                                 xT[:, (k + 5) % 2], start=part == 0, stop=part == 1)
                        last.then_inc(up_done, 1)
                    if live(n):
                        run_experts(n, k, k % 2, 0)
                    if live(n + 4):
                        m, b = n + 4, k % G
                        pe.wait_ge(logits_copied, m + 1)
                        if b == 0 and due(q):
                            pe.wait_ge(gate_sum, q)
                    if live(n + 6):
                        m = n + 6
                        pe.wait_ge(x_cut, m + 1)
                        if due(m):
                            pe.wait_ge(xT_set, m)
                        if due(m - 1):
                            pe.wait_ge(logits_copied, m - 1)
                        for tile, (at, rows) in enumerate(TILES):
                            last = pe.transpose(turned_x[:, at:at + rows], xs[0:rows, tile].bitcast(F32),
                                                ident[0:rows, 0:rows])
                        last.then_inc(x_turned, 1)
                    if live(n + 4):
                        for tile, (at, rows) in enumerate(TILES):
                            last = pe.transpose(logits[0:rows, 2 * b + tile], logit_rows[:, at:at + rows],
                                                ident[0:EXPERTS, 0:EXPERTS])
                        last.then_inc(gated, 1)
                    if live(n):
                        run_experts(n, k, k % 2, 1)
                    if live(n + 5):
                        m, slot = n + 5, (k + 5) % 8
                        pe.wait_ge(h_cut, m + 1)
                        if live(m + 1):
                            pe.wait_ge(xT_set, m + 2)
                        acc = turned_x[0:EXPERTS, P * 2:P * 2 + SEQP]
                        for half in range(HALVES):
                            for h, part in ((H_hi, 0), (H_hi, 1), (H_lo, 0)):
                                last = pe.matmul(acc, wd[:, part, half, WIDE:], h[:, slot, half],
                                                 start=half == 0 and part == 0 and h is H_hi,
                                                 stop=half == HALVES - 1 and h is H_lo)
                        last.then_inc(logits_made, 1)

                for n in range(-7, 8):
                    step(n, n % 8, (n + 4) // G)
                with pe.Fori(1, B // 8 - 1) as i:
                    for k in range(8):
                        step(i * 8 + k, k, i * 2 + (k // G + 1))
                for n in range(B - 8, B):
                    step(n, n % 8, (n + 4) // G)



IMAGE_WEIGHTS = ("ln0_g", "ln0_b", "ln1_g", "ln1_b", "conv1_w", "conv1_b", "conv2_w", "conv2_b", "conv3_w",
                 "conv3_b", "out_w", "out_b")
TEXT_WEIGHTS = ("emb", "Wq", "bq", "Wv", "bv", "Wo", "bo", "W1", "b1", "W2", "b2", "ln1_g", "ln1_b", "ln2_g",
                "ln2_b", "fin_g", "fin_b")
ATTENTION_WEIGHTS = ("Wq", "bq", "Wk", "bk", "Wv", "bv", "Wo", "bo")
EXPERT_WEIGHTS = ("W1", "b1", "Wg", "bg", "Wd", "bd")


def early_fusion_embed(nc, x, x_txt, pos, weights, out):
    def of(prefix, names):
        return {name: weights[prefix + name] for name in names}

    with ExitStack() as ctx:
        p = Program(nc, ctx, B)
        ident = p.sb("ident", [P, P])
        h_img, h_txt = p.sb("h_img", [T, B, LAT]), p.sb("h_txt", [S_TXT, B, D])

        def rows_of(n, tile, count=None):
            h = h_txt if tile else h_img
            v = h[:, bass.ds(n, count or 1)]
            return v if count else v.rearrange("p a d -> p (a d)")

        text = TextInputs(p, x_txt, pos, of("L0_txt_", TEXT_WEIGHTS))
        attention = AttentionInputs(p, of("L0_attn_", ATTENTION_WEIGHTS))
        expert = ExpertInputs(p, of("L0_ffn_", EXPERT_WEIGHTS))
        constants(p, ident, [text.cols_all, attention.cols, expert.b_raw])
        image_branch(p, x, of("L0_tok_", IMAGE_WEIGHTS), ident, h_img, [text, attention, expert])
        text_branch(p, text, ident, h_txt)
        fusion_attention(p, attention, ident, rows_of)
        experts(p, expert, ident, rows_of, out)


def positional_table():
    at = np.arange(S_TXT, dtype=np.float32)[:, None]
    freq = np.exp(np.arange(0, D, 2, dtype=np.float32) * np.float32(-np.log(10000.0) / D))
    table = np.zeros((S_TXT, D), np.float32)
    table[:, 0::2], table[:, 1::2] = np.sin(at * freq), np.cos(at * freq)
    return table


def kernel(**inputs):
    import concourse.bacc as _bacc
    from concourse import mybir as _mybir
    from concourse.bass_utils import run_bass_kernel_spmd as _run

    nc = _bacc.Bacc("TRN2", target_bir_lowering=False, num_devices=1)
    arrays = {name: np.ascontiguousarray(a) for name, a in inputs.items()}
    arrays["pos"] = positional_table()
    dram = {name: nc.dram_tensor(name, a.shape, _mybir.dt.from_np(a.dtype), kind="ExternalInput").ap()
            for name, a in arrays.items()}
    out = nc.dram_tensor("out", (B, T + S_TXT, D), F32, kind="ExternalOutput").ap()
    weights = {name: ap for name, ap in dram.items() if name.startswith("L0_")}
    early_fusion_embed(nc, dram["x"], dram["x_txt"], dram["pos"], weights, out)
    r = _run(nc, [arrays], core_ids=[0])
    return r.results[0]["out"]
```
